# Optimizing a Trainium2 kernel written in Bass

```python
import numpy as np
import jax
import jax.numpy as jnp

def _softmax(x, axis=-1):
    return jax.nn.softmax(x, axis=axis)

def _gelu(x):
    return jax.nn.gelu(x, approximate=True)

def _silu(x):
    return jax.nn.silu(x)

def _sigmoid(x):
    return jax.nn.sigmoid(x)

def _layernorm(x, axis=-1, eps=1e-05):
    m = jnp.mean(x, axis=axis, keepdims=True)
    v = jnp.var(x, axis=axis, keepdims=True)
    return (x - m) / jnp.sqrt(v + eps)

def _scatter_add(tgt, idx, src, axis=0):
    return tgt.at[idx].add(src)

def _segment_sum(src, seg, n):
    return jax.ops.segment_sum(src, seg, n)
kernel_name = 'mk_macaron_d2_jaxref_r8_ffe9b1'

def setup_inputs(seed: int=0):
    np.random.seed(seed)
    _w = jnp.asarray

    def _L0_attn_setup():
        import jax, jax.numpy as jnp
        import numpy as np
        D_MODEL = 128
        D_STATE = 64
        EXPAND = 2
        N_HEADS = 32
        NGROUPS = 1
        CHUNK = 128
        R = 2
        D_INNER = EXPAND * D_MODEL
        HEAD_DIM = D_INNER // N_HEADS
        BC = NGROUPS * D_STATE
        D_PROJ = D_INNER + D_INNER * R + BC * R + BC + 2 * N_HEADS + D_STATE // 2
        SCALE = (D_STATE * R) ** (-0.5)
        EPS = 1e-06
        NEG = -1e+30

        def _rms(x):
            return x * jax.lax.rsqrt(jnp.mean(x * x, axis=-1, keepdims=True) + EPS)

        def _rope(x, cos, sin):
            h = x.shape[-1] // 2
            x1, x2 = (x[..., :h], x[..., h:])
            return jnp.concatenate([x1 * cos - x2 * sin, x1 * sin + x2 * cos], axis=-1)
        key = jax.random.key(seed)
        ks = jax.random.split(key, 7)
        B, T = (2, 256)
        return {'x': jax.random.normal(ks[0], (B, T, D_MODEL), jnp.float32), 'W_in': jax.random.normal(ks[1], (D_MODEL, D_PROJ), jnp.float32) * 0.02, 'A_log': jax.random.normal(ks[2], (N_HEADS,), jnp.float32) * 0.5, 'dt_bias': jax.random.normal(ks[3], (N_HEADS,), jnp.float32) * 0.5, 'B_norm_bias': 1.0 + 0.1 * jax.random.normal(ks[4], (NGROUPS, D_STATE), jnp.float32), 'C_norm_bias': 1.0 + 0.1 * jax.random.normal(ks[5], (NGROUPS, D_STATE), jnp.float32), 'W_out': jax.random.normal(ks[6], (D_INNER, D_MODEL), jnp.float32) * 0.02}
    _L0_attn_in = _L0_attn_setup()

    def _L0_ffn_setup():
        import jax, jax.numpy as jnp
        import numpy as np
        B, T, D, H, E, K = (2, 256, 128, 512, 8, 2)
        EPS = 1e-12

        def moe_forward(x, Wg, bg, W1, b1, W2, b2):
            gates = jax.nn.softmax(x @ Wg + bg, axis=-1)
            _, top_idx = jax.lax.top_k(gates, K)
            mask = jax.nn.one_hot(top_idx, E, dtype=gates.dtype).sum(axis=-2)
            g = gates * mask
            g = g / jnp.maximum(jnp.sum(jnp.abs(g), axis=-1, keepdims=True), EPS)
            h = jnp.einsum('btd,edh->bteh', x, W1) + b1[None, None]
            h = jax.nn.gelu(h, approximate=False)
            eo = jnp.einsum('bteh,ehd->bted', h, W2) + b2[None, None]
            return jnp.einsum('bte,bted->btd', g, eo)
        key = jax.random.key(seed)
        ks = jax.random.split(key, 8)
        s_d = 1.0 / np.sqrt(D)
        s_h = 1.0 / np.sqrt(H)
        return {'x': jax.random.normal(ks[0], (B, T, D), dtype=jnp.float32), 'Wg': jax.random.uniform(ks[1], (D, E), jnp.float32, -s_d, s_d), 'bg': jax.random.uniform(ks[2], (E,), jnp.float32, -s_d, s_d), 'W1': jax.random.uniform(ks[3], (E, D, H), jnp.float32, -s_d, s_d), 'b1': jax.random.uniform(ks[4], (E, H), jnp.float32, -s_d, s_d), 'W2': jax.random.uniform(ks[5], (E, H, D), jnp.float32, -s_h, s_h), 'b2': jax.random.uniform(ks[6], (E, D), jnp.float32, -s_h, s_h)}
    _L0_ffn_in = _L0_ffn_setup()

    def _L1_attn_setup():
        import jax, jax.numpy as jnp
        import numpy as np
        D_MODEL = 128
        NHEAD = 16
        D_K = D_MODEL // NHEAD
        SCALE = 1.0 / np.sqrt(D_K * 2.0)
        TEMP = 1.5
        EPS = 1e-08

        def _l2norm(t):
            n = jnp.sqrt(jnp.sum(t * t, axis=-1, keepdims=True))
            return t / jnp.maximum(n, EPS)
        key = jax.random.key(seed)
        ks = jax.random.split(key, 9)
        B, T = (2, 256)
        x = jax.random.normal(ks[0], (B, T, D_MODEL), dtype=jnp.float32)

        def w(k):
            return 0.02 * jax.random.normal(k, (D_MODEL, D_MODEL), dtype=jnp.float32)
        return {'x': x, 'Wq': w(ks[1]), 'bq': jnp.zeros((D_MODEL,), jnp.float32), 'Wk': w(ks[2]), 'bk': jnp.zeros((D_MODEL,), jnp.float32), 'Wv': w(ks[3]), 'bv': jnp.zeros((D_MODEL,), jnp.float32), 'Wo': w(ks[4]), 'bo': jnp.zeros((D_MODEL,), jnp.float32)}
    _L1_attn_in = _L1_attn_setup()

    def _L1_ffn_setup():
        import jax, jax.numpy as jnp
        import numpy as np
        D_MODEL = 128
        D_OUT = 128
        RANK = 16
        NUM_TRUE = 8
        NUM_NULL = 2
        TOP_K = 2
        SCALING = 32.0 / 16.0
        key = jax.random.key(seed)
        ks = jax.random.split(key, 6)
        x = jax.random.normal(ks[0], (4, 512, D_MODEL), dtype=jnp.float32)
        base_w = jax.random.normal(ks[1], (D_OUT, D_MODEL), dtype=jnp.float32) / np.sqrt(D_MODEL)
        base_b = jax.random.normal(ks[2], (D_OUT,), dtype=jnp.float32) * 0.01
        gate_w = jax.random.normal(ks[3], (NUM_TRUE + NUM_NULL, D_MODEL), dtype=jnp.float32) / np.sqrt(D_MODEL)
        lora_A = jax.random.normal(ks[4], (NUM_TRUE, RANK, D_MODEL), dtype=jnp.float32) / np.sqrt(D_MODEL)
        lora_B = jax.random.normal(ks[5], (NUM_TRUE, D_OUT, RANK), dtype=jnp.float32) * 0.01
        return {'x': x, 'base_w': base_w, 'base_b': base_b, 'gate_w': gate_w, 'lora_A': lora_A, 'lora_B': lora_B}
    _L1_ffn_in = _L1_ffn_setup()
    _d = {'L0_attn_x': _L0_attn_in['x'], 'L0_attn_W_in': _L0_attn_in['W_in'], 'L0_attn_A_log': _L0_attn_in['A_log'], 'L0_attn_dt_bias': _L0_attn_in['dt_bias'], 'L0_attn_B_norm_bias': _L0_attn_in['B_norm_bias'], 'L0_attn_C_norm_bias': _L0_attn_in['C_norm_bias'], 'L0_attn_W_out': _L0_attn_in['W_out'], 'L0_ffn_Wg': _L0_ffn_in['Wg'], 'L0_ffn_bg': _L0_ffn_in['bg'], 'L0_ffn_W1': _L0_ffn_in['W1'], 'L0_ffn_b1': _L0_ffn_in['b1'], 'L0_ffn_W2': _L0_ffn_in['W2'], 'L0_ffn_b2': _L0_ffn_in['b2'], 'L1_attn_Wq': _L1_attn_in['Wq'], 'L1_attn_bq': _L1_attn_in['bq'], 'L1_attn_Wk': _L1_attn_in['Wk'], 'L1_attn_bk': _L1_attn_in['bk'], 'L1_attn_Wv': _L1_attn_in['Wv'], 'L1_attn_bv': _L1_attn_in['bv'], 'L1_attn_Wo': _L1_attn_in['Wo'], 'L1_attn_bo': _L1_attn_in['bo'], 'L1_ffn_base_w': _L1_ffn_in['base_w'], 'L1_ffn_base_b': _L1_ffn_in['base_b'], 'L1_ffn_gate_w': _L1_ffn_in['gate_w'], 'L1_ffn_lora_A': _L1_ffn_in['lora_A'], 'L1_ffn_lora_B': _L1_ffn_in['lora_B']}
    _x0 = _d['L0_attn_x']
    _d['L0_attn_x'] = jax.random.normal(jax.random.fold_in(jax.random.key(seed), 1), (4, 1024, 128), dtype=_x0.dtype)
    del _x0
    return _d

def reference(L0_attn_x, L0_attn_W_in, L0_attn_A_log, L0_attn_dt_bias, L0_attn_B_norm_bias, L0_attn_C_norm_bias, L0_attn_W_out, L0_ffn_Wg, L0_ffn_bg, L0_ffn_W1, L0_ffn_b1, L0_ffn_W2, L0_ffn_b2, L1_attn_Wq, L1_attn_bq, L1_attn_Wk, L1_attn_bk, L1_attn_Wv, L1_attn_bv, L1_attn_Wo, L1_attn_bo, L1_ffn_base_w, L1_ffn_base_b, L1_ffn_gate_w, L1_ffn_lora_A, L1_ffn_lora_B):

    def _L0_attn_ref(x, W_in, A_log, dt_bias, B_norm_bias, C_norm_bias, W_out):
        import jax, jax.numpy as jnp
        import numpy as np
        D_MODEL = 128
        D_STATE = 64
        EXPAND = 2
        N_HEADS = 32
        NGROUPS = 1
        CHUNK = 128
        R = 2
        D_INNER = EXPAND * D_MODEL
        HEAD_DIM = D_INNER // N_HEADS
        BC = NGROUPS * D_STATE
        D_PROJ = D_INNER + D_INNER * R + BC * R + BC + 2 * N_HEADS + D_STATE // 2
        SCALE = (D_STATE * R) ** (-0.5)
        EPS = 1e-06
        NEG = -1e+30

        def _rms(x):
            return x * jax.lax.rsqrt(jnp.mean(x * x, axis=-1, keepdims=True) + EPS)

        def _rope(x, cos, sin):
            h = x.shape[-1] // 2
            x1, x2 = (x[..., :h], x[..., h:])
            return jnp.concatenate([x1 * cos - x2 * sin, x1 * sin + x2 * cos], axis=-1)
        B, T, _ = x.shape
        L = CHUNK
        NC = T // L
        G, H, N, P = (NGROUPS, N_HEADS, D_STATE, HEAD_DIM)
        E = H // G
        proj = x @ W_in
        o = 0
        z = proj[..., :D_INNER]
        o = D_INNER
        x_raw = proj[..., o:o + D_INNER * R]
        o += D_INNER * R
        Bm = proj[..., o:o + BC * R]
        o += BC * R
        Cm = proj[..., o:o + BC]
        o += BC
        dt_raw = proj[..., o:o + H]
        o += H
        lam_raw = proj[..., o:o + H]
        o += H
        theta = proj[..., o:]
        x_raw = jax.nn.silu(x_raw)
        Bm = _rms(Bm.reshape(B, T, G, R, N)) * B_norm_bias[:, None, :]
        Cm = _rms(Cm.reshape(B, T, G, N)) * C_norm_bias
        A = -jnp.exp(A_log)
        dt = jnp.clip(jax.nn.softplus(dt_raw + dt_bias), 0.0001, 0.5)
        ang = -jnp.cumsum(jnp.mean(dt, axis=-1, keepdims=True) * theta, axis=1)
        cos, sin = (jnp.cos(ang), jnp.sin(ang))
        Cr = _rope(Cm, cos[:, :, None, :], sin[:, :, None, :])
        Br = _rope(Bm, cos[:, :, None, None, :], sin[:, :, None, None, :])
        xh = x_raw.reshape(B, T, H, R, P)
        log_dA = dt * A
        alpha = jnp.exp(log_dA)
        lam = jax.nn.sigmoid(lam_raw)
        xg = (lam * dt)[..., None, None] * xh
        x_prev = jnp.pad(xh, ((0, 0), (1, 0), (0, 0), (0, 0), (0, 0)))[:, :T]
        xb = ((1.0 - lam) * dt * alpha)[..., None, None] * x_prev
        Bb = jnp.pad(Br, ((0, 0), (1, 0), (0, 0), (0, 0), (0, 0)))[:, :T]

        def ch(a):
            return a.reshape(B, NC, L, *a.shape[2:])
        cum = jnp.cumsum(ch(log_dA), axis=2)
        mask = jnp.tril(jnp.ones((L, L), bool))
        diff = cum[:, :, :, None, :] - cum[:, :, None, :, :]
        dmat = jnp.exp(jnp.where(mask[None, None, :, :, None], diff, NEG))
        Cc = ch(Cr)
        Bgc, Bbc = (ch(Br), ch(Bb))
        xgc = ch(xg).reshape(B, NC, L, G, E, R, P)
        xbc = ch(xb).reshape(B, NC, L, G, E, R, P)
        sg = jnp.einsum('bclgn,bcmgrn->bclmgr', Cc, Bgc) * SCALE
        sb = jnp.einsum('bclgn,bcmgrn->bclmgr', Cc, Bbc) * SCALE
        dg = dmat.reshape(B, NC, L, L, G, E)
        y_intra = jnp.einsum('bclmgr,bclmge,bcmgerp->bclgep', sg, dg, xgc) + jnp.einsum('bclmgr,bclmge,bcmgerp->bclgep', sb, dg, xbc)
        dec_end = jnp.exp(cum[:, :, -1:, :] - cum).reshape(B, NC, L, G, E)
        st = (jnp.einsum('bclge,bclgrn,bclgerp->bcgenp', dec_end, Bgc, xgc) + jnp.einsum('bclge,bclgrn,bclgerp->bcgenp', dec_end, Bbc, xbc)).reshape(B, NC, H, N, P)
        cdec = jnp.exp(cum[:, :, -1, :])

        def step(S, inp):
            cd, s = inp
            return (cd[..., None, None] * S + s, S)
        _, Sprev = jax.lax.scan(step, jnp.zeros((B, H, N, P), x.dtype), (jnp.moveaxis(cdec, 1, 0), jnp.moveaxis(st, 1, 0)))
        Sprev = jnp.moveaxis(Sprev, 0, 1).reshape(B, NC, G, E, N, P)
        dec_in = jnp.exp(cum).reshape(B, NC, L, G, E)
        y_inter = SCALE * jnp.einsum('bclgn,bclge,bcgenp->bclgep', Cc, dec_in, Sprev)
        y = (y_intra + y_inter).reshape(B, T, D_INNER)
        y = _rms(y * jax.nn.silu(z))
        return y @ W_out

    def _L0_ffn_ref(x, Wg, bg, W1, b1, W2, b2):
        import jax, jax.numpy as jnp
        import numpy as np
        B, T, D, H, E, K = (2, 256, 128, 512, 8, 2)
        EPS = 1e-12

        def moe_forward(x, Wg, bg, W1, b1, W2, b2):
            gates = jax.nn.softmax(x @ Wg + bg, axis=-1)
            _, top_idx = jax.lax.top_k(gates, K)
            mask = jax.nn.one_hot(top_idx, E, dtype=gates.dtype).sum(axis=-2)
            g = gates * mask
            g = g / jnp.maximum(jnp.sum(jnp.abs(g), axis=-1, keepdims=True), EPS)
            h = jnp.einsum('btd,edh->bteh', x, W1) + b1[None, None]
            h = jax.nn.gelu(h, approximate=False)
            eo = jnp.einsum('bteh,ehd->bted', h, W2) + b2[None, None]
            return jnp.einsum('bte,bted->btd', g, eo)
        return moe_forward(x, Wg, bg, W1, b1, W2, b2)

    def _L1_attn_ref(x, Wq, bq, Wk, bk, Wv, bv, Wo, bo):
        import jax, jax.numpy as jnp
        import numpy as np
        D_MODEL = 128
        NHEAD = 16
        D_K = D_MODEL // NHEAD
        SCALE = 1.0 / np.sqrt(D_K * 2.0)
        TEMP = 1.5
        EPS = 1e-08

        def _l2norm(t):
            n = jnp.sqrt(jnp.sum(t * t, axis=-1, keepdims=True))
            return t / jnp.maximum(n, EPS)
        B, T, D = x.shape

        def heads(W, b):
            y = x @ W.T + b
            return y.reshape(B, T, NHEAD, D_K).transpose(0, 2, 1, 3)
        q = _l2norm(heads(Wq, bq))
        k = _l2norm(heads(Wk, bk))
        v = heads(Wv, bv)
        scores = jnp.einsum('bhqd,bhkd->bhqk', q, k) * SCALE
        scores = jnp.clip(scores, -5.0, 5.0)
        causal = jnp.triu(jnp.ones((T, T), dtype=bool), k=1)
        scores = jnp.where(causal[None, None], -10000.0, scores)
        attn = jax.nn.softmax(scores / TEMP, axis=-1)
        out = jnp.einsum('bhqk,bhkd->bhqd', attn, v)
        out = out.transpose(0, 2, 1, 3).reshape(B, T, D)
        return (out @ Wo.T + bo) * 0.5

    def _L1_ffn_ref(x, base_w, base_b, gate_w, lora_A, lora_B):
        import jax, jax.numpy as jnp
        import numpy as np
        D_MODEL = 128
        D_OUT = 128
        RANK = 16
        NUM_TRUE = 8
        NUM_NULL = 2
        TOP_K = 2
        SCALING = 32.0 / 16.0
        xf = x.reshape(-1, x.shape[-1])
        logits = jnp.einsum('td,ed->te', xf, gate_w)
        probs = jax.nn.softmax(logits, axis=-1)
        weights, selected = jax.lax.top_k(probs, TOP_K)
        true_mask = (selected < NUM_TRUE).astype(weights.dtype)
        tw = weights * true_mask
        denom = tw.sum(axis=-1, keepdims=True)
        denom = jnp.where(denom > 0, denom, jnp.ones_like(denom))
        nw = tw / denom
        onehot = jax.nn.one_hot(selected, NUM_TRUE, dtype=nw.dtype)
        ew = jnp.einsum('tk,tke->te', nw, onehot)
        z = jnp.einsum('td,erd->ter', xf, lora_A)
        moe = jnp.einsum('ter,te,eor->to', z, ew, lora_B) * SCALING
        base = jnp.einsum('td,od->to', xf, base_w) + base_b
        out = (base + moe).reshape(x.shape[:-1] + (D_OUT,))
        return out
    x = L0_attn_x
    x = x + 0.5 * _L0_ffn_ref(_layernorm(x, axis=-1), L0_ffn_Wg, L0_ffn_bg, L0_ffn_W1, L0_ffn_b1, L0_ffn_W2, L0_ffn_b2)
    x = x + _L0_attn_ref(_layernorm(x, axis=-1), L0_attn_W_in, L0_attn_A_log, L0_attn_dt_bias, L0_attn_B_norm_bias, L0_attn_C_norm_bias, L0_attn_W_out)
    x = x + 0.5 * _L0_ffn_ref(_layernorm(x, axis=-1), L0_ffn_Wg, L0_ffn_bg, L0_ffn_W1, L0_ffn_b1, L0_ffn_W2, L0_ffn_b2)
    x = x + 0.5 * _L1_ffn_ref(_layernorm(x, axis=-1), L1_ffn_base_w, L1_ffn_base_b, L1_ffn_gate_w, L1_ffn_lora_A, L1_ffn_lora_B)
    x = x + _L1_attn_ref(_layernorm(x, axis=-1), L1_attn_Wq, L1_attn_bq, L1_attn_Wk, L1_attn_bk, L1_attn_Wv, L1_attn_bv, L1_attn_Wo, L1_attn_bo)
    x = x + 0.5 * _L1_ffn_ref(_layernorm(x, axis=-1), L1_ffn_base_w, L1_ffn_base_b, L1_ffn_gate_w, L1_ffn_lora_A, L1_ffn_lora_B)
    return x

_drawn_inputs = setup_inputs


def setup_inputs(seed=0):
    import zlib

    import numpy as np

    out = dict(_drawn_inputs(seed))
    spreads = {'L1_attn_bq': (0.0, 0.8),
     'L1_attn_bk': (0.0, 0.8),
     'L1_attn_bv': (0.0, 0.8),
     'L1_attn_bo': (0.0, 0.1)}
    factors = {'L0_ffn_b1': 3.933,
     'L0_ffn_b2': 2.998,
     'L1_attn_Wq': 8.0,
     'L1_attn_Wk': 8.0,
     'L1_attn_Wv': 8.0,
     'L1_attn_Wo': 5.661,
     'L1_ffn_base_b': 7.987}
    for name, (base, spread) in spreads.items():
        noise = np.random.default_rng([zlib.crc32(name.encode()), seed]).standard_normal(out[name].shape)
        drawn = base * np.exp(spread * noise) if base else spread * noise
        out[name] = jnp.asarray(drawn.astype(out[name].dtype))
    for name, factor in factors.items():
        out[name] = (out[name] * factor).astype(out[name].dtype)
    return out
```

```python
from contextlib import ExitStack

import numpy as np

import concourse.bass as bass
from concourse import mybir

ALU = mybir.AluOpType
ACT = mybir.ActivationFunctionType
F32 = mybir.dt.float32
F16 = mybir.dt.float16
AX_X = mybir.AxisListType.X

P = 128
D = 128
BATCHES, TIME = 4, 1024
TILES = BATCHES * TIME // P
BATCH_TILES = TIME // P
GROUP = 4
GROUPS = TILES // GROUP
LN_EPS = 1e-5


class Chain:

    def __init__(self, eng, sem):
        self.eng, self.sem, self.base, self.n = eng, sem, 0, 0

    def link(self, ins):
        ins.then_inc(self.sem, 1)
        self.n += 1
        self.eng.wait_ge(self.sem, self.base + self.n)

    def enter(self, before, i, per):
        self.base, self.n, self.per = i * per + before, 0, per

    def leave(self, before, count):
        assert self.n == self.per, (self.n, self.per)
        self.base, self.n = 0, before + count * self.per


class Core:

    def __init__(self, nc, ctx, x_in, consts):
        self.nc, self.ctx, self.used = nc, ctx, []
        self.x = ctx.enter_context(nc.sbuf_tensor("x_res", [P, TILES, D], F32))
        self.ident = ctx.enter_context(nc.sbuf_tensor("ident", [P, P], F32))
        self.stats = ctx.enter_context(nc.sbuf_tensor("ln_stats", [P, TILES, 6], F32))
        self.mean = ctx.enter_context(nc.sbuf_tensor("ln_mean", [P, TILES], F32))
        self.rstd = ctx.enter_context(nc.sbuf_tensor("ln_rstd", [P, TILES], F32))
        self.tmp1 = ctx.enter_context(nc.sbuf_tensor("ln_tmp1", [P, TILES], F32))
        self.tmp2 = ctx.enter_context(nc.sbuf_tensor("ln_tmp2", [P, TILES], F32))
        self.minus_half = ctx.enter_context(nc.sbuf_tensor("minus_half", [P, 256], F32))
        self.warm = ctx.enter_context(nc.sbuf_tensor("warm", [P, 1], F32))
        self.x_loaded = self.sem("x_loaded")
        self.half_ready = self.sem("half_ready")
        self.passed = self.sem("waits_passed")
        with nc.Block() as block:
            @block.gpsimd
            def _(pool):
                nc.gpsimd.memset(self.minus_half[:], -0.5).then_inc(self.half_ready, 1)

            @block.sync
            def _(sp):
                sp.wait_ge(self.half_ready, 1)
                sp.dma_start(self.x[:], x_in.rearrange("b (t p) d -> p (b t) d", p=P)).then_inc(self.x_loaded, 16)
                sp.dma_start(self.ident[:], consts["ident"]).then_inc(self.x_loaded, 16)
                sp.wait_ge(self.x_loaded, 32)

    def sem(self, name):
        return self.ctx.enter_context(self.nc.semaphore(name))

    def scoped_sem(self, ctx, name):
        handle = ctx.enter_context(self.nc.semaphore(name))
        self.used.append(handle)
        return handle

    def clear(self):
        with self.nc.Block() as block:
            @block.gpsimd
            def _(pool):
                for handle in self.used:
                    pool.sem_clear(handle)
        self.used = []

    def ln_stats(self, dve, chain, sem, var_ready, rstd_ready, tiles=TILES, first=0):
        v = self.nc.vector
        with dve.Fori(0, tiles) as t:
            v.bn_stats(self.stats[:, bass.ds(t + first, 1), :].rearrange("p a b -> p (a b)"),
                       self.x[:, bass.ds(t + first, 1), :].rearrange("p a b -> p (a b)")).then_inc(sem, 1)
        dve.wait_ge(sem, tiles)
        ts = slice(first, first + tiles)
        even, odd = self.stats[:, ts, 1], self.stats[:, ts, 4]
        half, var = self.tmp1[:, ts], self.tmp2[:, ts]
        v.tensor_tensor(half, even, odd, ALU.subtract).then_inc(chain.sem, 1)
        v.tensor_tensor(self.mean[:, ts], even, odd, ALU.add).then_inc(chain.sem, 1)
        chain.n += 2
        chain.link(v.tensor_tensor(var, self.stats[:, ts, 2], self.stats[:, ts, 5], ALU.add))
        chain.link(v.tensor_tensor(half, half, half, ALU.mult))
        v.tensor_scalar(self.mean[:, ts], self.mean[:, ts], 0.5, None, ALU.mult).then_inc(chain.sem, 1)
        chain.n += 1
        chain.link(v.tensor_scalar(var, var, 1.0 / D, LN_EPS, ALU.mult, ALU.add))
        v.scalar_tensor_tensor(var, half, 0.25, var, ALU.mult, ALU.add).then_inc(var_ready, 1)
        dve.wait_ge(rstd_ready, 1)

    def ln_rsqrt(self, pool, var_ready, rstd_ready):
        pool.wait_ge(var_ready, 1)
        self.nc.gpsimd.tensor_tensor(self.rstd[:], self.tmp2[:], self.minus_half[:, 0:TILES], ALU.pow).then_inc(rstd_ready, 1)

    def normalize(self, out, t):
        return self.nc.vector.tensor_scalar(out, self.x[:, bass.ds(t, 1), :].rearrange("p a b -> p (a b)"),
                                            self.mean[:, bass.ds(t, 1)], self.rstd[:, bass.ds(t, 1)],
                                            ALU.subtract, ALU.mult)


def hold(eng, sem, value, passed):
    eng.wait_ge(sem, value)
    eng.sem_inc(passed, 1)


def flat(ap):
    return ap.rearrange("p a b -> p (a b)")


def select_top2(nc, chain, logits, both, left, eq, key, top, order, E):
    v = nc.vector
    shape = [P, TILES, E]
    order_b = order.unsqueeze(1).broadcast_to(shape)

    def pick(values):
        chain.link(v.tensor_reduce(top[:], values, AX_X, ALU.max))
        chain.link(v.tensor_tensor(eq, values, top[:].unsqueeze(2).broadcast_to(shape), ALU.is_equal))
        chain.link(v.tensor_tensor(key, eq, order_b, ALU.mult))

    pick(logits)
    chain.link(v.tensor_tensor(left, logits, top[:].unsqueeze(2).broadcast_to(shape), ALU.subtract))
    chain.link(v.tensor_reduce(top[:], key, AX_X, ALU.max))
    chain.link(v.tensor_tensor(both, key, top[:].unsqueeze(2).broadcast_to(shape), ALU.is_equal))
    chain.link(v.scalar_tensor_tensor(flat(logits), flat(both), -1e30, flat(logits), ALU.mult, ALU.add))
    pick(logits)
    chain.link(v.tensor_reduce(top[:], key, AX_X, ALU.max))
    chain.link(v.tensor_tensor(key, key, top[:].unsqueeze(2).broadcast_to(shape), ALU.is_equal))
    chain.link(v.tensor_tensor(both, both, key, ALU.add))


def moe_ffn(core, tag, Wg, bg, W1, b1, W2, b2, order_in):
    nc = core.nc
    E, _, H = W1.shape
    HC = H // P
    with ExitStack() as ctx:
        def sb(name, shape, dt=F32):
            return ctx.enter_context(nc.sbuf_tensor(f"{tag}_{name}", shape, dt))

        def ps(name, shape, dt=F32):
            return ctx.enter_context(nc.psum_tensor(f"{tag}_{name}", shape, dt))

        def sem(name):
            return core.scoped_sem(ctx, f"{tag}_{name}")

        yT = sb("yT", [P, TILES * P])
        gates = sb("gates", [P, TILES, E])
        b1T = sb("b1T", [P, E * HC])
        w1 = sb("w1", [P, 2, H])
        w2 = sb("w2", [P, 2, HC, D])
        w_loaded = [sem("w_loaded0"), sem("w_loaded1")]

        with ExitStack() as rctx:
            def rsb(name, shape, dt=F32):
                return rctx.enter_context(nc.sbuf_tensor(f"{tag}_{name}", shape, dt))

            def rps(name, shape, dt=F32):
                return rctx.enter_context(nc.psum_tensor(f"{tag}_{name}", shape, dt))

            y = rsb("y", [P, 2, GROUP, D])
            wg = rsb("wg", [P, E])
            bg_col = rsb("bg", [E, 1])
            b1_rows = rsb("b1_rows", [E * HC, P])
            b2_sb = rsb("b2", [E, D])
            order = rsb("order", [P, E])
            lgT = rsb("lgT", [E, 2, GROUP * P])
            gT = rsb("gT", [E, 2, GROUP * P])
            gstage = rsb("gstage", [P, 2, GROUP, E])
            logits = rsb("logits", [P, TILES, E])
            left = rsb("left", [P, TILES, E])
            eq = rsb("eq", [P, TILES, E])
            key = rsb("key", [P, TILES, E])
            both = rsb("both", [P, TILES, E])
            top = rsb("top", [P, TILES])
            ps_y = rps("ps_y", [P, 2, GROUP * P])
            ps_l = rps("ps_l", [P, 2, GROUP * P])
            ps_g = rps("ps_g", [P, 2, 512])
            small_loaded = sem("small_loaded")
            stat_done = sem("stat_done")
            dve_chain = sem("dve_chain")
            var_ready = sem("var_ready")
            rstd_ready = sem("rstd_ready")
            y_ready = sem("y_ready")
            y_turned = sem("y_turned")
            yT_ready = sem("yT_ready")
            lg_done = sem("lg_done")
            lgT_ready = sem("lgT_ready")
            lg_turned = sem("lg_turned")
            logits_ready = sem("logits_ready")
            left_ready = sem("left_ready")
            exp_ready = sem("exp_ready")
            b1_turned = sem("b1_turned")
            b1T_ready = sem("b1T_ready")
            gstage_ready = sem("gstage_ready")
            g_turned = sem("g_turned")
            gT_ready = sem("gT_ready")
            bias_done = sem("bias_done")
            bias_added = sem("bias_added")

            with nc.Block() as block:
                @block.gpsimd
                def _(pool):
                    core.ln_rsqrt(pool, var_ready, rstd_ready)

                @block.sync
                def _(sp):
                    sp.dma_start(wg[:], Wg).then_inc(small_loaded, 16)
                    sp.dma_start(bg_col[:], bg.unsqueeze(1)).then_inc(small_loaded, 16)
                    sp.dma_start(b1_rows[:], b1.rearrange("e (c h) -> (e c) h", c=HC)).then_inc(small_loaded, 16)
                    sp.dma_start(b2_sb[:], b2).then_inc(small_loaded, 16)
                    sp.dma_start(order[:], order_in[:, 0:E]).then_inc(small_loaded, 16)
                    for e in range(2):
                        sp.dma_start(w1[:, e, :], W1[e]).then_inc(w_loaded[e % 2], 16)
                        sp.dma_start(w2[:, e], W2[e].rearrange("(c h) d -> h c d", c=HC)).then_inc(w_loaded[e % 2], 16)

                @block.vector
                def _(dve):
                    chain = Chain(dve, dve_chain)
                    dve.sem_inc(lg_done, 2)
                    dve.sem_inc(gT_ready, 2)
                    core.ln_stats(dve, chain, stat_done, var_ready, rstd_ready)
                    with dve.Fori(0, GROUPS // 2) as g2:
                        for par in range(2):
                            g = g2 * 2 + par
                            dve.wait_ge(lg_done, g + 1)
                            for j in range(GROUP):
                                ins = core.normalize(y[:, par, j, :], g * GROUP + j)
                            ins.then_inc(y_ready, 1)
                    dve.wait_ge(logits_ready, GROUPS)
                    dve.wait_ge(small_loaded, 80)
                    select_top2(nc, chain, logits[:], both[:], left[:], eq[:], key[:], top, order[:], E)
                    nc.vector.tensor_copy(flat(left[:]), flat(left[:])).then_inc(left_ready, 1)
                    dve.wait_ge(exp_ready, 1)
                    v = nc.vector
                    chain.link(v.tensor_tensor(gates[:], eq[:], both[:], ALU.mult))
                    chain.link(v.tensor_reduce(top[:], gates[:], AX_X, ALU.add))
                    chain.link(v.tensor_scalar(top[:], top[:], 1e-12, 2.0, ALU.max, ALU.mult))
                    chain.link(v.reciprocal(top[:], top[:]))
                    chain.link(v.tensor_tensor(gates[:], gates[:], top[:].unsqueeze(2).broadcast_to([P, TILES, E]), ALU.mult))
                    with dve.Fori(0, GROUPS // 2) as g2:
                        for par in range(2):
                            g = g2 * 2 + par
                            dve.wait_ge(gT_ready, g + 1)
                            v.tensor_copy(gstage[:, par], gates[:, bass.ds(g * GROUP, GROUP), :]).then_inc(gstage_ready, 1)
                            dve.wait_ge(bias_done, g + 1)
                            xg = core.x[:, bass.ds(g * GROUP, GROUP), :]
                            v.tensor_tensor(xg, xg, ps_l[:, par, :].rearrange("p (t d) -> p t d", t=GROUP), ALU.add).then_inc(bias_added, 1)

                @block.tensor
                def _(pe):
                    t = nc.tensor
                    pe.wait_ge(small_loaded, 80)
                    t.transpose(ps_g[:, 0, 0:E * HC], b1_rows[:], core.ident[0:E * HC, 0:E * HC]).then_inc(b1_turned, 1)
                    pe.wait_ge(b1T_ready, 1)
                    with pe.Fori(0, GROUPS // 2) as g2:
                        for par in range(2):
                            g = g2 * 2 + par
                            pe.wait_ge(y_ready, g + 1)
                            for j in range(GROUP):
                                ins = t.transpose(ps_y[:, par, j * P:(j + 1) * P], y[:, par, j, :], core.ident[:])
                            ins.then_inc(y_turned, 1)
                            pe.wait_ge(yT_ready, g + 1)
                            t.matmul(ps_l[0:E, par, :], wg[:], yT[:, bass.ds(g * GROUP * P, GROUP * P)],
                                     start=True, stop=True).then_inc(lg_done, 1)
                            hold(pe, lgT_ready, g + 1, core.passed)
                            for j in range(GROUP):
                                ins = t.transpose(ps_g[:, par, j * E:(j + 1) * E], lgT[:, par, j * P:(j + 1) * P],
                                                  core.ident[0:E, 0:E])
                            ins.then_inc(lg_turned, 1)
                    with pe.Fori(0, GROUPS // 2) as g2:
                        for par in range(2):
                            g = g2 * 2 + par
                            pe.wait_ge(gstage_ready, g + 1)
                            for j in range(GROUP):
                                ins = t.transpose(ps_y[0:E, par, j * P:(j + 1) * P], gstage[:, par, j, :], core.ident[:])
                            ins.then_inc(g_turned, 1)
                            pe.wait_ge(gT_ready, g + 3)
                            for j in range(GROUP):
                                ins = t.matmul(ps_l[:, par, j * D:(j + 1) * D], gT[:, par, j * P:(j + 1) * P], b2_sb[:],
                                               start=True, stop=True)
                            ins.then_inc(bias_done, 1)

                @block.scalar
                def _(act):
                    s = nc.scalar
                    act.wait_ge(b1_turned, 1)
                    s.copy(b1T[:], ps_g[:, 0, 0:E * HC]).then_inc(b1T_ready, 1)
                    act.wait_ge(small_loaded, 80)
                    with act.Fori(0, GROUPS // 2) as g2:
                        for par in range(2):
                            g = g2 * 2 + par
                            act.wait_ge(y_turned, g + 1)
                            s.copy(yT[:, bass.ds(g * GROUP * P, GROUP * P)], ps_y[:, par, :]).then_inc(yT_ready, 1)
                            hold(act, lg_done, g + 3, core.passed)
                            s.activation(lgT[:, par, :], ps_l[0:E, par, :], ACT.Identity, bias=bg_col[:]).then_inc(lgT_ready, 1)
                            act.wait_ge(lg_turned, g + 1)
                            s.copy(logits[:, bass.ds(g * GROUP, GROUP), :],
                                   ps_g[:, par, 0:GROUP * E].rearrange("p (t e) -> p t e", t=GROUP)).then_inc(logits_ready, 1)
                    act.wait_ge(left_ready, 1)
                    s.activation(flat(eq[:]), flat(left[:]), ACT.Exp).then_inc(exp_ready, 1)
                    with act.Fori(0, GROUPS // 2) as g2:
                        for par in range(2):
                            g = g2 * 2 + par
                            act.wait_ge(g_turned, g + 1)
                            s.copy(gT[:, par, :], ps_y[0:E, par, :]).then_inc(gT_ready, 1)

        hT = sb("hT", [P, 2, HC, GROUP * P])
        ps_h = ps("ps_h", [P, HC, GROUP * P])
        ps_o = ps("ps_o", [P, 2, GROUP, D])
        h_done = sem("h_done")
        act_done = sem("act_done")
        out_done = sem("out_done")
        added = sem("added")

        with nc.Block() as block:
            @block.sync
            def _(sp):
                for e in range(2, E):
                    sp.wait_ge(out_done, (e - 1) * GROUPS)
                    sp.dma_start(w1[:, e % 2, :], W1[e]).then_inc(w_loaded[e % 2], 16)
                    sp.dma_start(w2[:, e % 2], W2[e].rearrange("(c h) d -> h c d", c=HC)).then_inc(w_loaded[e % 2], 16)

            @block.tensor
            def _(pe):
                t = nc.tensor

                with pe.Fori(0, E // 2) as e2:
                    for slot in range(2):
                        e = e2 * 2 + slot
                        k0 = e * GROUPS
                        hold(pe, w_loaded[slot], e2 * 32 + 32, core.passed)
                        with pe.Fori(0, GROUPS // 2) as g2:
                            for par in range(2):
                                g = g2 * 2 + par
                                k = k0 + g
                                for c in range(HC):
                                    pe.wait_ge(act_done, k * HC + c + 1)
                                    t.matmul(ps_h[:, c, :], w1[:, slot, c * P:(c + 1) * P],
                                             yT[:, bass.ds(g * GROUP * P, GROUP * P)],
                                             start=True, stop=True).then_inc(h_done, 1)
                                for c in range(HC):
                                    pe.wait_ge(act_done, (k + 1) * HC + c + 1)
                                    if c == 0:
                                        pe.wait_ge(added, k + 1)
                                    for j in range(GROUP):
                                        ins = t.matmul(ps_o[:, par, j, :], hT[:, par, c, j * P:(j + 1) * P],
                                                       w2[:, slot, c, :], start=(c == 0 and j == 0),
                                                       stop=(c == HC - 1), skip_group_check=True)
                                ins.then_inc(out_done, 1)

            @block.scalar
            def _(act):
                act.sem_inc(act_done, HC)
                nc.scalar.activation(core.warm[:], core.minus_half[:, 0:1], ACT.Gelu).then_inc(core.passed, 1)
                with act.Fori(0, E // 2) as e2:
                    for slot in range(2):
                        e = e2 * 2 + slot
                        with act.Fori(0, GROUPS // 2) as g2:
                            for par in range(2):
                                k = e * GROUPS + g2 * 2 + par
                                hold(act, added, k + 1, core.passed)
                                for c in range(HC):
                                    hold(act, h_done, k * HC + c + 1, core.passed)
                                    nc.scalar.activation(hT[:, par, c, :], ps_h[:, c, :], ACT.Gelu,
                                                         bias=b1T[:, bass.ds(e * HC + c, 1)]).then_inc(act_done, 1)

            @block.vector
            def _(dve):
                dve.sem_inc(added, 2)
                with dve.Fori(0, E // 2) as e2:
                    for slot in range(2):
                        e = e2 * 2 + slot
                        with dve.Fori(0, GROUPS // 2) as g2:
                            for par in range(2):
                                g = g2 * 2 + par
                                k = e * GROUPS + g
                                dve.wait_ge(out_done, k + 1)
                                dve.wait_ge(added, k + 2)
                                for j in range(GROUP):
                                    tile = g * GROUP + j
                                    xt = flat(core.x[:, bass.ds(tile, 1), :])
                                    ins = nc.vector.scalar_tensor_tensor(
                                        xt, ps_o[:, par, j, :], flat(gates[:, bass.ds(tile, 1), bass.ds(e, 1)]), xt,
                                        ALU.mult, ALU.add)
                                ins.then_inc(added, 1)
        core.clear()


LEAF = 8
LEVELS = (8, 16, 32, 64)
LEAF_FLOOR = -18.0
TWO_PI = 2 * np.pi
PI_F32 = float(np.nextafter(np.float32(np.pi), np.float32(0)))
TWO_PI_HI = float(np.float32(6.28125))
TWO_PI_LO = float(np.float32(TWO_PI - 6.28125))
ROUND_MAGIC = 1.5 * 2.0 ** 23
DVE_LINKS = 58
RMS_EPS = 1e-6


def ssm_constants():
    k, t = np.meshgrid(np.arange(P), np.arange(P), indexing="ij")
    sums = np.zeros((P, 8, P), np.float32)
    mid = (t // LEAF) * LEAF + LEAF // 2 - 1
    sums[:, 0] = ((mid < k) & (k <= t)).astype(np.float32) - ((t < k) & (k <= mid)).astype(np.float32)
    for n, size in enumerate(LEVELS):
        mid = (t // (2 * size)) * 2 * size + size - 1
        sums[:, 1 + n] = ((mid < k) & (k <= t)) | ((t < k) & (k <= mid))
    sums[:, 5] = k <= t
    sums[:, 6] = k > t
    sums[:, 7] = 1
    shift = np.zeros((P, 2, P), np.float32)
    shift[:, 0] = k == t + 1
    shift[:, 1] = (k == 0) & (t == P - 1)
    m, l = k, t
    masks = np.zeros((P, 6, P), np.float32)
    same = m // LEAF == l // LEAF
    masks[:, 0] = same & (m <= l)
    masks[:, 1] = same & (m < l)
    for n, size in enumerate(LEVELS):
        masks[:, 2 + n] = (m // (2 * size) == l // (2 * size)) & (m // size % 2 == 0) & (l // size % 2 == 1)
    return {"sums": sums, "shift": shift, "masks": masks}


def ssm(core, tag, a, consts):
    nc = core.nc
    NT, H, N, R, PD = BATCH_TILES, 32, 64, 2, 8
    DI = H * PD
    XR = DI * R
    K_OUT, K_X = 6, 7
    SCALE = float((N * R) ** -0.5)
    W_in, W_out = a["L0_attn_W_in"], a["L0_attn_W_out"]
    DP = W_in.shape[1]
    v, s, t_, g_ = nc.vector, nc.scalar, nc.tensor, nc.gpsimd
    with ExitStack() as ctx:
        def sb(name, shape, dt=F32):
            return ctx.enter_context(nc.sbuf_tensor(f"{tag}_{name}", shape, dt))

        def sem(name):
            return core.scoped_sem(ctx, f"{tag}_{name}")

        win = sb("win", [P, DP])
        wout = sb("wout", [P, 2, D])
        sums = sb("sums", [P, 8, P])
        shift = sb("shift", [P, 2, P])
        masks = sb("masks", [P, 6, P])
        A_b = sb("A_b", [P, H])
        bias_b = sb("bias_b", [P, H])
        norm_b = sb("norm_b", [P, 3, N])
        y = sb("y", [P, 2, D])
        yT = sb("yT", [P, 2, P])
        zx = sb("zx", [P, NT, DI + XR])
        raw = sb("raw", [P, NT, 288])
        rot = sb("rot", [P, NT, 3, N])
        half = [sb(f"half{i}", [P, NT, 3, N // 2]) for i in range(2)]
        sm = {n: sb(n, [P, NT, H]) for n in ("u", "e", "dt", "lam", "g", "vn", "w", "ld", "ldf", "thm", "ang",
                                             "turn", "sin", "cos", "leafx", "carry", "el")}
        dtm = sb("dtm", [P, NT])
        ss = sb("ss", [P, NT * 3])
        rs = sb("rs", [P, NT * 3])
        outp = sb("outp", [P, NT, 8, H])
        xw = sb("xw", [P, NT, K_X, H])
        X = sb("X", [P, 2, K_X, XR])
        SM = sb("SM", [P, 2, 6, 2, P])
        Y6 = sb("Y6", [P, K_OUT, DI])
        ysum = sb("ysum", [P, DI])
        u = sb("u_out", [P, 2, DI])
        usq = sb("usq", [P, 2, DI])
        uT = sb("uT", [P, 2, 2, P])
        uss = sb("uss", [P, 2])
        ums = sb("ums", [P, 2])
        urs = sb("urs", [P, 2])
        bct = sb("bct", [N, 2, 3, P])
        state = sb("state", [N, 2, DI])
        bank = ctx.enter_context(nc.psum_tensor(f"{tag}_ps", [P, 8, 512], F32))
        ps_y = [bank[:, i, 0:P] for i in (0, 7)]
        ps_theta = [bank[:, i, 0:H] for i in (5, 6)]
        ps_exp = bank[:, 1:5, :].rearrange("p b c -> p (b c)")
        ps_ang = bank[:, 5, 0:256]
        ps_tot = bank[:, 5, 256:512]
        ps_vn = bank[:, 6, 0:256]
        ps_t = [bank[0:N, i, 0:3 * P].rearrange("p (j d) -> p j d", j=3) for i in (0, 7)]
        ps_s = bank[:, 6, :].rearrange("p (s r l) -> p s r l", s=2, r=2)
        ps_o = bank[:, 1:4, :].rearrange("p b c -> p (b c)")
        ps_st = bank[0:N, 4, 0:DI]
        ps_u = bank[:, 5, 0:256].rearrange("p (i d) -> p i d", i=2)
        ps_r = bank[:, 5, 256:384]

        names = ("loaded stat_done dve_chain var_ready rstd_ready setup A_ready y_ready y_turned yT_ready proj_done "
                 "silu_done raw_done dt_in_ready dt_exp lam_in_ready lam_exp sp_ready ln_done coef_in sums_done v_ready "
                 "v_done exp_ready leafx_ready thm_ready ang_done r_ready sin_ready ss_ready rs_ready rot_ready "
                 "bc_turned bct_ready s_done sm_ready x_ready outs_done st_done scaled state_ready u_ready u_turned uT_ready "
                 "uss_ready urs_ready r_done added ums_ready w_ready").split()
        S = {n: sem(n) for n in names}

        class Eng:

            def __init__(self, eng, b):
                self.eng, self.b = eng, b

            def wait(self, name, n, per, extra=0):
                hold(self.eng, S[name], self.b * per + (n + extra), core.passed)

        with nc.Block() as block:
            @block.sync
            def _(sp):
                for dst, src in ((win[:], W_in), (wout[:], W_out.rearrange("(i p) d -> p i d", p=P)),
                                 (sums[:], consts["sums"]), (shift[:], consts["shift"]), (masks[:], consts["masks"]),
                                 (A_b[:], a["L0_attn_A_log"].unsqueeze(0).broadcast_to([P, H])),
                                 (bias_b[:], a["L0_attn_dt_bias"].unsqueeze(0).broadcast_to([P, H])),
                                 (norm_b[:, 0, :], a["L0_attn_B_norm_bias"].broadcast_to([P, N])),
                                 (norm_b[:, 1, :], a["L0_attn_B_norm_bias"].broadcast_to([P, N])),
                                 (norm_b[:, 2, :], a["L0_attn_C_norm_bias"].broadcast_to([P, N]))):
                    sp.dma_start(dst, src).then_inc(S["loaded"], 16)

            LOADS = 160

            @block.gpsimd
            def _(pool):
                core.ln_rsqrt(pool, S["var_ready"], S["rstd_ready"])
                with pool.Fori(0, BATCHES) as b:
                    E = Eng(pool, b)
                    E.wait("ss_ready", 1, 1)
                    g_.tensor_tensor(rs[:], ss[:], core.minus_half[:, 0:NT * 3], ALU.pow).then_inc(S["rs_ready"], 1)
                    for i in range(NT):
                        E.wait("uss_ready", i + 1, NT)
                        if i % 2 == 0 and i == 0:
                            pass
                        g_.tensor_scalar(ums[:, i % 2:i % 2 + 1], uss[:, i % 2:i % 2 + 1], 1.0 / DI, RMS_EPS,
                                         ALU.mult, ALU.add).then_inc(S["ums_ready"], 1)
                        E.wait("ums_ready", i + 1, NT)
                        g_.tensor_tensor(urs[:, i % 2:i % 2 + 1], ums[:, i % 2:i % 2 + 1], core.minus_half[:, 0:1],
                                         ALU.pow).then_inc(S["urs_ready"], 1)

            @block.scalar
            def _(act):
                act.wait_ge(S["loaded"], LOADS)
                s.activation(A_b[:], A_b[:], ACT.Exp).then_inc(S["A_ready"], 1)
                with act.Fori(0, BATCHES) as b:
                    E = Eng(act, b)
                    E.wait("added", 1, NT)
                    for i in range(NT):
                        E.wait("y_turned", i + 1, NT)
                        s.copy(yT[:, i % 2, :], ps_y[i % 2]).then_inc(S["yT_ready"], 1)
                        E.wait("proj_done", i + 1, NT)
                        s0 = 1 + 2 * (i % 2)
                        s.activation(zx[:, i, 0:512], bank[:, s0, :], ACT.Silu).then_inc(S["silu_done"], 1)
                        s.activation(zx[:, i, 512:768], bank[:, s0 + 1, 0:256], ACT.Silu).then_inc(S["silu_done"], 1)
                    E.wait("dt_in_ready", 1, 1)
                    s.activation(sm["e"][:], sm["u"][:], ACT.Exp).then_inc(S["dt_exp"], 1)
                    E.wait("lam_in_ready", 1, 1)
                    s.activation(sm["el"][:], sm["lam"][:], ACT.Exp, scale=-1.0).then_inc(S["lam_exp"], 1)
                    E.wait("dt_exp", 1, 1)
                    s.activation(sm["u"][:], sm["e"][:], ACT.Ln, bias=1.0).then_inc(S["ln_done"], 1)
                    E.wait("sums_done", 1, 1)
                    s.activation(outp[:].rearrange("p t k h -> p k t h"),
                                 ps_exp.rearrange("p (k t h) -> p k t h", k=8, t=NT), ACT.Exp).then_inc(S["exp_ready"], 1)
                    s.activation(sm["leafx"][:], ps_exp[:, 0:256].rearrange("p (t h) -> p t h", t=NT), ACT.Exp,
                                 scale=-1.0).then_inc(S["leafx_ready"], 1)
                    E.wait("r_ready", 1, 1)
                    s.activation(sm["sin"][:], sm["ang"][:], ACT.Sin).then_inc(S["sin_ready"], 1)
                    s.activation(sm["cos"][:], sm["ang"][:], ACT.Sin, scale=0.5).then_inc(S["sin_ready"], 1)
                    def copy_bct(i):
                        E.wait("bc_turned", i + 1, NT)
                        s.copy(bct[:, i % 2], ps_t[i % 2]).then_inc(S["bct_ready"], 1)

                    def turn_u(j):
                        E.wait("u_ready", j + 1, NT)
                        if j >= 2:
                            E.wait("urs_ready", j - 1, NT)
                        s.activation(usq[:, j % 2, :], u[:, j % 2, :], ACT.Square,
                                     accum_out=uss[:, j % 2:j % 2 + 1]).then_inc(S["uss_ready"], 1)
                        E.wait("u_turned", j + 1, NT)
                        s.copy(uT[:, j % 2], ps_u).then_inc(S["uT_ready"], 1)

                    copy_bct(0)
                    for i in range(NT):
                        if i + 1 < NT:
                            copy_bct(i + 1)
                        if i >= 1:
                            turn_u(i - 1)
                    turn_u(NT - 1)

            @block.tensor
            def _(pe):
                pe.wait_ge(S["loaded"], LOADS)
                with pe.Fori(0, BATCHES) as b:
                    E = Eng(pe, b)
                    for i in range(NT):
                        E.wait("y_ready", i + 1, NT)
                        if i == 0:
                            E.wait("added", 1, NT)
                        t_.transpose(ps_y[i % 2], y[:, i % 2, :], core.ident[:]).then_inc(S["y_turned"], 1)
                        E.wait("yT_ready", i + 1, NT)
                        if i >= 2:
                            E.wait("silu_done", 2 * (i - 1), 2 * NT)
                            E.wait("raw_done", 2 * (i - 1), 2 * NT)
                        s0 = 1 + 2 * (i % 2)
                        lhsT = yT[:, i % 2, :]
                        t_.matmul(bank[:, s0, :], lhsT, win[:, 0:512], start=True, stop=True)
                        t_.matmul(bank[:, s0 + 1, :], lhsT, win[:, 512:1024], start=True, stop=True)
                        t_.matmul(ps_theta[i % 2], lhsT, win[:, 1024:DP], start=True,
                                  stop=True).then_inc(S["proj_done"], 1)
                    E.wait("coef_in", 1, 1)
                    E.wait("silu_done", 2 * NT, 2 * NT)
                    E.wait("raw_done", 2 * NT, 2 * NT)
                    for k in range(8):
                        ins = t_.matmul(ps_exp[:, k * 256:(k + 1) * 256], sums[:, k, :],
                                        (sm["ldf"] if k == 0 else sm["ld"])[:].rearrange("p t h -> p (t h)"),
                                        start=True, stop=True)
                    ins.then_inc(S["sums_done"], 1)
                    thm = sm["thm"][:].rearrange("p t h -> p (t h)")
                    t_.matmul(ps_ang, sums[:, 5, :], thm, start=True, stop=True)
                    t_.matmul(ps_tot, sums[:, 7, :], thm, start=True, stop=True).then_inc(S["ang_done"], 1)
                    vn = sm["vn"][:].rearrange("p t h -> p (t h)")
                    t_.matmul(ps_vn, shift[:, 0, :], vn, start=True, stop=False, skip_group_check=True)
                    t_.matmul(ps_vn[:, 0:(NT - 1) * H], shift[:, 1, :], vn[:, H:NT * H], start=False, stop=True,
                              skip_group_check=True).then_inc(S["v_done"], 1)
                    E.wait("rot_ready", 1, 1)
                    E.wait("w_ready", 1, 1)

                    def turn(i):
                        if i >= 2:
                            E.wait("bct_ready", i - 1, NT)
                        for j in range(3):
                            ins = t_.transpose(ps_t[i % 2][:, j, :], rot[:, i, j, :], core.ident[:])
                        ins.then_inc(S["bc_turned"], 1)

                    def dots(i):
                        E.wait("bct_ready", i + 1, NT)
                        if i >= 2:
                            E.wait("sm_ready", i - 1, NT)
                        for r in range(R):
                            ins = t_.matmul(ps_s[:, i % 2, r, :], bct[:, i % 2, r, :], bct[:, i % 2, 2, :],
                                            start=True, stop=True)
                        ins.then_inc(S["s_done"], 1)

                    def xr(i, k, r):
                        return X[:, i % 2, k, :].rearrange("p (h r d) -> p h r d", h=H, r=R)[:, :, r, :]

                    def close(j):
                        E.wait("u_ready", j + 1, NT)
                        if j >= 1:
                            E.wait("added", j, NT, 1)
                        for i2 in range(2):
                            ins = t_.transpose(ps_u[:, i2, :], u[:, j % 2, i2 * P:(i2 + 1) * P], core.ident[:])
                        ins.then_inc(S["u_turned"], 1)
                        E.wait("uT_ready", j + 1, NT)
                        for i2 in range(2):
                            ins = t_.matmul(ps_r, uT[:, j % 2, i2, :], wout[:, i2, :], start=(i2 == 0), stop=(i2 == 1))
                        ins.then_inc(S["r_done"], 1)

                    turn(0)
                    dots(0)
                    for i in range(NT):
                        if i + 1 < NT:
                            turn(i + 1)
                        E.wait("x_ready", i + 1, NT)
                        E.wait("sm_ready", i + 1, NT)
                        if i >= 1:
                            E.wait("scaled", i, NT)
                            E.wait("state_ready", i, NT)
                        else:
                            E.wait("exp_ready", 1, 1)
                            E.wait("leafx_ready", 1, 1)
                        for k in range(6):
                            o = 0 if k < 2 else k - 1
                            for r in range(R):
                                t_.matmul(ps_o[:, o * DI:(o + 1) * DI], SM[:, i % 2, k, r, :], xr(i, k, r),
                                          start=(k != 1 and r == 0), stop=(k != 0 and r == 1), skip_group_check=True)
                        for r in range(R):
                            ins = t_.matmul(ps_st, rot[:, i, r, :], xr(i, 6, r), start=(r == 0), stop=(r == 1))
                        ins.then_inc(S["st_done"], 1)
                        t_.matmul(ps_o[:, 5 * DI:6 * DI], bct[:, i % 2, 2, :], state[:, i % 2, :],
                                  start=True, stop=True).then_inc(S["outs_done"], 1)
                        if i + 1 < NT:
                            dots(i + 1)
                        if i >= 1:
                            close(i - 1)
                    close(NT - 1)

            @block.vector
            def _(dve):
                dve.sem_inc(S["added"], 1)
                chain = Chain(dve, S["dve_chain"])
                core.ln_stats(dve, chain, S["stat_done"], S["var_ready"], S["rstd_ready"])
                dve.wait_ge(S["loaded"], LOADS)
                dve.wait_ge(S["A_ready"], 1)
                chain.link(v.tensor_scalar(A_b[:], A_b[:], -1.0, None, ALU.mult))
                v.memset(sm["carry"][:, 0, :], 0.0).then_inc(S["dve_chain"], 1)
                chain.n += 1
                chain.link(v.tensor_scalar(norm_b[:, 2, :], norm_b[:, 2, :], SCALE, None, ALU.mult))
                before = chain.n
                with dve.Fori(0, BATCHES) as b:
                    E = Eng(dve, b)
                    chain.enter(before, b, DVE_LINKS)
                    for i in range(NT + 1):
                        if i < NT:
                            if i >= 2:
                                E.wait("y_turned", i - 1, NT)
                            core.normalize(y[:, i % 2, :], b * NT + i).then_inc(S["y_ready"], 1)
                        if i >= 1:
                            j = i - 1
                            E.wait("silu_done", 2 * (j + 1), 2 * NT)
                            v.tensor_copy(raw[:, j, 0:256], bank[:, 2 + 2 * (j % 2), 256:512]).then_inc(S["raw_done"], 1)
                            v.tensor_copy(raw[:, j, 256:288], ps_theta[j % 2]).then_inc(S["raw_done"], 1)
                    E.wait("raw_done", 2 * NT, 2 * NT)
                    T3 = [P, NT, H]
                    c = {n: x[:] for n, x in sm.items()}
                    chain.link(v.tensor_tensor(c["u"], raw[:, :, 192:224], bias_b[:].unsqueeze(1).broadcast_to(T3), ALU.add))
                    v.tensor_scalar(c["u"], c["u"], 30.0, None, ALU.min).then_inc(S["dt_in_ready"], 1)
                    v.tensor_scalar(c["lam"], raw[:, :, 224:256], -80.0, None, ALU.max).then_inc(S["lam_in_ready"], 1)
                    chain.link(v.tensor_tensor(rot[:].rearrange("p t j n -> p t (j n)"), raw[:, :, 0:192], raw[:, :, 0:192], ALU.mult))
                    chain.link(v.tensor_reduce(ss[:], rot[:].rearrange("p t j n -> p (t j) n"), AX_X, ALU.add))
                    v.tensor_scalar(ss[:], ss[:], 1.0 / N, RMS_EPS, ALU.mult, ALU.add).then_inc(S["ss_ready"], 1)
                    E.wait("ln_done", 1, 1)
                    chain.link(v.tensor_scalar(c["dt"], c["u"], 0.5, 0.0001, ALU.min, ALU.max))
                    E.wait("lam_exp", 1, 1)
                    chain.link(v.tensor_scalar(c["el"], c["el"], 1.0, None, ALU.add))
                    chain.link(v.reciprocal(c["lam"], c["el"]))
                    chain.link(v.tensor_tensor(c["ld"], c["dt"], A_b[:].unsqueeze(1).broadcast_to(T3), ALU.mult))
                    chain.link(v.tensor_scalar(c["ldf"], c["ld"], LEAF_FLOOR, None, ALU.max))
                    chain.link(v.tensor_tensor(c["g"], c["lam"], c["dt"], ALU.mult))
                    chain.link(v.tensor_scalar(c["lam"], c["lam"], -1.0, 1.0, ALU.mult, ALU.add))
                    chain.link(v.tensor_tensor(c["vn"], c["lam"], c["dt"], ALU.mult))
                    chain.link(v.tensor_reduce(dtm[:], c["dt"], AX_X, ALU.add))
                    chain.link(v.tensor_scalar(dtm[:], dtm[:], 1.0 / H, None, ALU.mult))
                    v.tensor_tensor(c["thm"], raw[:, :, 256:288], dtm[:].unsqueeze(2).broadcast_to(T3),
                                    ALU.mult).then_inc(S["coef_in"], 1)
                    E.wait("rs_ready", 1, 1)
                    bc3 = raw[:, :, 0:192].rearrange("p t (j n) -> p t j n", j=3)
                    chain.link(v.tensor_tensor(bc3, bc3, rs[:].rearrange("p (t j) -> p t j", j=3).unsqueeze(3)
                                               .broadcast_to([P, NT, 3, N]), ALU.mult))
                    chain.link(v.tensor_tensor(raw[:, :, 0:192], raw[:, :, 0:192],
                                               norm_b[:].rearrange("p j n -> p (j n)").unsqueeze(1)
                                               .broadcast_to([P, NT, 3 * N]), ALU.mult))
                    E.wait("ang_done", 1, 1)
                    tot = ps_tot.rearrange("p (t h) -> p t h", t=NT)
                    for i in range(1, NT):
                        chain.link(v.tensor_tensor(c["carry"][:, i, :], c["carry"][:, i - 1, :], tot[:, i - 1, :], ALU.add))
                    chain.link(v.tensor_tensor(c["ang"], c["carry"], ps_ang.rearrange("p (t h) -> p t h", t=NT), ALU.add))
                    chain.link(v.tensor_scalar(c["turn"], c["ang"], 1.0 / TWO_PI, ROUND_MAGIC, ALU.mult, ALU.add))
                    chain.link(v.tensor_scalar(c["turn"], c["turn"], ROUND_MAGIC, None, ALU.subtract))
                    chain.link(v.scalar_tensor_tensor(c["ang"], c["turn"], -TWO_PI_HI, c["ang"], ALU.mult, ALU.add))
                    chain.link(v.scalar_tensor_tensor(c["ang"], c["turn"], -TWO_PI_LO, c["ang"], ALU.mult, ALU.add))
                    v.tensor_scalar(c["ang"], c["ang"], PI_F32, -PI_F32, ALU.min, ALU.max).then_inc(S["r_ready"], 1)
                    E.wait("v_done", 1, 1)
                    E.wait("exp_ready", 1, 1)
                    E.wait("leafx_ready", 1, 1)
                    vn = ps_vn.rearrange("p (t h) -> p t h", t=NT)
                    chain.link(v.tensor_tensor(xw[:, :, 0, :], c["leafx"], c["g"], ALU.mult))
                    chain.link(v.tensor_tensor(xw[:, :, 1, :], c["leafx"], vn, ALU.mult))
                    chain.link(v.tensor_tensor(c["w"], c["g"], vn, ALU.add))
                    chain.link(v.tensor_tensor(xw[:, :, 2:6, :], outp[:, :, 1:5, :], c["w"].unsqueeze(2)
                                               .broadcast_to([P, NT, 4, H]), ALU.mult))
                    chain.link(v.tensor_tensor(xw[:, :, 6, :], outp[:, :, 6, :], c["w"], ALU.mult))
                    E.wait("sin_ready", 2, 2)
                    chain.link(v.tensor_tensor(c["cos"], c["cos"], c["cos"], ALU.mult))
                    chain.link(v.tensor_scalar(c["cos"], c["cos"], -2.0, 1.0, ALU.mult, ALU.add))
                    b1, b2 = bc3[:, :, :, 0:N // 2], bc3[:, :, :, N // 2:N]
                    cosb = c["cos"].unsqueeze(2).broadcast_to([P, NT, 3, N // 2])
                    sinb = c["sin"].unsqueeze(2).broadcast_to([P, NT, 3, N // 2])
                    for out_half, p, q, op in ((slice(0, N // 2), b1, b2, ALU.add), (slice(N // 2, N), b2, b1, ALU.subtract)):
                        chain.link(v.tensor_tensor(half[0][:], p, cosb, ALU.mult))
                        chain.link(v.tensor_tensor(half[1][:], q, sinb, ALU.mult))
                        chain.link(v.tensor_tensor(rot[:, :, :, out_half], half[0][:], half[1][:], op))
                    v.memset(state[:, 0, :], 0.0).then_inc(S["dve_chain"], 1)
                    chain.n += 1
                    chain.link(v.tensor_copy(dtm[:], dtm[:]))
                    v.tensor_copy(ss[:, 0:1], ss[:, 0:1]).then_inc(S["rot_ready"], 1)
                    v.tensor_copy(ss[:, 1:2], ss[:, 1:2]).then_inc(S["w_ready"], 1)

                    def weigh(i):
                        if i >= 2:
                            E.wait("outs_done", i - 1, NT)
                        xin = zx[:, i, 256:768].rearrange("p (h d) -> p h d", h=H).unsqueeze(1).broadcast_to([P, K_X, H, 16])
                        v.tensor_tensor(X[:, i % 2].rearrange("p k (h d) -> p k h d", h=H), xin,
                                        xw[:, i].unsqueeze(3).broadcast_to([P, K_X, H, 16]), ALU.mult).then_inc(S["x_ready"], 1)
                        E.wait("s_done", i + 1, NT)
                        v.tensor_tensor(SM[:, i % 2], ps_s[:, i % 2].unsqueeze(1).broadcast_to([P, 6, 2, P]),
                                        masks[:].unsqueeze(2).broadcast_to([P, 6, 2, P]), ALU.mult).then_inc(S["sm_ready"], 1)

                    def finish(j):
                        E.wait("r_done", j + 1, NT)
                        E.wait("urs_ready", j + 1, NT)
                        xt = flat(core.x[:, bass.ds(b * NT + j, 1), :])
                        v.scalar_tensor_tensor(xt, ps_r, urs[:, j % 2:j % 2 + 1], xt, ALU.mult, ALU.add).then_inc(S["added"], 1)

                    weigh(0)
                    for i in range(NT):
                        E.wait("outs_done", i + 1, NT)
                        chain.link(v.tensor_tensor(
                            state[:, (i + 1) % 2, :].rearrange("p (h d) -> p h d", h=H),
                            state[:, i % 2, :].rearrange("p (h d) -> p h d", h=H),
                            outp[0:N, i, 7, :].unsqueeze(2).broadcast_to([N, H, PD]), ALU.mult))
                        v.tensor_tensor(state[:, (i + 1) % 2, :], state[:, (i + 1) % 2, :], ps_st, ALU.add).then_inc(S["state_ready"], 1)
                        v.tensor_tensor(Y6[:].rearrange("p k (h d) -> p (k h) d", h=H),
                                        ps_o.rearrange("p (q d) -> p q d", d=PD),
                                        outp[:, i, 0:6, :].rearrange("p k h -> p (k h)").unsqueeze(2)
                                        .broadcast_to([P, K_OUT * H, PD]), ALU.mult).then_inc(S["scaled"], 1)
                        if i + 1 < NT:
                            weigh(i + 1)
                        E.wait("scaled", i + 1, NT)
                        chain.link(v.tensor_reduce(ysum[:], Y6[:].rearrange("p k f -> p f k"), AX_X, ALU.add))
                        if i >= 2:
                            E.wait("uss_ready", i - 1, NT)
                            E.wait("u_turned", i - 1, NT)
                        v.tensor_tensor(u[:, i % 2, :], ysum[:], zx[:, i, 0:256], ALU.mult).then_inc(S["u_ready"], 1)
                        if i >= 1:
                            finish(i - 1)
                    finish(NT - 1)
                    chain.leave(before, BATCHES)
        core.clear()


def turn_weights(nc, core, ctx, tag, names, loaded, loads, bank):
    turned, copied = core.scoped_sem(ctx, f"{tag}_w_turned"), core.scoped_sem(ctx, f"{tag}_w_copied")
    with nc.Block() as block:
        @block.tensor
        def _(pe):
            pe.wait_ge(loaded, loads)
            for n, (src, dst, cols) in enumerate(names):
                nc.tensor.transpose(bank[:, n, 0:cols], src, core.ident[0:cols, 0:cols]).then_inc(turned, 1)

        @block.scalar
        def _(act):
            for n, (src, dst, cols) in enumerate(names):
                act.wait_ge(turned, n + 1)
                nc.scalar.copy(dst, bank[:, n, 0:cols]).then_inc(copied, 1)
            act.wait_ge(copied, len(names))


def lora_ffn(core, tag, base_w, base_b, gate_w, lora_A, lora_B, order_in):
    nc = core.nc
    ET, RANK, _ = lora_A.shape
    E = gate_w.shape[0]
    v, s, t_, g_ = nc.vector, nc.scalar, nc.tensor, nc.gpsimd
    with ExitStack() as ctx:
        def sb(name, shape, dt=F32):
            return ctx.enter_context(nc.sbuf_tensor(f"{tag}_{name}", shape, dt))

        def sem(name):
            return core.scoped_sem(ctx, f"{tag}_{name}")

        bank = ctx.enter_context(nc.psum_tensor(f"{tag}_ps", [P, 8, 512], F32))
        rows = sb("rows", [P, 4, P])
        wcat = sb("wcat", [P, 2 * D + E])
        lB = sb("lB", [P, D])
        bias = sb("bias", [1, D])
        ones = sb("ones", [1, P])
        order = sb("order", [P, E])
        y = sb("y", [P, 2, GROUP, D])
        yT = sb("yT", [P, 2, GROUP * P])
        z = sb("z", [P, TILES, D])
        zw = sb("zw", [P, 2, GROUP, D])
        zwT = sb("zwT", [P, 2, GROUP * P])
        logits, left, eq, key, both = (sb(n, [P, TILES, E]) for n in ("logits", "left", "eq", "key", "both"))
        te = sb("te", [P, TILES, ET])
        top = sb("top", [P, TILES])
        zero = sb("zero", [P, TILES])
        names = ("loaded ones_ready stat_done var_ready rstd_ready dve_chain y_ready y_turned yT_ready proj_done "
                 "z_ready base_added left_ready exp_ready zw_ready zw_turned zwT_ready moe_done added").split()
        S = {n: sem(n) for n in names}
        with nc.Block() as block:
            @block.vector
            def _(dve):
                v.memset(ones[:], 1.0).then_inc(S["ones_ready"], 1)

            @block.sync
            def _(sp):
                sp.wait_ge(S["ones_ready"], 1)
                for dst, src in ((rows[:, 0, :], base_w), (rows[:, 1, :], lora_A.rearrange("e r d -> (e r) d")),
                                 (rows[0:E, 2, :], gate_w), (bias[:], base_b.unsqueeze(0)), (order[:], order_in[:, 0:E]),
                                 (rows[:, 3, :].rearrange("p (e r) -> p e r", e=ET), lora_B.rearrange("e o r -> o e r"))):
                    sp.dma_start(dst, src).then_inc(S["loaded"], 16)
        turn_weights(nc, core, ctx, tag, [(rows[:, 0, :], wcat[:, 0:D], P), (rows[:, 1, :], wcat[:, D:2 * D], P),
                                     (rows[0:E, 2, :], wcat[:, 2 * D:2 * D + E], E), (rows[:, 3, :], lB[:], P)],
                     S["loaded"], 96, bank)

        ps_y = [bank[:, i, :] for i in (0, 1)]
        ps_p = [bank[:, i:i + 2, :].rearrange("p b (j c) -> p (b j) c", j=2) for i in (2, 5)]
        ps_l = [bank[:, i, 0:GROUP * E].rearrange("p (j e) -> p j e", j=GROUP) for i in (4, 7)]
        with nc.Block() as block:
            @block.gpsimd
            def _(pool):
                core.ln_rsqrt(pool, S["var_ready"], S["rstd_ready"])

            @block.vector
            def _(dve):
                dve.sem_inc(S["yT_ready"], 2)
                chain = Chain(dve, S["dve_chain"])
                core.ln_stats(dve, chain, S["stat_done"], S["var_ready"], S["rstd_ready"])
                with dve.Fori(0, GROUPS // 2) as g2:
                    for par in range(2):
                        g = g2 * 2 + par
                        hold(dve, S["yT_ready"], g + 1, core.passed)
                        for j in range(GROUP):
                            ins = core.normalize(y[:, par, j, :], g * GROUP + j)
                        ins.then_inc(S["y_ready"], 1)
                        hold(dve, S["z_ready"], g + 1, core.passed)
                        hold(dve, S["y_ready"], g + 1, core.passed)
                        xg = core.x[:, bass.ds(g * GROUP, GROUP), :]
                        v.scalar_tensor_tensor(xg, ps_p[par][:, :, 0:D], 0.5, xg, ALU.mult, ALU.add).then_inc(S["base_added"], 1)
                T3 = [P, TILES, ET]
                select_top2(nc, chain, logits[:], both[:], left[:], eq[:], key[:], top, order[:], E)
                v.tensor_copy(top[:], top[:]).then_inc(S["left_ready"], 1)
                dve.wait_ge(S["exp_ready"], 1)
                chain.link(v.tensor_tensor(te[:], eq[:, :, 0:ET], both[:, :, 0:ET], ALU.mult))
                chain.link(v.tensor_reduce(top[:], te[:], AX_X, ALU.add))
                chain.link(v.tensor_scalar(zero[:], top[:], 0.0, None, ALU.is_equal))
                chain.link(v.tensor_tensor(top[:], top[:], zero[:], ALU.add))
                chain.link(v.reciprocal(top[:], top[:]))
                chain.link(v.tensor_tensor(te[:], te[:], top[:].unsqueeze(2).broadcast_to(T3), ALU.mult))

                def weigh(g, par):
                    v.tensor_tensor(zw[:, par].rearrange("p j (e r) -> p (j e) r", e=ET),
                                    z[:, bass.ds(g * GROUP, GROUP), :].rearrange("p j (e r) -> p (j e) r", e=ET),
                                    te[:, bass.ds(g * GROUP, GROUP), :].rearrange("p j e -> p (j e)").unsqueeze(2)
                                    .broadcast_to([P, GROUP * ET, RANK]), ALU.mult).then_inc(S["zw_ready"], 1)

                dve.sem_inc(S["zwT_ready"], 2)
                with dve.Fori(0, GROUPS // 2) as g2:
                    for par in range(2):
                        g = g2 * 2 + par
                        hold(dve, S["zwT_ready"], g + 1, core.passed)
                        weigh(g, par)
                        hold(dve, S["moe_done"], g + 1, core.passed)
                        xg = core.x[:, bass.ds(g * GROUP, GROUP), :]
                        v.tensor_tensor(xg, xg, ps_p[par][:, :, 0:D], ALU.add).then_inc(S["added"], 1)

            @block.tensor
            def _(pe):
                with pe.Fori(0, GROUPS // 2) as g2:
                    for par in range(2):
                        g = g2 * 2 + par
                        hold(pe, S["y_ready"], g + 1, core.passed)
                        for j in range(GROUP):
                            ins = t_.transpose(ps_y[par][:, j * P:(j + 1) * P], y[:, par, j, :], core.ident[:])
                        ins.then_inc(S["y_turned"], 1)
                        hold(pe, S["yT_ready"], g + 3, core.passed)
                        for j in range(GROUP):
                            lhsT = yT[:, par, j * P:(j + 1) * P]
                            t_.matmul(ps_p[par][:, j, :], lhsT, wcat[:, 0:2 * D], start=True, stop=False, skip_group_check=True)
                            t_.matmul(ps_p[par][:, j, 0:D], ones[:], bias[:], start=False, stop=True, skip_group_check=True)
                            ins = t_.matmul(ps_l[par][:, j, :], lhsT, wcat[:, 2 * D:2 * D + E], start=True, stop=True)
                        ins.then_inc(S["proj_done"], 1)
                with pe.Fori(0, GROUPS // 2) as g2:
                    for par in range(2):
                        g = g2 * 2 + par
                        hold(pe, S["zw_ready"], g + 1, core.passed)
                        for j in range(GROUP):
                            ins = t_.transpose(ps_y[par][:, j * P:(j + 1) * P], zw[:, par, j, :], core.ident[:])
                        ins.then_inc(S["zw_turned"], 1)
                        hold(pe, S["zwT_ready"], g + 3, core.passed)
                        for j in range(GROUP):
                            ins = t_.matmul(ps_p[par][:, j, 0:D], zwT[:, par, j * P:(j + 1) * P], lB[:], start=True, stop=True)
                        ins.then_inc(S["moe_done"], 1)

            @block.scalar
            def _(act):
                with act.Fori(0, GROUPS // 2) as g2:
                    for par in range(2):
                        g = g2 * 2 + par
                        hold(act, S["y_turned"], g + 1, core.passed)
                        s.copy(yT[:, par, :], ps_y[par]).then_inc(S["yT_ready"], 1)
                        hold(act, S["proj_done"], g + 1, core.passed)
                        s.copy(logits[:, bass.ds(g * GROUP, GROUP), :], ps_l[par])
                        s.copy(z[:, bass.ds(g * GROUP, GROUP), :], ps_p[par][:, :, D:2 * D]).then_inc(S["z_ready"], 1)
                act.wait_ge(S["left_ready"], 1)
                s.activation(flat(eq[:]), flat(left[:]), ACT.Exp).then_inc(S["exp_ready"], 1)
                with act.Fori(0, GROUPS // 2) as g2:
                    for par in range(2):
                        g = g2 * 2 + par
                        hold(act, S["zw_turned"], g + 1, core.passed)
                        s.copy(zwT[:, par, :], ps_y[par]).then_inc(S["zwT_ready"], 1)
        core.clear()


def attention(core, tag, a, consts):
    nc = core.nc
    NH, DK = 16, 8
    HG = 4
    SPLIT = 4
    SCALE = float(1.0 / np.sqrt(DK * 2.0) / 1.5)
    UNIT = 64.0
    T = TIME
    VW = DK + 1
    v, s, t_, g_ = nc.vector, nc.scalar, nc.tensor, nc.gpsimd
    with ExitStack() as ctx:
        def sb(name, shape, dt=F32):
            return ctx.enter_context(nc.sbuf_tensor(f"{tag}_{name}", shape, dt))

        def sem(name):
            return core.scoped_sem(ctx, f"{tag}_{name}")

        bank = ctx.enter_context(nc.psum_tensor(f"{tag}_ps", [P, 7, 512], F32))
        bank16 = ctx.enter_context(nc.psum_tensor(f"{tag}_ps16", [P, 1024], F16))
        wqkv = sb("wqkv", [P, 3 * D])
        wo = sb("wo", [P, D])
        bias = sb("bias", [1, 4 * D])
        ones = sb("ones", [1, P])
        ident16 = sb("ident16", [P, P], F16)
        tri = sb("tri", [P, P])
        qkT = sb("qkT", [P, 2 * HG, BATCHES * T], F16)
        V = sb("V", [P, TILES, NH, VW])
        O = sb("O", [P, TILES, D])
        names = ("loaded ones_ready stat_done var_ready rstd_ready dve_chain y_ready y_turned yT_ready proj_done "
                 "qk_ready ss_ready rn_ready qn_ready hi_ready lo_ready split_turned qkT_ready staged s_done e_done m_done "
                 "pv_done rec_ready rec_used o_read ost_ready o_turned oT_ready out_done added").split()
        S = {n: sem(n) for n in names}
        with ExitStack() as c2:
            rows = c2.enter_context(nc.sbuf_tensor(f"{tag}_rows", [P, 4, P], F32))
            with nc.Block() as block:
                @block.vector
                def _(dve):
                    v.memset(ones[:], 1.0).then_inc(S["ones_ready"], 1)
                    v.memset(V[:], 1.0).then_inc(S["ones_ready"], 1)
                    v.tensor_copy(ident16[:], core.ident[:]).then_inc(S["ones_ready"], 1)

                @block.sync
                def _(sp):
                    sp.wait_ge(S["ones_ready"], 3)
                    for n, x in enumerate("qkvo"):
                        sp.dma_start(rows[:, n, :], a[f"L1_attn_W{x}"]).then_inc(S["loaded"], 16)
                        sp.dma_start(bias[:, n * D:(n + 1) * D], a[f"L1_attn_b{x}"].unsqueeze(0)).then_inc(S["loaded"], 16)
                    sp.dma_start(tri[:], consts["tri"]).then_inc(S["loaded"], 16)
            turn_weights(nc, core, ctx, tag, [(rows[:, n, :], wqkv[:, n * D:(n + 1) * D] if n < 3 else wo[:], P)
                                         for n in range(4)], S["loaded"], 144, bank)

        with ExitStack() as c2:
            def sb2(name, shape, dt=F32):
                return c2.enter_context(nc.sbuf_tensor(f"{tag}_{name}", shape, dt))

            y = sb2("y", [P, GROUP, D])
            yT = sb2("yT", [P, GROUP * P])
            qk = sb2("qk", [P, GROUP, 2 * D])
            sq = sb2("sq", [P, GROUP, 2 * D])
            ss = sb2("ss", [P, GROUP * 2 * NH])
            rn = sb2("rn", [P, GROUP * 2 * NH])
            split = sb2("split", [P, GROUP, 2, NH, SPLIT, DK], F16)
            ps_y = bank[:, 0, :]
            ps_qkv = bank[:, 1:5, 0:3 * D]
            with nc.Block() as block:
                @block.gpsimd
                def _(pool):
                    core.ln_rsqrt(pool, S["var_ready"], S["rstd_ready"])
                    with pool.Fori(0, GROUPS) as g:
                        hold(pool, S["ss_ready"], g + 1, core.passed)
                        g_.tensor_tensor(rn[:], ss[:], core.minus_half[:, 0:GROUP * 2 * NH], ALU.pow).then_inc(S["rn_ready"], 1)

                @block.vector
                def _(dve):
                    dve.sem_inc(S["yT_ready"], 1)
                    chain = Chain(dve, S["dve_chain"])
                    core.ln_stats(dve, chain, S["stat_done"], S["var_ready"], S["rstd_ready"])
                    before = chain.n
                    with dve.Fori(0, GROUPS) as g:
                        chain.enter(before, g, 3)
                        hold(dve, S["yT_ready"], g + 1, core.passed)
                        for j in range(GROUP):
                            ins = core.normalize(y[:, j, :], g * GROUP + j)
                        ins.then_inc(S["y_ready"], 1)
                        hold(dve, S["qk_ready"], g + 1, core.passed)
                        chain.link(v.tensor_tensor(sq[:], qk[:], qk[:], ALU.mult))
                        chain.link(v.tensor_reduce(ss[:], sq[:].rearrange("p j (h d) -> p (j h) d", d=DK), AX_X, ALU.add))
                        v.tensor_scalar(ss[:], ss[:], 1e-16, None, ALU.max).then_inc(S["ss_ready"], 1)
                        hold(dve, S["rn_ready"], g + 1, core.passed)
                        qkh = qk[:].rearrange("p j (h d) -> p (j h) d", d=DK)
                        v.scalar_tensor_tensor(qkh, qkh, UNIT, rn[:].unsqueeze(2).broadcast_to([P, GROUP * 2 * NH, DK]),
                                               ALU.mult, ALU.mult).then_inc(S["qn_ready"], 1)
                        hold(dve, S["hi_ready"], 4 * g + 4, core.passed)
                        for n in range(2):
                            qn = qk[:].rearrange("p j (n h d) -> p j n h d", n=2, d=DK)[:, :, n]
                            for m in range(2):
                                hi, lo = ((m, 2 + m) if n == 0 else (2 * m, 2 * m + 1))
                                ins = v.tensor_tensor(split[:, :, n, :, lo, :], qn, split[:, :, n, :, hi, :], ALU.subtract)
                        ins.then_inc(S["lo_ready"], 1)
                        hold(dve, S["lo_ready"], g + 1, core.passed)
                        chain.link(v.tensor_copy(ss[:, 0:1], ss[:, 0:1]))

                @block.scalar
                def _(act):
                    with act.Fori(0, GROUPS) as g:
                        hold(act, S["y_turned"], g + 1, core.passed)
                        s.copy(yT[:], ps_y).then_inc(S["yT_ready"], 1)
                        hold(act, S["proj_done"], g + 1, core.passed)
                        s.copy(V[:, bass.ds(g * GROUP, GROUP), :, 0:DK],
                               ps_qkv[:, :, 2 * D:3 * D].rearrange("p j (h d) -> p j h d", d=DK))
                        s.copy(qk[:], ps_qkv[:, :, 0:2 * D]).then_inc(S["qk_ready"], 1)
                        hold(act, S["qn_ready"], g + 1, core.passed)
                        for n in range(2):
                            qn = qk[:].rearrange("p j (n h d) -> p j n h d", n=2, d=DK)[:, :, n]
                            for m in range(2):
                                s.copy(split[:, :, n, :, m if n == 0 else 2 * m, :], qn).then_inc(S["hi_ready"], 1)
                        for j in range(GROUP):
                            hold(act, S["split_turned"], g * GROUP + j + 1, core.passed)
                            s.copy(qkT[:, :, bass.ds((g * GROUP + j) * P, P)],
                                   bank16[:].rearrange("p (n c) -> p n c", n=2 * HG)).then_inc(S["qkT_ready"], 1)

                @block.tensor
                def _(pe):
                    pe.sem_inc(S["qkT_ready"], 1)
                    with pe.Fori(0, GROUPS) as g:
                        hold(pe, S["y_ready"], g + 1, core.passed)
                        for j in range(GROUP):
                            ins = t_.transpose(ps_y[:, j * P:(j + 1) * P], y[:, j, :], core.ident[:])
                        ins.then_inc(S["y_turned"], 1)
                        hold(pe, S["yT_ready"], g + 2, core.passed)
                        for j in range(GROUP):
                            t_.matmul(ps_qkv[:, j, :], yT[:, j * P:(j + 1) * P], wqkv[:], start=True, stop=False)
                            ins = t_.matmul(ps_qkv[:, j, :], ones[:], bias[:, 0:3 * D], start=False, stop=True)
                        ins.then_inc(S["proj_done"], 1)
                        hold(pe, S["lo_ready"], g + 1, core.passed)
                        for j in range(GROUP):
                            hold(pe, S["qkT_ready"], g * GROUP + j + 1, core.passed)
                            for n in range(2 * HG):
                                ins = t_.transpose(bank16[:, n * P:(n + 1) * P],
                                                   split[:, j, n // HG, n % HG * HG:n % HG * HG + HG].rearrange("p h x d -> p (h x d)"),
                                                   ident16[:])
                            ins.then_inc(S["split_turned"], 1)

        with ExitStack() as c2:
            def sb2(name, shape, dt=F32):
                return c2.enter_context(nc.sbuf_tensor(f"{tag}_{name}", shape, dt))

            SLOTS = 3
            qs = sb2("qs", [P, T], F16)
            ks = sb2("ks", [P, T], F16)
            vs = sb2("vs", [P, BATCH_TILES, HG, VW])
            probs = sb2("probs", [P, SLOTS, 1024])
            rec = sb2("rec", [P, BATCH_TILES * HG])
            oraw = sb2("oraw", [P, BATCH_TILES * HG, VW])
            ps_s = [bank[:, 2 * i:2 * i + 2, :].rearrange("p b c -> p (b c)") for i in range(SLOTS)]
            ps_o = bank[:, 6, 0:BATCH_TILES * HG * VW]
            works = []
            for h in (0, 2):
                full = [[(x, 0, 0)] for x in (h, h + 1)]
                pairs = [[(x, k, 0), (x, BATCH_TILES - k, (BATCH_TILES - k) * P)] for x in (h, h + 1) for k in (1, 2, 3)]
                works += [full[0]] + pairs[0:3] + [[(h, 4, 0), (h + 1, 4, 512)]] + [full[1]] + pairs[3:6]
            NW = len(works)
            STEPS = BATCHES * HG

            with nc.Block() as block:
                @block.vector
                def _(dve):
                    with dve.Fori(0, BATCHES) as b:
                        with dve.Fori(0, HG) as g:
                            it = b * HG + g
                            v.tensor_copy(qs[:], qkT[:, bass.ds(g, 1), bass.ds(b * T, T)].rearrange("p a c -> p (a c)")).then_inc(S["staged"], 1)
                            v.tensor_copy(ks[:], qkT[:, bass.ds(g + HG, 1), bass.ds(b * T, T)].rearrange("p a c -> p (a c)")).then_inc(S["staged"], 1)
                            v.tensor_copy(vs[:], V[:, bass.ds(b * BATCH_TILES, BATCH_TILES), bass.ds(g * HG, HG), :]).then_inc(S["staged"], 1)
                            for n, work in enumerate(works):
                                hold(dve, S["e_done"], it * NW + n + 1, core.passed)
                                if len(work) == 1:
                                    p = probs[:, n % SLOTS, 0:P]
                                    v.tensor_tensor(p, p, tri[:], ALU.mult).then_inc(S["m_done"], 1)
                                else:
                                    at = work[1][2]
                                    for q in (0, at):
                                        p = probs[:, n % SLOTS, q:q + P]
                                        ins = v.tensor_tensor(p, p, tri[:], ALU.mult)
                                    ins.then_inc(S["m_done"], 1)
                            hold(dve, S["pv_done"], SLOTS + (it + 1) * NW, core.passed)
                            v.tensor_copy(oraw[:].rearrange("p q d -> p (q d)"), ps_o).then_inc(S["o_read"], 1)
                            hold(dve, S["o_read"], it + 1, core.passed)
                            v.reciprocal(rec[:].unsqueeze(2), oraw[:, :, DK:VW]).then_inc(S["rec_ready"], 1)
                            hold(dve, S["rec_ready"], it + 1, core.passed)
                            v.tensor_tensor(O[:, bass.ds(b * BATCH_TILES, BATCH_TILES), bass.ds(g * HG * DK, HG * DK)]
                                            .rearrange("p t (h d) -> p t h d", d=DK),
                                            oraw[:, :, 0:DK].rearrange("p (t h) d -> p t h d", h=HG),
                                            rec[:].rearrange("p (t h) -> p t h", h=HG).unsqueeze(3)
                                            .broadcast_to([P, BATCH_TILES, HG, DK]), ALU.mult).then_inc(S["rec_used"], 1)

                @block.scalar
                def _(act):
                    s.activation(core.warm[:], core.minus_half[:, 0:1], ACT.Exp).then_inc(core.passed, 1)
                    act.sem_inc(S["pv_done"], SLOTS)
                    with act.Fori(0, STEPS) as it:
                        for n in range(NW):
                            hold(act, S["pv_done"], it * NW + n + 1, core.passed)
                            hold(act, S["s_done"], it * NW + n + 1, core.passed)
                            s.activation(probs[:, n % SLOTS, :], ps_s[n % SLOTS], ACT.Exp,
                                         scale=SCALE / (UNIT * UNIT)).then_inc(S["e_done"], 1)

                @block.tensor
                def _(pe):
                    def score(it, n):
                        if n >= SLOTS:
                            hold(pe, S["e_done"], it * NW + n - SLOTS + 1, core.passed)
                        for h, kb, at in works[n]:
                            rows_ = slice(h * 32, h * 32 + 32)
                            width = T - kb * P
                            q0 = kb * P
                            while width:
                                w = min(width, 512 - at % 512)
                                ins = t_.matmul(ps_s[n % SLOTS][:, at:at + w], ks[rows_, kb * P:(kb + 1) * P],
                                                qs[rows_, q0:q0 + w], start=True, stop=True, skip_group_check=True)
                                at, q0, width = at + w, q0 + w, width - w
                        ins.then_inc(S["s_done"], 1)

                    def gather(it, n):
                        hold(pe, S["m_done"], it * NW + n + 1, core.passed)
                        for h, kb, at in works[n]:
                            for qt in range(kb, BATCH_TILES):
                                q = qt * HG + h
                                ins = t_.matmul(ps_o[:, q * VW:(q + 1) * VW],
                                                probs[:, n % SLOTS, at + (qt - kb) * P:at + (qt - kb + 1) * P],
                                                vs[:, kb, h, :], start=(n == 0 and qt == kb), stop=(n == NW - 1),
                                                skip_group_check=True)
                        ins.then_inc(S["pv_done"], 1)
                        return ins

                    with pe.Fori(0, STEPS) as it:
                        hold(pe, S["staged"], it * 3 + 3, core.passed)
                        score(it, 0)
                        score(it, 1)
                        for n in range(NW):
                            if n + 2 < NW:
                                score(it, n + 2)
                            gather(it, n)

        ostage = sb("ostage", [P, 2, GROUP, D])
        oT = sb("oT", [P, 2, GROUP * P])
        ps_t = [bank[:, i, :] for i in (0, 1)]
        ps_f = [bank[:, i, :].rearrange("p (j d) -> p j d", j=GROUP) for i in (2, 3)]
        with nc.Block() as block:
            @block.vector
            def _(dve):
                dve.sem_inc(S["oT_ready"], 2)
                with dve.Fori(0, GROUPS // 2) as g2:
                    for par in range(2):
                        g = g2 * 2 + par
                        hold(dve, S["oT_ready"], g + 1, core.passed)
                        v.tensor_copy(ostage[:, par], O[:, bass.ds(g * GROUP, GROUP), :]).then_inc(S["ost_ready"], 1)
                        hold(dve, S["out_done"], g + 1, core.passed)
                        xg = core.x[:, bass.ds(g * GROUP, GROUP), :]
                        v.scalar_tensor_tensor(xg, ps_f[par], 0.5, xg, ALU.mult, ALU.add).then_inc(S["added"], 1)

            @block.tensor
            def _(pe):
                with pe.Fori(0, GROUPS // 2) as g2:
                    for par in range(2):
                        g = g2 * 2 + par
                        hold(pe, S["ost_ready"], g + 1, core.passed)
                        for j in range(GROUP):
                            ins = t_.transpose(ps_t[par][:, j * P:(j + 1) * P], ostage[:, par, j, :], core.ident[:])
                        ins.then_inc(S["o_turned"], 1)
                        hold(pe, S["oT_ready"], g + 3, core.passed)
                        for j in range(GROUP):
                            t_.matmul(ps_f[par][:, j, :], oT[:, par, j * P:(j + 1) * P], wo[:], start=True, stop=False)
                            ins = t_.matmul(ps_f[par][:, j, :], ones[:], bias[:, 3 * D:4 * D], start=False, stop=True)
                        ins.then_inc(S["out_done"], 1)

            @block.scalar
            def _(act):
                with act.Fori(0, GROUPS // 2) as g2:
                    for par in range(2):
                        g = g2 * 2 + par
                        hold(act, S["o_turned"], g + 1, core.passed)
                        s.copy(oT[:, par, :], ps_t[par]).then_inc(S["oT_ready"], 1)
        core.clear()


def transformer(nc, a, consts, out, stages):
    with ExitStack() as ctx:
        core = Core(nc, ctx, a["L0_attn_x"], consts)
        ffn = (a["L0_ffn_Wg"], a["L0_ffn_bg"], a["L0_ffn_W1"], a["L0_ffn_b1"], a["L0_ffn_W2"], a["L0_ffn_b2"],
               consts["order"])
        lora = (a["L1_ffn_base_w"], a["L1_ffn_base_b"], a["L1_ffn_gate_w"], a["L1_ffn_lora_A"], a["L1_ffn_lora_B"],
                consts["order"])
        steps = [lambda: moe_ffn(core, "ffn1", *ffn),
                 lambda: ssm(core, "ssm", a, consts),
                 lambda: moe_ffn(core, "ffn2", *ffn),
                 lambda: lora_ffn(core, "lora1", *lora),
                 lambda: attention(core, "attn", a, consts),
                 lambda: lora_ffn(core, "lora2", *lora)]
        for n in stages:
            steps[n]()
        stored = core.sem("stored")
        with nc.Block() as block:
            @block.sync
            def _(sp):
                sp.dma_start(out.rearrange("b (t p) d -> p (b t) d", p=P), core.x[:]).then_inc(stored, 16)
                sp.wait_ge(stored, 16)


_INS = ['L0_attn_x', 'L0_attn_W_in', 'L0_attn_A_log', 'L0_attn_dt_bias', 'L0_attn_B_norm_bias', 'L0_attn_C_norm_bias',
        'L0_attn_W_out', 'L0_ffn_Wg', 'L0_ffn_bg', 'L0_ffn_W1', 'L0_ffn_b1', 'L0_ffn_W2', 'L0_ffn_b2', 'L1_attn_Wq',
        'L1_attn_bq', 'L1_attn_Wk', 'L1_attn_bk', 'L1_attn_Wv', 'L1_attn_bv', 'L1_attn_Wo', 'L1_attn_bo',
        'L1_ffn_base_w', 'L1_ffn_base_b', 'L1_ffn_gate_w', 'L1_ffn_lora_A', 'L1_ffn_lora_B']
STAGES = (0, 1, 2, 3, 4, 5)


def constants():
    c = {"ident": np.eye(P, dtype=np.float32),
         "order": np.tile(np.arange(16, 0, -1, dtype=np.float32), (P, 1))}
    c["tri"] = np.triu(np.ones((P, P), np.float32))
    c.update(ssm_constants())
    return c


def kernel(**inputs):
    import numpy as _np
    import concourse.bacc as _bacc
    from concourse.bass_utils import run_bass_kernel_spmd as _run

    nc = _bacc.Bacc("TRN2", target_bir_lowering=False, num_devices=1)
    arrays, args, consts = {}, {}, {}
    for name in _INS:
        a = _np.ascontiguousarray(inputs[name])
        arrays[f"in_{name}"] = a
        args[name] = nc.dram_tensor(f"in_{name}", a.shape, mybir.dt.from_np(a.dtype), kind="ExternalInput").ap()
    for name, a in constants().items():
        arrays[f"const_{name}"] = a
        consts[name] = nc.dram_tensor(f"const_{name}", a.shape, mybir.dt.from_np(a.dtype), kind="ExternalInput").ap()
    out = nc.dram_tensor("out_x", (BATCHES, TIME, D), F32, kind="ExternalOutput").ap()
    transformer(nc, args, consts, out, STAGES)
    r = _run(nc, [arrays], core_ids=[0])
    return r.results[0]["out_x"]
```

```python
from contextlib import ExitStack

import numpy as np

import concourse.bass as bass
from concourse import mybir

ALU = mybir.AluOpType
ACT = mybir.ActivationFunctionType
F32 = mybir.dt.float32
F16 = mybir.dt.float16
F32R = mybir.dt.float32r
AX_X = mybir.AxisListType.X

P = 128
D = 128
BATCHES, TIME = 4, 1024
TILES = BATCHES * TIME // P
BATCH_TILES = TIME // P
GROUP = 4
GROUPS = TILES // GROUP
LN_EPS = 1e-5


class Chain:

    def __init__(self, eng, sem):
        self.eng, self.sem, self.base, self.n = eng, sem, 0, 0

    def link(self, ins):
        ins.then_inc(self.sem, 1)
        self.n += 1
        self.eng.wait_ge(self.sem, self.base + self.n)

    def enter(self, before, i, per):
        self.base, self.n, self.per = i * per + before, 0, per

    def leave(self, before, count):
        assert self.n == self.per, (self.n, self.per)
        self.base, self.n = 0, before + count * self.per


class Core:

    def __init__(self, nc, ctx, x_in, consts):
        self.nc, self.ctx, self.used = nc, ctx, []
        self.x = ctx.enter_context(nc.sbuf_tensor("x_res", [P, TILES, D], F32))
        self.ident = ctx.enter_context(nc.sbuf_tensor("ident", [P, P], F32))
        self.stats = ctx.enter_context(nc.sbuf_tensor("ln_stats", [P, TILES, 6], F32))
        self.mean = ctx.enter_context(nc.sbuf_tensor("ln_mean", [P, TILES], F32))
        self.rstd = ctx.enter_context(nc.sbuf_tensor("ln_rstd", [P, TILES], F32))
        self.tmp1 = ctx.enter_context(nc.sbuf_tensor("ln_tmp1", [P, TILES], F32))
        self.tmp2 = ctx.enter_context(nc.sbuf_tensor("ln_tmp2", [P, TILES], F32))
        self.minus_half = ctx.enter_context(nc.sbuf_tensor("minus_half", [P, 256], F32))
        self.warm = ctx.enter_context(nc.sbuf_tensor("warm", [P, 1], F32))
        self.x_loaded = self.sem("x_loaded")
        self.half_ready = self.sem("half_ready")
        self.passed = self.sem("waits_passed")
        with nc.Block() as block:
            @block.gpsimd
            def _(pool):
                nc.gpsimd.memset(self.minus_half[:], -0.5).then_inc(self.half_ready, 1)

            @block.sync
            def _(sp):
                sp.wait_ge(self.half_ready, 1)
                sp.dma_start(self.x[:], x_in.rearrange("b (t p) d -> p (b t) d", p=P)).then_inc(self.x_loaded, 16)
                sp.dma_start(self.ident[:], consts["ident"]).then_inc(self.x_loaded, 16)
                sp.wait_ge(self.x_loaded, 32)

    def sem(self, name):
        return self.ctx.enter_context(self.nc.semaphore(name))

    def scoped_sem(self, ctx, name):
        handle = ctx.enter_context(self.nc.semaphore(name))
        self.used.append(handle)
        return handle

    def clear(self):
        with self.nc.Block() as block:
            @block.gpsimd
            def _(pool):
                for handle in self.used:
                    pool.sem_clear(handle)
        self.used = []

    def ln_stats(self, dve, chain, sem, var_ready, rstd_ready, tiles=TILES, first=0):
        v = self.nc.vector
        with dve.Fori(0, tiles // 8) as t8:
            for i in range(8):
                t = bass.ds(t8 * 8 + (first + i), 1)
                v.bn_stats(flat(self.stats[:, t, :]), flat(self.x[:, t, :])).then_inc(sem, 1)
        dve.wait_ge(sem, tiles)
        ts = slice(first, first + tiles)
        even, odd = self.stats[:, ts, 1], self.stats[:, ts, 4]
        half, var = self.tmp1[:, ts], self.tmp2[:, ts]
        v.tensor_tensor(half, even, odd, ALU.subtract).then_inc(chain.sem, 1)
        v.tensor_tensor(self.mean[:, ts], even, odd, ALU.add).then_inc(chain.sem, 1)
        chain.n += 2
        chain.link(v.tensor_tensor(var, self.stats[:, ts, 2], self.stats[:, ts, 5], ALU.add))
        chain.link(v.tensor_tensor(half, half, half, ALU.mult))
        v.tensor_scalar(self.mean[:, ts], self.mean[:, ts], 0.5, None, ALU.mult).then_inc(chain.sem, 1)
        chain.n += 1
        chain.link(v.tensor_scalar(var, var, 1.0 / D, LN_EPS, ALU.mult, ALU.add))
        v.scalar_tensor_tensor(var, half, 0.25, var, ALU.mult, ALU.add).then_inc(var_ready, 1)
        dve.wait_ge(rstd_ready, 1)

    def ln_rsqrt(self, pool, var_ready, rstd_ready):
        pool.wait_ge(var_ready, 1)
        self.nc.gpsimd.tensor_tensor(self.rstd[:], self.tmp2[:], self.minus_half[:, 0:TILES], ALU.pow).then_inc(rstd_ready, 1)

    def normalize(self, out, t):
        return self.nc.vector.tensor_scalar(out, self.x[:, bass.ds(t, 1), :].rearrange("p a b -> p (a b)"),
                                            self.mean[:, bass.ds(t, 1)], self.rstd[:, bass.ds(t, 1)],
                                            ALU.subtract, ALU.mult)


def flat(ap):
    return ap.rearrange("p a b -> p (a b)")


def select_top2(nc, chain, logits, both, left, eq, key, top, order, E, left_ready):
    v = nc.vector
    shape = [P, TILES, E]
    order_b = order.unsqueeze(1).broadcast_to(shape)

    def pick(values):
        chain.link(v.tensor_reduce(top[:], values, AX_X, ALU.max))
        chain.link(v.tensor_tensor(eq, values, top[:].unsqueeze(2).broadcast_to(shape), ALU.is_equal))
        chain.link(v.tensor_tensor(key, eq, order_b, ALU.mult))

    pick(logits)
    v.tensor_tensor(left, logits, top[:].unsqueeze(2).broadcast_to(shape), ALU.subtract).then_inc(left_ready, 1)
    chain.eng.wait_ge(left_ready, 1)
    chain.link(v.tensor_reduce(top[:], key, AX_X, ALU.max))
    chain.link(v.tensor_tensor(both, key, top[:].unsqueeze(2).broadcast_to(shape), ALU.is_equal))
    chain.link(v.scalar_tensor_tensor(flat(logits), flat(both), -1e30, flat(logits), ALU.mult, ALU.add))
    pick(logits)
    chain.link(v.tensor_reduce(top[:], key, AX_X, ALU.max))
    chain.link(v.tensor_tensor(key, key, top[:].unsqueeze(2).broadcast_to(shape), ALU.is_equal))
    chain.link(v.tensor_tensor(both, both, key, ALU.add))


def moe_ffn(core, tag, Wg, bg, W1, b1, W2, b2, order_in):
    nc = core.nc
    v, s, t, g_ = nc.vector, nc.scalar, nc.tensor, nc.gpsimd
    E, _, H = W1.shape
    HC = H // P
    SPLITS = 5
    with ExitStack() as ctx:
        def sb(name, shape, dt=F32):
            return ctx.enter_context(nc.sbuf_tensor(f"{tag}_{name}", shape, dt))

        def ps(name, shape, dt=F32):
            return ctx.enter_context(nc.psum_tensor(f"{tag}_{name}", shape, dt))

        def sem(name):
            return core.scoped_sem(ctx, f"{tag}_{name}")

        yTh = sb("yTh", [P, TILES * P], F32R)
        yTl = sb("yTl", [P, TILES * P], F32R)
        accT = sb("accT", [P, TILES * P])
        gT = sb("gT", [2 * E, TILES * P], F32R)
        b1T = sb("b1T", [P, E * HC])
        b2T = sb("b2T", [P, E])
        w_raw = sb("w_raw", [P, 2, 2, H])
        w_high = sb("w_high", [P, 2, 2, H], F32R)
        w_low = sb("w_low", [P, 2, 2, H], F32R)
        select = sb("select", [2 * E, 2, P], F32R)
        w_loaded = [sem("w_loaded0"), sem("w_loaded1")]
        w_split = sem("w_split")

        def load_weights(sp, e):
            sp.dma_start(w_raw[:, e % 2, 0, :], W1[e]).then_inc(w_loaded[e % 2], 16)
            sp.dma_start(w_raw[:, e % 2, 1, :].rearrange("p (c d) -> p c d", c=HC),
                         W2[e].rearrange("(c h) d -> h c d", c=HC)).then_inc(w_loaded[e % 2], 16)

        def split_weights(pool, e):
            slot = e % 2
            pool.wait_ge(w_loaded[slot], 32 * (e // 2) + 32)
            for w in range(2):
                g_.tensor_copy(w_high[:, slot, w, :], w_raw[:, slot, w, :]).then_inc(w_split, 1)
            g_.tensor_tensor(select[:, slot, :], core.ident[0:2 * E, e:e + 1].broadcast_to([2 * E, P]),
                             core.ident[0:2 * E, E + e:E + e + 1].broadcast_to([2 * E, P]), ALU.add).then_inc(w_split, 1)
            pool.wait_ge(w_split, SPLITS * e + 3)
            for w in range(2):
                g_.tensor_tensor(w_low[:, slot, w, :], w_raw[:, slot, w, :], w_high[:, slot, w, :].bitcast(F32),
                                 ALU.subtract).then_inc(w_split, 1)

        with ExitStack() as rctx:
            def rsb(name, shape, dt=F32):
                return rctx.enter_context(nc.sbuf_tensor(f"{tag}_{name}", shape, dt))

            def rps(name, shape, dt=F32):
                return rctx.enter_context(nc.psum_tensor(f"{tag}_{name}", shape, dt))

            y = rsb("y", [P, 2, GROUP, D])
            yT = rsb("yT", [P, 2, GROUP * P])
            wg = rsb("wg", [P, E])
            bg_all = rsb("bg", [P, E])
            b1_rows = rsb("b1_rows", [E * HC, P])
            b2_rows = rsb("b2_rows", [E, D])
            order = rsb("order", [P, E])
            gates = rsb("gates", [P, TILES, E])
            g_high = rsb("g_high", [P, TILES, E], F32R)
            g_low = rsb("g_low", [P, TILES, E])
            gstage = rsb("gstage", [P, 2, GROUP, 2, E])
            logits = rsb("logits", [P, TILES, E])
            left = rsb("left", [P, TILES, E])
            eq = rsb("eq", [P, TILES, E])
            key = rsb("key", [P, TILES, E])
            both = rsb("both", [P, TILES, E])
            top = rsb("top", [P, TILES])
            ps_y = rps("ps_y", [P, 2, GROUP * P])
            ps_l = rps("ps_l", [P, 2, 512])
            ps_g = rps("ps_g", [P, 2, 512])
            small_loaded = sem("small_loaded")
            stat_done = sem("stat_done")
            dve_chain = sem("dve_chain")
            var_ready = sem("var_ready")
            rstd_ready = sem("rstd_ready")
            y_ready = sem("y_ready")
            y_turned = sem("y_turned")
            yT_ready = sem("yT_ready")
            yTh_ready = sem("yTh_ready")
            yTl_ready = sem("yTl_ready")
            lg_done = sem("lg_done")
            logits_ready = sem("logits_ready")
            left_ready = sem("left_ready")
            exp_ready = sem("exp_ready")
            b_turned = sem("b_turned")
            bT_ready = sem("bT_ready")
            acc_cleared = sem("acc_cleared")
            gstage_ready = sem("gstage_ready")
            g_turned = sem("g_turned")
            gT_ready = sem("gT_ready")

            with nc.Block() as block:
                @block.gpsimd
                def _(pool):
                    core.ln_rsqrt(pool, var_ready, rstd_ready)
                    g_.memset(accT[:], 0.0).then_inc(acc_cleared, 1)
                    for e in range(2):
                        split_weights(pool, e)
                    pool.wait_ge(acc_cleared, 1)

                @block.sync
                def _(sp):
                    sp.dma_start(wg[:], Wg).then_inc(small_loaded, 16)
                    sp.dma_start(bg_all[:], bg.unsqueeze(0).broadcast_to([P, E])).then_inc(small_loaded, 16)
                    sp.dma_start(b1_rows[:], b1.rearrange("e (c h) -> (e c) h", c=HC)).then_inc(small_loaded, 16)
                    sp.dma_start(b2_rows[:], b2).then_inc(small_loaded, 16)
                    sp.dma_start(order[:], order_in[:, 0:E]).then_inc(small_loaded, 16)
                    for e in range(2):
                        load_weights(sp, e)

                @block.vector
                def _(dve):
                    chain = Chain(dve, dve_chain)
                    core.ln_stats(dve, chain, stat_done, var_ready, rstd_ready)

                    def normalize(g, par):
                        dve.wait_ge(yT_ready, g + 1)
                        dve.sem_inc(core.passed, 1)
                        for j in range(GROUP):
                            ins = core.normalize(y[:, par, j, :], g * GROUP + j)
                        ins.then_inc(y_ready, 1)

                    def after(g, par):
                        dve.wait_ge(yTh_ready, g + 3)
                        dve.sem_inc(core.passed, 1)
                        tokens = bass.ds(g * GROUP * P, GROUP * P)
                        v.tensor_tensor(yTl[:, tokens], yT[:, par, :], yTh[:, tokens].bitcast(F32),
                                        ALU.subtract).then_inc(yTl_ready, 1)
                        dve.wait_ge(lg_done, g + 3)
                        dve.sem_inc(core.passed, 1)
                        v.tensor_tensor(logits[:, bass.ds(g * GROUP, GROUP), :],
                                        ps_l[:, par, 0:GROUP * E].rearrange("p (t e) -> p t e", t=GROUP),
                                        bg_all[:].unsqueeze(1).broadcast_to([P, GROUP, E]), ALU.add).then_inc(logits_ready, 1)

                    dve.sem_inc(yT_ready, 2)
                    dve.wait_ge(small_loaded, 80)
                    for par in range(2):
                        normalize(par, par)
                    with dve.Fori(0, GROUPS // 2 - 1) as g2:
                        for par in range(2):
                            normalize(g2 * 2 + par + 2, par)
                            after(g2 * 2 + par, par)
                    for par in range(2):
                        after(GROUPS - 2 + par, par)
                    dve.wait_ge(logits_ready, GROUPS + 2)
                    select_top2(nc, chain, logits[:], both[:], left[:], eq[:], key[:], top, order[:], E, left_ready)
                    dve.wait_ge(exp_ready, 1)
                    chain.link(v.tensor_tensor(gates[:], left[:], both[:], ALU.mult))
                    chain.link(v.tensor_reduce(top[:], gates[:], AX_X, ALU.add))
                    chain.link(v.tensor_scalar(top[:], top[:], 1e-12, 2.0, ALU.max, ALU.mult))
                    chain.link(v.reciprocal(top[:], top[:]))
                    chain.link(v.tensor_tensor(gates[:], gates[:], top[:].unsqueeze(2).broadcast_to([P, TILES, E]), ALU.mult))
                    chain.link(v.tensor_copy(g_high[:], gates[:]))
                    chain.link(v.tensor_tensor(g_low[:], gates[:], g_high[:].bitcast(F32), ALU.subtract))
                    dve.sem_inc(gT_ready, 2)
                    with dve.Fori(0, GROUPS // 2) as g2:
                        for par in range(2):
                            g = g2 * 2 + par
                            dve.wait_ge(g_turned, g + 1)
                            dve.sem_inc(core.passed, 1)
                            tiles = bass.ds(g * GROUP, GROUP)
                            v.tensor_copy(gstage[:, par, :, 0, :], g_high[:, tiles, :].bitcast(F32)).then_inc(gstage_ready, 1)
                            v.tensor_copy(gstage[:, par, :, 1, :], g_low[:, tiles, :]).then_inc(gstage_ready, 1)

                @block.tensor
                def _(pe):
                    def turn(g, par):
                        pe.wait_ge(y_ready, g + 1)
                        pe.sem_inc(core.passed, 1)
                        pe.wait_ge(yTh_ready, g + 1)
                        pe.sem_inc(core.passed, 1)
                        for j in range(GROUP):
                            ins = t.transpose(ps_y[:, par, j * P:(j + 1) * P], y[:, par, j, :], core.ident[:])
                        ins.then_inc(y_turned, 1)

                    def score(g, par):
                        pe.wait_ge(yT_ready, g + 3)
                        pe.sem_inc(core.passed, 1)
                        pe.wait_ge(logits_ready, g + 1)
                        pe.sem_inc(core.passed, 1)
                        for j in range(GROUP):
                            ins = t.matmul(ps_l[:, par, j * E:(j + 1) * E], yT[:, par, j * P:(j + 1) * P], wg[:],
                                           start=True, stop=True)
                        ins.then_inc(lg_done, 1)

                    pe.wait_ge(small_loaded, 80)
                    t.transpose(ps_g[:, 0, 0:E * HC], b1_rows[:], core.ident[0:E * HC, 0:E * HC]).then_inc(b_turned, 1)
                    t.transpose(ps_g[:, 1, 0:E], b2_rows[:], core.ident[0:E, 0:E]).then_inc(b_turned, 1)
                    pe.wait_ge(bT_ready, 2)
                    turn(0, 0)
                    with pe.Fori(0, GROUPS // 2 - 1) as g2:
                        for par in range(2):
                            turn(g2 * 2 + par + 1, 1 - par)
                            score(g2 * 2 + par, par)
                    turn(GROUPS - 1, 1)
                    score(GROUPS - 2, 0)
                    score(GROUPS - 1, 1)
                    pe.sem_inc(g_turned, 2)
                    with pe.Fori(0, GROUPS // 2) as g2:
                        for par in range(2):
                            g = g2 * 2 + par
                            pe.wait_ge(gstage_ready, 2 * g + 2)
                            pe.sem_inc(core.passed, 1)
                            pe.wait_ge(gT_ready, g + 1)
                            pe.sem_inc(core.passed, 1)
                            for j in range(GROUP):
                                ins = t.transpose(ps_g[0:2 * E, par, j * P:(j + 1) * P], gstage[:, par, j]
                                                  .rearrange("p n e -> p (n e)"), core.ident[:])
                            ins.then_inc(g_turned, 1)

                @block.scalar
                def _(act):
                    act.wait_ge(b_turned, 2)
                    s.copy(b1T[:], ps_g[:, 0, 0:E * HC]).then_inc(bT_ready, 1)
                    s.copy(b2T[:], ps_g[:, 1, 0:E]).then_inc(bT_ready, 1)
                    act.sem_inc(yTh_ready, 2)
                    act.sem_inc(logits_ready, 2)
                    act.sem_inc(yTl_ready, 2)
                    act.sem_inc(lg_done, 2)
                    with act.Fori(0, GROUPS // 2) as g2:
                        for par in range(2):
                            g = g2 * 2 + par
                            act.wait_ge(y_turned, g + 1)
                            act.sem_inc(core.passed, 1)
                            act.wait_ge(yTl_ready, g + 1)
                            act.sem_inc(core.passed, 1)
                            act.wait_ge(lg_done, g + 1)
                            act.sem_inc(core.passed, 1)
                            s.copy(yT[:, par, :], ps_y[:, par, :]).then_inc(yT_ready, 1)
                            s.copy(yTh[:, bass.ds(g * GROUP * P, GROUP * P)], ps_y[:, par, :]).then_inc(yTh_ready, 1)
                    act.wait_ge(left_ready, 1)
                    s.activation(flat(left[:]), flat(left[:]), ACT.Exp).then_inc(exp_ready, 1)
                    with act.Fori(0, GROUPS // 2) as g2:
                        for par in range(2):
                            g = g2 * 2 + par
                            act.wait_ge(g_turned, g + 3)
                            act.sem_inc(core.passed, 1)
                            s.copy(gT[:, bass.ds(g * GROUP * P, GROUP * P)], ps_g[0:2 * E, par, :]).then_inc(gT_ready, 1)

        with ExitStack() as ectx:
            hT = ectx.enter_context(nc.sbuf_tensor(f"{tag}_hT", [P, 2, HC, GROUP * P], F32))
            h_high = ectx.enter_context(nc.sbuf_tensor(f"{tag}_h_high", [P, 2, HC, GROUP * P], F32R))
            h_low = ectx.enter_context(nc.sbuf_tensor(f"{tag}_h_low", [P, 2, HC, GROUP * P], F32R))
            weighted = ectx.enter_context(nc.sbuf_tensor(f"{tag}_weighted", [P, 2, GROUP * P], F32))
            ps_h = ectx.enter_context(nc.psum_tensor(f"{tag}_ps_h", [P, HC, GROUP * P], F32))
            ps_o = ectx.enter_context(nc.psum_tensor(f"{tag}_ps_o", [P, 2, GROUP * P], F32))
            ps_w = ectx.enter_context(nc.psum_tensor(f"{tag}_ps_w", [P, 2, GROUP * P], F32))
            gate = ectx.enter_context(nc.sbuf_tensor(f"{tag}_gate", [P, 2, GROUP * P], F32))
            gate_done = sem("gate_done")
            gate_ready = sem("gate_ready")
            h_done = sem("h_done")
            h_ready = sem("h_ready")
            high_ready = sem("high_ready")
            high2_ready = sem("high2_ready")
            low_ready = sem("low_ready")
            out_done = sem("out_done")
            weighted_ready = sem("weighted_ready")
            added = sem("added")
            PAIRS = GROUPS // 2
            HALF = HC // 2

            with nc.Block() as block:
                @block.sync
                def _(sp):
                    for e in range(2, E):
                        sp.wait_ge(w_split, SPLITS * (e - 1))
                        load_weights(sp, e)

                @block.gpsimd
                def _(pool):
                    for e in range(2, E):
                        pool.wait_ge(out_done, 2 + (e - 1) * GROUPS)
                        split_weights(pool, e)

                @block.tensor
                def _(pe):
                    def tokens(g):
                        return bass.ds(g * GROUP * P, GROUP * P)

                    def first(slot, k, g, par):
                        pe.wait_ge(gate_ready, k + 1)
                        pe.sem_inc(core.passed, 1)
                        t.matmul(ps_w[:, par, :], select[:, slot, :], gT[:, tokens(g)], start=True, stop=True).then_inc(gate_done, 1)
                        for c in range(HC):
                            pe.wait_ge(h_ready, k * HC + c + 1)
                            pe.sem_inc(core.passed, 1)
                            cols = slice(c * P, (c + 1) * P)
                            t.matmul(ps_h[:, c, :], w_high[:, slot, 0, cols], yTh[:, tokens(g)], start=True, stop=False)
                            t.matmul(ps_h[:, c, :], w_high[:, slot, 0, cols], yTl[:, tokens(g)], start=False, stop=False)
                            t.matmul(ps_h[:, c, :], w_low[:, slot, 0, cols], yTh[:, tokens(g)],
                                     start=False, stop=True).then_inc(h_done, 1)

                    def second(slot, k, g, par):
                        pe.wait_ge(weighted_ready, k + 1)
                        pe.sem_inc(core.passed, 1)
                        for c in range(HC):
                            if c % HALF == 0:
                                pe.wait_ge(low_ready, 2 * k + 5 + c // HALF)
                                pe.sem_inc(core.passed, 1)
                            cols = slice(c * P, (c + 1) * P)
                            t.matmul(ps_o[:, par, :], w_high[:, slot, 1, cols], h_high[:, par, c, :],
                                     start=(c == 0), stop=False)
                            t.matmul(ps_o[:, par, :], w_high[:, slot, 1, cols], h_low[:, par, c, :], start=False, stop=False)
                            ins = t.matmul(ps_o[:, par, :], w_low[:, slot, 1, cols], h_high[:, par, c, :],
                                           start=False, stop=(c == HC - 1))
                        ins.then_inc(out_done, 1)

                    def expert(e, slot, ahead):
                        k0 = e * GROUPS
                        with pe.Fori(0, PAIRS - 1) as g2:
                            for par in range(2):
                                g = g2 * 2 + par
                                first(slot, k0 + g + 1, g + 1, 1 - par)
                                second(slot, k0 + g, g, par)
                        first(slot, k0 + GROUPS - 1, GROUPS - 1, 1)
                        second(slot, k0 + GROUPS - 2, GROUPS - 2, 0)
                        if ahead:
                            pe.wait_ge(w_split, SPLITS * e + 2 * SPLITS)
                            pe.sem_inc(core.passed, 1)
                            first(1 - slot, k0 + GROUPS, 0, 0)
                        second(slot, k0 + GROUPS - 1, GROUPS - 1, 1)

                    pe.wait_ge(w_split, SPLITS)
                    first(0, 0, 0, 0)
                    with pe.Fori(0, E // 2 - 1) as e2:
                        for slot in range(2):
                            expert(e2 * 2 + slot, slot, True)
                    expert(E - 2, 0, True)
                    expert(E - 1, 1, False)

                @block.scalar
                def _(act):
                    act.sem_inc(h_ready, HC)
                    act.sem_inc(low_ready, 4)
                    act.sem_inc(out_done, 2)
                    act.sem_inc(gate_ready, 2)
                    s.activation(core.warm[:], core.minus_half[:, 0:1], ACT.Gelu).then_inc(core.passed, 1)
                    with act.Fori(0, E) as e:
                        with act.Fori(0, PAIRS) as g2:
                            for par in range(2):
                                k = e * GROUPS + g2 * 2 + par
                                act.wait_ge(low_ready, 2 * k + 2)
                                act.sem_inc(core.passed, 1)
                                for c in range(HC):
                                    act.wait_ge(h_done, k * HC + c + 1)
                                    act.sem_inc(core.passed, 1)
                                    s.activation(hT[:, par, c, :], ps_h[:, c, :], ACT.Gelu,
                                                 bias=b1T[:, bass.ds(e * HC + c, 1)]).then_inc(h_ready, 1)
                                act.wait_ge(out_done, k + 1)
                                act.sem_inc(core.passed, 1)
                                act.wait_ge(h_ready, (k + 2) * HC)
                                act.sem_inc(core.passed, 1)
                                s.copy(h_high[:, par, HALF:, :], hT[:, par, HALF:, :]).then_inc(high2_ready, 1)
                                act.wait_ge(gate_done, k + 1)
                                act.sem_inc(core.passed, 1)
                                act.wait_ge(weighted_ready, k + 1)
                                act.sem_inc(core.passed, 1)
                                s.copy(gate[:, par, :], ps_w[:, par, :]).then_inc(gate_ready, 1)

                @block.vector
                def _(dve):
                    def halves(k, par):
                        dve.wait_ge(h_ready, (k + 1) * HC + HALF)
                        dve.sem_inc(core.passed, 1)
                        dve.wait_ge(out_done, k + 1)
                        dve.sem_inc(core.passed, 1)
                        v.tensor_copy(h_high[:, par, 0:HALF, :], hT[:, par, 0:HALF, :]).then_inc(high_ready, 1)
                        dve.wait_ge(high_ready, k + 1)
                        dve.sem_inc(core.passed, 1)
                        v.tensor_tensor(h_low[:, par, 0:HALF, :], hT[:, par, 0:HALF, :],
                                        h_high[:, par, 0:HALF, :].bitcast(F32), ALU.subtract).then_inc(low_ready, 1)
                        dve.wait_ge(high2_ready, k + 1)
                        dve.sem_inc(core.passed, 1)
                        v.tensor_tensor(h_low[:, par, HALF:, :], hT[:, par, HALF:, :],
                                        h_high[:, par, HALF:, :].bitcast(F32), ALU.subtract).then_inc(low_ready, 1)

                    def weigh(e, k, par):
                        dve.wait_ge(out_done, k + 3)
                        dve.sem_inc(core.passed, 1)
                        dve.wait_ge(added, k + 1)
                        dve.sem_inc(core.passed, 1)
                        dve.wait_ge(gate_ready, k + 3)
                        dve.sem_inc(core.passed, 1)
                        v.scalar_tensor_tensor(weighted[:, par, :], ps_o[:, par, :], b2T[:, bass.ds(e, 1)], gate[:, par, :],
                                               ALU.add, ALU.mult).then_inc(weighted_ready, 1)

                    def add(k, g, par):
                        dve.wait_ge(weighted_ready, k + 3)
                        dve.sem_inc(core.passed, 1)
                        a = accT[:, bass.ds(g * GROUP * P, GROUP * P)]
                        v.tensor_tensor(a, a, weighted[:, par, :], ALU.add).then_inc(added, 1)

                    def step(e, g2, ahead):
                        for par in range(2):
                            g = g2 * 2 + par
                            k = e * GROUPS + g
                            weigh(e, k, par)
                            if ahead:
                                halves(k + 2, par)
                            add(k, g, par)

                    dve.sem_inc(weighted_ready, 2)
                    dve.sem_inc(added, 2)
                    for par in range(2):
                        halves(par, par)
                    with dve.Fori(0, E - 1) as e:
                        with dve.Fori(0, PAIRS) as g2:
                            step(e, g2, True)
                    with dve.Fori(0, PAIRS - 1) as g2:
                        step(E - 1, g2, True)
                    step(E - 1, PAIRS - 1, False)

        ps_t = ps("ps_t", [P, 2, GROUP * P])
        turn_in = sb("turn_in", [P, 2, GROUP * P])
        staged = sem("staged")
        turned = sem("turned")
        x_added = sem("x_added")
        with nc.Block() as block:
            @block.scalar
            def _(act):
                with act.Fori(0, GROUPS // 2) as g2:
                    for par in range(2):
                        g = g2 * 2 + par
                        act.wait_ge(turned, g + 1)
                        act.sem_inc(core.passed, 1)
                        s.copy(turn_in[:, par, :], accT[:, bass.ds(g * GROUP * P, GROUP * P)]).then_inc(staged, 1)

            @block.tensor
            def _(pe):
                pe.sem_inc(turned, 2)
                with pe.Fori(0, GROUPS // 2) as g2:
                    for par in range(2):
                        g = g2 * 2 + par
                        pe.wait_ge(staged, g + 1)
                        pe.sem_inc(core.passed, 1)
                        pe.wait_ge(x_added, g + 1)
                        pe.sem_inc(core.passed, 1)
                        for j in range(GROUP):
                            ins = t.transpose(ps_t[:, par, j * P:(j + 1) * P], turn_in[:, par, j * P:(j + 1) * P], core.ident[:])
                        ins.then_inc(turned, 1)

            @block.vector
            def _(dve):
                dve.sem_inc(x_added, 2)
                with dve.Fori(0, GROUPS // 2) as g2:
                    for par in range(2):
                        g = g2 * 2 + par
                        dve.wait_ge(turned, g + 3)
                        dve.sem_inc(core.passed, 1)
                        xg = core.x[:, bass.ds(g * GROUP, GROUP), :]
                        v.tensor_tensor(xg, xg, ps_t[:, par, :].rearrange("p (t d) -> p t d", t=GROUP), ALU.add).then_inc(x_added, 1)
        core.clear()


LEAF = 8
LEVELS = (8, 16, 32, 64)
LEAF_FLOOR = -18.0
TWO_PI = 2 * np.pi
PI_F32 = float(np.nextafter(np.float32(np.pi), np.float32(0)))
TWO_PI_HI = float(np.float32(6.28125))
TWO_PI_LO = float(np.float32(TWO_PI - 6.28125))
ROUND_MAGIC = 1.5 * 2.0 ** 23
DVE_LINKS = 57
RMS_EPS = 1e-6


def ssm_constants():
    k, t = np.meshgrid(np.arange(P), np.arange(P), indexing="ij")
    sums = np.zeros((P, 8, P), np.float32)
    mid = (t // LEAF) * LEAF + LEAF // 2 - 1
    sums[:, 0] = ((mid < k) & (k <= t)).astype(np.float32) - ((t < k) & (k <= mid)).astype(np.float32)
    for n, size in enumerate(LEVELS):
        mid = (t // (2 * size)) * 2 * size + size - 1
        sums[:, 1 + n] = ((mid < k) & (k <= t)) | ((t < k) & (k <= mid))
    sums[:, 5] = k <= t
    sums[:, 6] = k > t
    sums[:, 7] = 1
    shift = np.zeros((P, 2, P), np.float32)
    shift[:, 0] = k == t + 1
    shift[:, 1] = (k == 0) & (t == P - 1)
    m, l = k, t
    masks = np.zeros((P, 6, P), np.float32)
    same = m // LEAF == l // LEAF
    masks[:, 0] = same & (m <= l)
    masks[:, 1] = same & (m < l)
    for n, size in enumerate(LEVELS):
        masks[:, 2 + n] = (m // (2 * size) == l // (2 * size)) & (m // size % 2 == 0) & (l // size % 2 == 1)
    return {"sums": sums, "shift": shift, "masks": masks}


def ssm(core, tag, a, consts):
    nc = core.nc
    NT, H, N, R, PD = BATCH_TILES, 32, 64, 2, 8
    DI = H * PD
    XR = DI * R
    K_OUT, K_X = 6, 7
    K_V = 5
    SCALE = float((N * R) ** -0.5)
    W_in, W_out = a["L0_attn_W_in"], a["L0_attn_W_out"]
    DP = W_in.shape[1]
    v, s, t_, g_ = nc.vector, nc.scalar, nc.tensor, nc.gpsimd
    with ExitStack() as ctx:
        def sb(name, shape, dt=F32):
            return ctx.enter_context(nc.sbuf_tensor(f"{tag}_{name}", shape, dt))

        def sem(name):
            return core.scoped_sem(ctx, f"{tag}_{name}")

        win = sb("win", [P, DP])
        wout = sb("wout", [P, 2, D])
        sums = sb("sums", [P, 8, P])
        shift = sb("shift", [P, 2, P])
        masks = sb("masks", [P, 6, P])
        A_b = sb("A_b", [P, H])
        bias_b = sb("bias_b", [P, H])
        norm_b = sb("norm_b", [P, 3, N])
        y = sb("y", [P, 2, D])
        yT = sb("yT", [P, 2, P])
        zx = sb("zx", [P, NT, DI + XR])
        raw = sb("raw", [P, NT, 288])
        rot = sb("rot", [P, NT, 3, N])
        half = [sb(f"half{i}", [P, NT, 3, N // 2]) for i in range(2)]
        sm = {n: sb(n, [P, NT, H]) for n in ("u", "e", "dt", "lam", "g", "vn", "w", "ld", "ldf", "thm", "ang",
                                             "turn", "sin", "cos", "leafx", "carry", "el")}
        dtm = sb("dtm", [P, NT])
        ss = sb("ss", [P, NT * 3])
        rs = sb("rs", [P, NT * 3])
        outp = sb("outp", [P, NT, 8, H])
        xw = sb("xw", [P, NT, K_X, H])
        X = sb("X", [P, 2, K_X, XR])
        SM = sb("SM", [P, 2, 6, 2, P])
        Y6 = sb("Y6", [P, K_OUT, DI])
        ysum = sb("ysum", [P, DI])
        u = sb("u_out", [P, 2, DI])
        usq = sb("usq", [P, 2, DI])
        uT = sb("uT", [P, 2, 2, P])
        uss = sb("uss", [P, 2])
        ums = sb("ums", [P, 2])
        urs = sb("urs", [P, 2])
        bct = sb("bct", [N, 2, 3, P])
        state = sb("state", [N, 2, DI])
        bank = ctx.enter_context(nc.psum_tensor(f"{tag}_ps", [P, 8, 512], F32))
        ps_y = [bank[:, i, 0:P] for i in (0, 7)]
        ps_theta = [bank[:, i, 0:H] for i in (5, 6)]
        ps_exp = bank[:, 1:5, :].rearrange("p b c -> p (b c)")
        ps_ang = bank[:, 5, 0:256]
        ps_tot = bank[:, 5, 256:512]
        ps_vn = bank[:, 6, 0:256]
        ps_t = [bank[0:N, i, 0:3 * P].rearrange("p (j d) -> p j d", j=3) for i in (0, 7)]
        ps_s = bank[:, 6, :].rearrange("p (s r l) -> p s r l", s=2, r=2)
        ps_o = bank[:, 1:4, :].rearrange("p b c -> p (b c)")
        ps_st = bank[0:N, 4, 0:DI]
        ps_u = bank[:, 5, 0:256].rearrange("p (i d) -> p i d", i=2)
        ps_r = bank[:, 5, 256:384]

        names = ("loaded stat_done dve_chain var_ready rstd_ready setup A_ready y_ready y_turned yT_ready proj_done "
                 "silu_done raw_done dt_in_ready dt_exp lam_in_ready lam_exp sp_ready ln_done coef_in sums_done v_ready "
                 "v_done exp_ready leafx_ready thm_ready ang_done r_ready sin_ready ss_ready rs_ready rot_ready "
                 "bc_turned bct_ready s_done sm_ready x_ready x2_ready outs_done st_done scaled state_ready u_ready u_turned uT_ready "
                 "uss_ready urs_ready r_done added ums_ready w_ready").split()
        S = {n: sem(n) for n in names}

        class Eng:

            def __init__(self, eng, b):
                self.eng, self.b = eng, b

            def wait(self, name, n, per, extra=0):
                self.eng.wait_ge(S[name], self.b * per + (n + extra))
                self.eng.sem_inc(core.passed, 1)

        with nc.Block() as block:
            @block.sync
            def _(sp):
                for dst, src in ((win[:], W_in), (wout[:], W_out.rearrange("(i p) d -> p i d", p=P)),
                                 (sums[:], consts["sums"]), (shift[:], consts["shift"]), (masks[:], consts["masks"]),
                                 (A_b[:], a["L0_attn_A_log"].unsqueeze(0).broadcast_to([P, H])),
                                 (bias_b[:], a["L0_attn_dt_bias"].unsqueeze(0).broadcast_to([P, H])),
                                 (norm_b[:, 0, :], a["L0_attn_B_norm_bias"].broadcast_to([P, N])),
                                 (norm_b[:, 1, :], a["L0_attn_B_norm_bias"].broadcast_to([P, N])),
                                 (norm_b[:, 2, :], a["L0_attn_C_norm_bias"].broadcast_to([P, N]))):
                    sp.dma_start(dst, src).then_inc(S["loaded"], 16)

            LOADS = 160

            @block.gpsimd
            def _(pool):
                core.ln_rsqrt(pool, S["var_ready"], S["rstd_ready"])
                with pool.Fori(0, BATCHES) as b:
                    E = Eng(pool, b)
                    E.wait("ss_ready", 1, 1)
                    g_.tensor_tensor(rs[:], ss[:], core.minus_half[:, 0:NT * 3], ALU.pow).then_inc(S["rs_ready"], 1)

                    def weigh(i):
                        if i >= 2:
                            E.wait("outs_done", i - 1, NT)
                        xin = zx[:, i, 256:768].rearrange("p (h d) -> p h d", h=H).unsqueeze(1).broadcast_to([P, K_X - K_V, H, 16])
                        g_.tensor_tensor(X[:, i % 2, K_V:].rearrange("p k (h d) -> p k h d", h=H), xin,
                                         xw[:, i, K_V:].unsqueeze(3).broadcast_to([P, K_X - K_V, H, 16]),
                                         ALU.mult).then_inc(S["x2_ready"], 1)

                    E.wait("w_ready", 1, 1)
                    def inverse_rms(j):
                        E.wait("uss_ready", j + 1, NT)
                        g_.tensor_scalar(ums[:, j % 2:j % 2 + 1], uss[:, j % 2:j % 2 + 1], 1.0 / DI, RMS_EPS,
                                         ALU.mult, ALU.add).then_inc(S["ums_ready"], 1)
                        E.wait("ums_ready", j + 1, NT)
                        g_.tensor_tensor(urs[:, j % 2:j % 2 + 1], ums[:, j % 2:j % 2 + 1], core.minus_half[:, 0:1],
                                         ALU.pow).then_inc(S["urs_ready"], 1)

                    weigh(0)
                    weigh(1)
                    for i in range(NT):
                        if i + 2 < NT:
                            weigh(i + 2)
                        if i >= 1:
                            inverse_rms(i - 1)
                    inverse_rms(NT - 1)

            @block.scalar
            def _(act):
                act.wait_ge(S["loaded"], LOADS)
                s.activation(A_b[:], A_b[:], ACT.Exp).then_inc(S["A_ready"], 1)
                with act.Fori(0, BATCHES) as b:
                    E = Eng(act, b)
                    E.wait("added", 1, NT)
                    for i in range(NT + 1):
                        if i < NT:
                            E.wait("y_turned", i + 1, NT)
                            s.copy(yT[:, i % 2, :], ps_y[i % 2]).then_inc(S["yT_ready"], 1)
                        if i == 0:
                            continue
                        i -= 1
                        E.wait("proj_done", i + 1, NT)
                        s0 = 1 + 2 * (i % 2)
                        s.activation(zx[:, i, 0:512], bank[:, s0, :], ACT.Silu).then_inc(S["silu_done"], 1)
                        s.activation(zx[:, i, 512:768], bank[:, s0 + 1, 0:256], ACT.Silu).then_inc(S["silu_done"], 1)
                    E.wait("dt_in_ready", 1, 1)
                    s.activation(sm["e"][:], sm["u"][:], ACT.Exp).then_inc(S["dt_exp"], 1)
                    E.wait("lam_in_ready", 1, 1)
                    s.activation(sm["el"][:], sm["lam"][:], ACT.Exp, scale=-1.0).then_inc(S["lam_exp"], 1)
                    E.wait("dt_exp", 1, 1)
                    s.activation(sm["u"][:], sm["e"][:], ACT.Ln, bias=1.0).then_inc(S["ln_done"], 1)
                    E.wait("sums_done", 1, 1)
                    s.activation(outp[:].rearrange("p t k h -> p k t h"),
                                 ps_exp.rearrange("p (k t h) -> p k t h", k=8, t=NT), ACT.Exp).then_inc(S["exp_ready"], 1)
                    s.activation(sm["leafx"][:], ps_exp[:, 0:256].rearrange("p (t h) -> p t h", t=NT), ACT.Exp,
                                 scale=-1.0).then_inc(S["leafx_ready"], 1)
                    E.wait("r_ready", 1, 1)
                    s.activation(sm["sin"][:], sm["ang"][:], ACT.Sin).then_inc(S["sin_ready"], 1)
                    s.activation(sm["cos"][:], sm["ang"][:], ACT.Sin, scale=0.5).then_inc(S["sin_ready"], 1)
                    def copy_bct(i):
                        E.wait("bc_turned", i + 1, NT)
                        s.copy(bct[:, i % 2], ps_t[i % 2]).then_inc(S["bct_ready"], 1)

                    def turn_u(j):
                        E.wait("u_ready", j + 1, NT)
                        if j >= 2:
                            E.wait("urs_ready", j - 1, NT)
                        s.activation(usq[:, j % 2, :], u[:, j % 2, :], ACT.Square,
                                     accum_out=uss[:, j % 2:j % 2 + 1]).then_inc(S["uss_ready"], 1)
                        E.wait("u_turned", j + 1, NT)
                        s.copy(uT[:, j % 2], ps_u).then_inc(S["uT_ready"], 1)

                    copy_bct(0)
                    copy_bct(1)
                    for i in range(NT):
                        if i + 2 < NT:
                            copy_bct(i + 2)
                        if i >= 1:
                            turn_u(i - 1)
                    turn_u(NT - 1)

            @block.tensor
            def _(pe):
                pe.wait_ge(S["loaded"], LOADS)
                with pe.Fori(0, BATCHES) as b:
                    E = Eng(pe, b)
                    E.wait("added", 1, NT)
                    for i in range(NT + 1):
                        if i < NT:
                            E.wait("y_ready", i + 1, NT)
                            t_.transpose(ps_y[i % 2], y[:, i % 2, :], core.ident[:]).then_inc(S["y_turned"], 1)
                        if i == 0:
                            continue
                        i -= 1
                        E.wait("yT_ready", i + 1, NT)
                        if i >= 2:
                            E.wait("silu_done", 2 * (i - 1), 2 * NT)
                            E.wait("raw_done", 2 * (i - 1), 2 * NT)
                        s0 = 1 + 2 * (i % 2)
                        lhsT = yT[:, i % 2, :]
                        t_.matmul(bank[:, s0, :], lhsT, win[:, 0:512], start=True, stop=True)
                        t_.matmul(bank[:, s0 + 1, :], lhsT, win[:, 512:1024], start=True, stop=True)
                        t_.matmul(ps_theta[i % 2], lhsT, win[:, 1024:DP], start=True,
                                  stop=True).then_inc(S["proj_done"], 1)
                    E.wait("coef_in", 1, 1)
                    E.wait("silu_done", 2 * NT, 2 * NT)
                    E.wait("raw_done", 2 * NT, 2 * NT)
                    for k in range(8):
                        ins = t_.matmul(ps_exp[:, k * 256:(k + 1) * 256], sums[:, k, :],
                                        (sm["ldf"] if k == 0 else sm["ld"])[:].rearrange("p t h -> p (t h)"),
                                        start=True, stop=True)
                    ins.then_inc(S["sums_done"], 1)
                    thm = sm["thm"][:].rearrange("p t h -> p (t h)")
                    t_.matmul(ps_ang, sums[:, 5, :], thm, start=True, stop=True)
                    t_.matmul(ps_tot, sums[:, 7, :], thm, start=True, stop=True).then_inc(S["ang_done"], 1)
                    vn = sm["vn"][:].rearrange("p t h -> p (t h)")
                    t_.matmul(ps_vn, shift[:, 0, :], vn, start=True, stop=False, skip_group_check=True)
                    t_.matmul(ps_vn[:, 0:(NT - 1) * H], shift[:, 1, :], vn[:, H:NT * H], start=False, stop=True,
                              skip_group_check=True).then_inc(S["v_done"], 1)
                    E.wait("rot_ready", 1, 1)
                    E.wait("w_ready", 1, 1)

                    def turn(i):
                        if i >= 2:
                            E.wait("bct_ready", i - 1, NT)
                        for j in range(3):
                            ins = t_.transpose(ps_t[i % 2][:, j, :], rot[:, i, j, :], core.ident[:])
                        ins.then_inc(S["bc_turned"], 1)

                    def dots(i):
                        E.wait("bct_ready", i + 1, NT)
                        if i >= 1:
                            E.wait("sm_ready", i, NT)
                        for r in range(R):
                            ins = t_.matmul(ps_s[:, i % 2, r, :], bct[:, i % 2, r, :], bct[:, i % 2, 2, :],
                                            start=True, stop=True)
                        ins.then_inc(S["s_done"], 1)

                    def xr(i, k, r):
                        return X[:, i % 2, k, :].rearrange("p (h r d) -> p h r d", h=H, r=R)[:, :, r, :]

                    def close(j):
                        E.wait("u_ready", j + 1, NT)
                        if j >= 1:
                            E.wait("added", j, NT, 1)
                        for i2 in range(2):
                            ins = t_.transpose(ps_u[:, i2, :], u[:, j % 2, i2 * P:(i2 + 1) * P], core.ident[:])
                        ins.then_inc(S["u_turned"], 1)
                        E.wait("uT_ready", j + 1, NT)
                        for i2 in range(2):
                            ins = t_.matmul(ps_r, uT[:, j % 2, i2, :], wout[:, i2, :], start=(i2 == 0), stop=(i2 == 1))
                        ins.then_inc(S["r_done"], 1)

                    turn(0)
                    turn(1)
                    dots(0)
                    dots(1)
                    for i in range(NT):
                        E.wait("x_ready", i + 1, NT)
                        E.wait("x2_ready", i + 1, NT)
                        E.wait("sm_ready", i + 1, NT)
                        if i >= 1:
                            E.wait("scaled", i, NT)
                            E.wait("state_ready", i, NT)
                        else:
                            E.wait("exp_ready", 1, 1)
                            E.wait("leafx_ready", 1, 1)
                        for k in range(6):
                            o = 0 if k < 2 else k - 1
                            for r in range(R):
                                t_.matmul(ps_o[:, o * DI:(o + 1) * DI], SM[:, i % 2, k, r, :], xr(i, k, r),
                                          start=(k != 1 and r == 0), stop=(k != 0 and r == 1), skip_group_check=True)
                        for r in range(R):
                            ins = t_.matmul(ps_st, rot[:, i, r, :], xr(i, 6, r), start=(r == 0), stop=(r == 1))
                        ins.then_inc(S["st_done"], 1)
                        t_.matmul(ps_o[:, 5 * DI:6 * DI], bct[:, i % 2, 2, :], state[:, i % 2, :],
                                  start=True, stop=True).then_inc(S["outs_done"], 1)
                        if i + 2 < NT:
                            turn(i + 2)
                        if i >= 1:
                            close(i - 1)
                        if i + 2 < NT:
                            dots(i + 2)
                    close(NT - 1)

            @block.vector
            def _(dve):
                dve.sem_inc(S["added"], 1)
                chain = Chain(dve, S["dve_chain"])
                core.ln_stats(dve, chain, S["stat_done"], S["var_ready"], S["rstd_ready"])
                dve.wait_ge(S["loaded"], LOADS)
                dve.wait_ge(S["A_ready"], 1)
                chain.link(v.tensor_scalar(A_b[:], A_b[:], -1.0, None, ALU.mult))
                v.memset(sm["carry"][:, 0, :], 0.0).then_inc(S["dve_chain"], 1)
                chain.n += 1
                chain.link(v.tensor_scalar(norm_b[:, 2, :], norm_b[:, 2, :], SCALE, None, ALU.mult))
                before = chain.n
                with dve.Fori(0, BATCHES) as b:
                    E = Eng(dve, b)
                    chain.enter(before, b, DVE_LINKS)
                    for i in range(NT + 2):
                        if i < NT:
                            if i >= 2:
                                E.wait("y_turned", i - 1, NT)
                            core.normalize(y[:, i % 2, :], b * NT + i).then_inc(S["y_ready"], 1)
                        if i >= 2:
                            j = i - 2
                            E.wait("silu_done", 2 * (j + 1), 2 * NT)
                            v.tensor_copy(raw[:, j, 0:256], bank[:, 2 + 2 * (j % 2), 256:512]).then_inc(S["raw_done"], 1)
                            v.tensor_copy(raw[:, j, 256:288], ps_theta[j % 2]).then_inc(S["raw_done"], 1)
                    E.wait("raw_done", 2 * NT, 2 * NT)
                    T3 = [P, NT, H]
                    c = {n: x[:] for n, x in sm.items()}
                    chain.link(v.tensor_tensor(c["u"], raw[:, :, 192:224], bias_b[:].unsqueeze(1).broadcast_to(T3), ALU.add))
                    v.tensor_scalar(c["u"], c["u"], 30.0, None, ALU.min).then_inc(S["dt_in_ready"], 1)
                    v.tensor_scalar(c["lam"], raw[:, :, 224:256], -80.0, None, ALU.max).then_inc(S["lam_in_ready"], 1)
                    chain.link(v.tensor_tensor(rot[:].rearrange("p t j n -> p t (j n)"), raw[:, :, 0:192], raw[:, :, 0:192], ALU.mult))
                    chain.link(v.tensor_reduce(ss[:], rot[:].rearrange("p t j n -> p (t j) n"), AX_X, ALU.add))
                    v.tensor_scalar(ss[:], ss[:], 1.0 / N, RMS_EPS, ALU.mult, ALU.add).then_inc(S["ss_ready"], 1)
                    E.wait("ln_done", 1, 1)
                    chain.link(v.tensor_scalar(c["dt"], c["u"], 0.5, 0.0001, ALU.min, ALU.max))
                    E.wait("lam_exp", 1, 1)
                    chain.link(v.tensor_scalar(c["el"], c["el"], 1.0, None, ALU.add))
                    chain.link(v.reciprocal(c["lam"], c["el"]))
                    chain.link(v.tensor_tensor(c["ld"], c["dt"], A_b[:].unsqueeze(1).broadcast_to(T3), ALU.mult))
                    chain.link(v.tensor_scalar(c["ldf"], c["ld"], LEAF_FLOOR, None, ALU.max))
                    chain.link(v.tensor_tensor(c["g"], c["lam"], c["dt"], ALU.mult))
                    chain.link(v.tensor_scalar(c["lam"], c["lam"], -1.0, 1.0, ALU.mult, ALU.add))
                    chain.link(v.tensor_tensor(c["vn"], c["lam"], c["dt"], ALU.mult))
                    chain.link(v.tensor_reduce(dtm[:], c["dt"], AX_X, ALU.add))
                    chain.link(v.tensor_scalar(dtm[:], dtm[:], 1.0 / H, None, ALU.mult))
                    v.tensor_tensor(c["thm"], raw[:, :, 256:288], dtm[:].unsqueeze(2).broadcast_to(T3),
                                    ALU.mult).then_inc(S["coef_in"], 1)
                    E.wait("rs_ready", 1, 1)
                    bc3 = raw[:, :, 0:192].rearrange("p t (j n) -> p t j n", j=3)
                    chain.link(v.tensor_tensor(bc3, bc3, rs[:].rearrange("p (t j) -> p t j", j=3).unsqueeze(3)
                                               .broadcast_to([P, NT, 3, N]), ALU.mult))
                    chain.link(v.tensor_tensor(raw[:, :, 0:192], raw[:, :, 0:192],
                                               norm_b[:].rearrange("p j n -> p (j n)").unsqueeze(1)
                                               .broadcast_to([P, NT, 3 * N]), ALU.mult))
                    E.wait("ang_done", 1, 1)
                    tot = ps_tot.rearrange("p (t h) -> p t h", t=NT)
                    for i in range(1, NT):
                        chain.link(v.tensor_tensor(c["carry"][:, i, :], c["carry"][:, i - 1, :], tot[:, i - 1, :], ALU.add))
                    chain.link(v.tensor_tensor(c["ang"], c["carry"], ps_ang.rearrange("p (t h) -> p t h", t=NT), ALU.add))
                    chain.link(v.tensor_scalar(c["turn"], c["ang"], 1.0 / TWO_PI, ROUND_MAGIC, ALU.mult, ALU.add))
                    chain.link(v.tensor_scalar(c["turn"], c["turn"], ROUND_MAGIC, None, ALU.subtract))
                    chain.link(v.scalar_tensor_tensor(c["ang"], c["turn"], -TWO_PI_HI, c["ang"], ALU.mult, ALU.add))
                    chain.link(v.scalar_tensor_tensor(c["ang"], c["turn"], -TWO_PI_LO, c["ang"], ALU.mult, ALU.add))
                    v.tensor_scalar(c["ang"], c["ang"], PI_F32, -PI_F32, ALU.min, ALU.max).then_inc(S["r_ready"], 1)
                    E.wait("v_done", 1, 1)
                    E.wait("exp_ready", 1, 1)
                    E.wait("leafx_ready", 1, 1)
                    vn = ps_vn.rearrange("p (t h) -> p t h", t=NT)
                    chain.link(v.tensor_tensor(xw[:, :, 0, :], c["leafx"], c["g"], ALU.mult))
                    chain.link(v.tensor_tensor(xw[:, :, 1, :], c["leafx"], vn, ALU.mult))
                    chain.link(v.tensor_tensor(c["w"], c["g"], vn, ALU.add))
                    chain.link(v.tensor_tensor(xw[:, :, 2:6, :], outp[:, :, 1:5, :], c["w"].unsqueeze(2)
                                               .broadcast_to([P, NT, 4, H]), ALU.mult))
                    chain.link(v.tensor_tensor(xw[:, :, 6, :], outp[:, :, 6, :], c["w"], ALU.mult))
                    dve.sem_inc(S["w_ready"], 1)
                    E.wait("sin_ready", 2, 2)
                    chain.link(v.tensor_tensor(c["cos"], c["cos"], c["cos"], ALU.mult))
                    chain.link(v.tensor_scalar(c["cos"], c["cos"], -2.0, 1.0, ALU.mult, ALU.add))
                    b1, b2 = bc3[:, :, :, 0:N // 2], bc3[:, :, :, N // 2:N]
                    cosb = c["cos"].unsqueeze(2).broadcast_to([P, NT, 3, N // 2])
                    sinb = c["sin"].unsqueeze(2).broadcast_to([P, NT, 3, N // 2])
                    for out_half, p, q, op in ((slice(0, N // 2), b1, b2, ALU.add), (slice(N // 2, N), b2, b1, ALU.subtract)):
                        chain.link(v.tensor_tensor(half[0][:], p, cosb, ALU.mult))
                        chain.link(v.tensor_tensor(half[1][:], q, sinb, ALU.mult))
                        chain.link(v.tensor_tensor(rot[:, :, :, out_half], half[0][:], half[1][:], op))
                    chain.link(v.memset(state[:, 0, :], 0.0))
                    dve.sem_inc(S["rot_ready"], 1)

                    def weigh(i):
                        if i >= 2:
                            E.wait("outs_done", i - 1, NT)
                        xin = zx[:, i, 256:768].rearrange("p (h d) -> p h d", h=H).unsqueeze(1).broadcast_to([P, K_V, H, 16])
                        v.tensor_tensor(X[:, i % 2, 0:K_V].rearrange("p k (h d) -> p k h d", h=H), xin,
                                        xw[:, i, 0:K_V].unsqueeze(3).broadcast_to([P, K_V, H, 16]), ALU.mult).then_inc(S["x_ready"], 1)
                        E.wait("s_done", i + 1, NT)
                        v.tensor_tensor(SM[:, i % 2], ps_s[:, i % 2].unsqueeze(1).broadcast_to([P, 6, 2, P]),
                                        masks[:].unsqueeze(2).broadcast_to([P, 6, 2, P]), ALU.mult).then_inc(S["sm_ready"], 1)

                    def finish(j):
                        E.wait("r_done", j + 1, NT)
                        E.wait("urs_ready", j + 1, NT)
                        xt = flat(core.x[:, bass.ds(b * NT + j, 1), :])
                        v.scalar_tensor_tensor(xt, ps_r, urs[:, j % 2:j % 2 + 1], xt, ALU.mult, ALU.add).then_inc(S["added"], 1)

                    weigh(0)
                    for i in range(NT):
                        if i + 1 < NT:
                            weigh(i + 1)
                        E.wait("outs_done", i + 1, NT)
                        chain.link(v.tensor_tensor(
                            state[:, (i + 1) % 2, :].rearrange("p (h d) -> p h d", h=H),
                            state[:, i % 2, :].rearrange("p (h d) -> p h d", h=H),
                            outp[0:N, i, 7, :].unsqueeze(2).broadcast_to([N, H, PD]), ALU.mult))
                        v.tensor_tensor(state[:, (i + 1) % 2, :], state[:, (i + 1) % 2, :], ps_st, ALU.add).then_inc(S["state_ready"], 1)
                        v.tensor_tensor(Y6[:].rearrange("p k (h d) -> p (k h) d", h=H),
                                        ps_o.rearrange("p (q d) -> p q d", d=PD),
                                        outp[:, i, 0:6, :].rearrange("p k h -> p (k h)").unsqueeze(2)
                                        .broadcast_to([P, K_OUT * H, PD]), ALU.mult).then_inc(S["scaled"], 1)
                        E.wait("scaled", i + 1, NT)
                        chain.link(v.tensor_reduce(ysum[:], Y6[:].rearrange("p k f -> p f k"), AX_X, ALU.add))
                        if i >= 2:
                            E.wait("uss_ready", i - 1, NT)
                            E.wait("u_turned", i - 1, NT)
                        v.tensor_tensor(u[:, i % 2, :], ysum[:], zx[:, i, 0:256], ALU.mult).then_inc(S["u_ready"], 1)
                        if i >= 1:
                            finish(i - 1)
                    finish(NT - 1)
                    chain.leave(before, BATCHES)
        core.clear()


def turn_weights(nc, core, ctx, tag, names, loaded, loads, bank):
    turned, copied = core.scoped_sem(ctx, f"{tag}_w_turned"), core.scoped_sem(ctx, f"{tag}_w_copied")
    with nc.Block() as block:
        @block.tensor
        def _(pe):
            pe.wait_ge(loaded, loads)
            for n, (src, dst, cols) in enumerate(names):
                nc.tensor.transpose(bank[:, n, 0:cols], src, core.ident[0:cols, 0:cols]).then_inc(turned, 1)

        @block.scalar
        def _(act):
            for n, (src, dst, cols) in enumerate(names):
                act.wait_ge(turned, n + 1)
                nc.scalar.copy(dst, bank[:, n, 0:cols]).then_inc(copied, 1)
            act.wait_ge(copied, len(names))


def lora_ffn(core, tag, base_w, base_b, gate_w, lora_A, lora_B, order_in):
    nc = core.nc
    ET, RANK, _ = lora_A.shape
    E = gate_w.shape[0]
    v, s, t_, g_ = nc.vector, nc.scalar, nc.tensor, nc.gpsimd
    with ExitStack() as ctx:
        def sb(name, shape, dt=F32):
            return ctx.enter_context(nc.sbuf_tensor(f"{tag}_{name}", shape, dt))

        def sem(name):
            return core.scoped_sem(ctx, f"{tag}_{name}")

        bank = ctx.enter_context(nc.psum_tensor(f"{tag}_ps", [P, 8, 512], F32))
        rows = sb("rows", [P, 4, P])
        wcat = sb("wcat", [P, 2 * D + E])
        lB = sb("lB", [P, D])
        bias = sb("bias", [P, D])
        order = sb("order", [P, E])
        y = sb("y", [P, 2, GROUP, D])
        yT = sb("yT", [P, 2, GROUP * P])
        z = sb("z", [P, TILES, D])
        zw = sb("zw", [P, 2, GROUP, D])
        zwT = sb("zwT", [P, 2, GROUP * P])
        logits, left, eq, key, both = (sb(n, [P, TILES, E]) for n in ("logits", "left", "eq", "key", "both"))
        te = sb("te", [P, TILES, ET])
        top = sb("top", [P, TILES])
        zero = sb("zero", [P, TILES])
        names = ("loaded stat_done var_ready rstd_ready dve_chain y_ready y_turned yT_ready proj_done "
                 "z_ready base_added left_ready exp_ready zw_ready zw_turned zwT_ready moe_done added").split()
        S = {n: sem(n) for n in names}
        with nc.Block() as block:
            @block.sync
            def _(sp):
                for dst, src in ((rows[:, 0, :], base_w), (rows[:, 1, :], lora_A.rearrange("e r d -> (e r) d")),
                                 (rows[0:E, 2, :], gate_w), (bias[:], base_b.unsqueeze(0).broadcast_to([P, D])), (order[:], order_in[:, 0:E]),
                                 (rows[:, 3, :].rearrange("p (e r) -> p e r", e=ET), lora_B.rearrange("e o r -> o e r"))):
                    sp.dma_start(dst, src).then_inc(S["loaded"], 16)
        turn_weights(nc, core, ctx, tag, [(rows[:, 0, :], wcat[:, 0:D], P), (rows[:, 1, :], wcat[:, D:2 * D], P),
                                     (rows[0:E, 2, :], wcat[:, 2 * D:2 * D + E], E), (rows[:, 3, :], lB[:], P)],
                     S["loaded"], 96, bank)

        ps_y = [bank[:, i, :] for i in (0, 1)]
        ps_p = [bank[:, i:i + 2, :].rearrange("p b (j c) -> p (b j) c", j=2) for i in (2, 5)]
        ps_l = [bank[:, i, 0:GROUP * E].rearrange("p (j e) -> p j e", j=GROUP) for i in (4, 7)]
        with nc.Block() as block:
            @block.gpsimd
            def _(pool):
                core.ln_rsqrt(pool, S["var_ready"], S["rstd_ready"])

            @block.vector
            def _(dve):
                chain = Chain(dve, S["dve_chain"])
                core.ln_stats(dve, chain, S["stat_done"], S["var_ready"], S["rstd_ready"])
                def normalize(g, par):
                    dve.wait_ge(S["y_turned"], g + 1)
                    dve.sem_inc(core.passed, 1)
                    for j in range(GROUP):
                        ins = core.normalize(y[:, par, j, :], g * GROUP + j)
                    ins.then_inc(S["y_ready"], 1)

                def add_base(g, par):
                    dve.wait_ge(S["z_ready"], g + 1)
                    dve.sem_inc(core.passed, 1)
                    xg = core.x[:, bass.ds(g * GROUP, GROUP), :]
                    v.scalar_tensor_tensor(xg, ps_p[par][:, :, 0:D], 0.5, xg, ALU.mult, ALU.add).then_inc(S["base_added"], 1)
                    dve.wait_ge(S["base_added"], 2 * g + 5)
                    dve.sem_inc(core.passed, 1)
                    v.tensor_tensor(xg, xg, bias[:].unsqueeze(1).broadcast_to([P, GROUP, D]), ALU.add).then_inc(S["base_added"], 1)

                chain.link(v.tensor_scalar(bias[:], bias[:], 0.5, None, ALU.mult))
                for par in range(2):
                    normalize(par, par)
                with dve.Fori(0, GROUPS // 2 - 1) as g2:
                    for par in range(2):
                        normalize(g2 * 2 + par + 2, par)
                        add_base(g2 * 2 + par, par)
                for par in range(2):
                    add_base(GROUPS - 2 + par, par)
                T3 = [P, TILES, ET]
                select_top2(nc, chain, logits[:], both[:], left[:], eq[:], key[:], top, order[:], E, S["left_ready"])
                dve.wait_ge(S["exp_ready"], 1)
                chain.link(v.tensor_tensor(te[:], left[:, :, 0:ET], both[:, :, 0:ET], ALU.mult))
                chain.link(v.tensor_reduce(top[:], te[:], AX_X, ALU.add))
                chain.link(v.tensor_scalar(zero[:], top[:], 0.0, None, ALU.is_equal))
                chain.link(v.tensor_tensor(top[:], top[:], zero[:], ALU.add))
                chain.link(v.reciprocal(top[:], top[:]))
                chain.link(v.tensor_tensor(te[:], te[:], top[:].unsqueeze(2).broadcast_to(T3), ALU.mult))

                def weigh(g, par):
                    dve.wait_ge(S["zw_turned"], g + 1)
                    dve.sem_inc(core.passed, 1)
                    v.tensor_tensor(zw[:, par].rearrange("p j (e r) -> p (j e) r", e=ET),
                                    z[:, bass.ds(g * GROUP, GROUP), :].rearrange("p j (e r) -> p (j e) r", e=ET),
                                    te[:, bass.ds(g * GROUP, GROUP), :].rearrange("p j e -> p (j e)").unsqueeze(2)
                                    .broadcast_to([P, GROUP * ET, RANK]), ALU.mult).then_inc(S["zw_ready"], 1)

                def add_experts(g, par):
                    dve.wait_ge(S["moe_done"], g + 1)
                    dve.sem_inc(core.passed, 1)
                    xg = core.x[:, bass.ds(g * GROUP, GROUP), :]
                    v.tensor_tensor(xg, xg, ps_p[par][:, :, 0:D], ALU.add).then_inc(S["added"], 1)

                for par in range(2):
                    weigh(par, par)
                with dve.Fori(0, GROUPS // 2 - 1) as g2:
                    for par in range(2):
                        weigh(g2 * 2 + par + 2, par)
                        add_experts(g2 * 2 + par, par)
                for par in range(2):
                    add_experts(GROUPS - 2 + par, par)

            @block.tensor
            def _(pe):
                pe.sem_inc(S["y_turned"], 2)
                pe.sem_inc(S["zw_turned"], 2)
                pe.sem_inc(S["base_added"], 4)
                pe.sem_inc(S["added"], 2)

                def turn(src, g, par, ready, turned):
                    pe.wait_ge(S[ready], g + 1)
                    pe.sem_inc(core.passed, 1)
                    for j in range(GROUP):
                        ins = t_.transpose(ps_y[par][:, j * P:(j + 1) * P], src[:, par, j, :], core.ident[:])
                    ins.then_inc(S[turned], 1)

                def project(g, par):
                    pe.wait_ge(S["base_added"], 2 * g + 2)
                    pe.sem_inc(core.passed, 1)
                    pe.wait_ge(S["yT_ready"], g + 1)
                    pe.sem_inc(core.passed, 1)
                    for j in range(GROUP):
                        lhsT = yT[:, par, j * P:(j + 1) * P]
                        t_.matmul(ps_p[par][:, j, :], lhsT, wcat[:, 0:2 * D], start=True, stop=True)
                        ins = t_.matmul(ps_l[par][:, j, :], lhsT, wcat[:, 2 * D:2 * D + E], start=True, stop=True)
                    ins.then_inc(S["proj_done"], 1)

                def experts(g, par):
                    pe.wait_ge(S["added"], g + 1)
                    pe.sem_inc(core.passed, 1)
                    pe.wait_ge(S["zwT_ready"], g + 1)
                    pe.sem_inc(core.passed, 1)
                    for j in range(GROUP):
                        ins = t_.matmul(ps_p[par][:, j, 0:D], zwT[:, par, j * P:(j + 1) * P], lB[:], start=True, stop=True)
                    ins.then_inc(S["moe_done"], 1)

                for src, ready, turned, multiply in ((y, "y_ready", "y_turned", project),
                                                     (zw, "zw_ready", "zw_turned", experts)):
                    turn(src, 0, 0, ready, turned)
                    with pe.Fori(0, GROUPS // 2 - 1) as g2:
                        for par in range(2):
                            turn(src, g2 * 2 + par + 1, 1 - par, ready, turned)
                            multiply(g2 * 2 + par, par)
                    turn(src, GROUPS - 1, 1, ready, turned)
                    multiply(GROUPS - 2, 0)
                    multiply(GROUPS - 1, 1)

            @block.scalar
            def _(act):
                def copy_turned(dst, g, par, turned, ready):
                    act.wait_ge(S[turned], g + 3)
                    act.sem_inc(core.passed, 1)
                    s.copy(dst[:, par, :], ps_y[par]).then_inc(S[ready], 1)

                def copy_out(g, par):
                    act.wait_ge(S["proj_done"], g + 1)
                    act.sem_inc(core.passed, 1)
                    s.copy(logits[:, bass.ds(g * GROUP, GROUP), :], ps_l[par])
                    s.copy(z[:, bass.ds(g * GROUP, GROUP), :], ps_p[par][:, :, D:2 * D]).then_inc(S["z_ready"], 1)

                copy_turned(yT, 0, 0, "y_turned", "yT_ready")
                with act.Fori(0, GROUPS // 2 - 1) as g2:
                    for par in range(2):
                        copy_turned(yT, g2 * 2 + par + 1, 1 - par, "y_turned", "yT_ready")
                        copy_out(g2 * 2 + par, par)
                copy_turned(yT, GROUPS - 1, 1, "y_turned", "yT_ready")
                copy_out(GROUPS - 2, 0)
                copy_out(GROUPS - 1, 1)
                act.wait_ge(S["left_ready"], 1)
                s.activation(flat(left[:]), flat(left[:]), ACT.Exp).then_inc(S["exp_ready"], 1)
                with act.Fori(0, GROUPS // 2) as g2:
                    for par in range(2):
                        copy_turned(zwT, g2 * 2 + par, par, "zw_turned", "zwT_ready")
        core.clear()


def attention(core, tag, a, consts):
    nc = core.nc
    NH, DK = 16, 8
    HG = 4
    SPLIT = 4
    SCALE = float(1.0 / np.sqrt(DK * 2.0) / 1.5)
    UNIT = 64.0
    T = TIME
    VW = DK + 1
    v, s, t_, g_ = nc.vector, nc.scalar, nc.tensor, nc.gpsimd
    with ExitStack() as ctx:
        def sb(name, shape, dt=F32):
            return ctx.enter_context(nc.sbuf_tensor(f"{tag}_{name}", shape, dt))

        def sem(name):
            return core.scoped_sem(ctx, f"{tag}_{name}")

        wqkv = sb("wqkv", [P, 3 * D])
        wo = sb("wo", [P, D])
        bias = sb("bias", [1, 4 * D])
        ones = sb("ones", [1, P])
        ident16 = sb("ident16", [P, P], F16)
        tri = sb("tri", [P, P])
        STEPS = BATCHES * HG
        qkT = sb("qkT", [P, STEPS, 2, T], F16)
        V = sb("V", [P, STEPS, BATCH_TILES, HG, VW])
        O = sb("O", [P, STEPS, BATCH_TILES, HG * DK])
        names = ("loaded ones_ready stat_done var_ready rstd_ready dve_chain y_ready y_turned yT_ready proj_done "
                 "qk_ready v_ready ss_ready norm_ready qn_ready hi_ready lo_ready split_turned qkT_ready zeroed staged s_done "
                 "e_done m_done pv_done oT_read sums_turned rec_ready o_read ost_ready o_turned oT_ready out_done added").split()
        S = {n: sem(n) for n in names}
        with ExitStack() as c2:
            rows = c2.enter_context(nc.sbuf_tensor(f"{tag}_rows", [P, 4, P], F32))
            with nc.Block() as block:
                @block.vector
                def _(dve):
                    v.memset(ones[:], 1.0).then_inc(S["ones_ready"], 1)
                    v.memset(V[:], 1.0).then_inc(S["ones_ready"], 1)
                    v.tensor_copy(ident16[:], core.ident[:]).then_inc(S["ones_ready"], 1)

                @block.sync
                def _(sp):
                    sp.wait_ge(S["ones_ready"], 3)
                    for n, x in enumerate("qkvo"):
                        sp.dma_start(rows[:, n, :], a[f"L1_attn_W{x}"]).then_inc(S["loaded"], 16)
                        sp.dma_start(bias[:, n * D:(n + 1) * D], a[f"L1_attn_b{x}"].unsqueeze(0)).then_inc(S["loaded"], 16)
                    sp.dma_start(tri[:], consts["tri"]).then_inc(S["loaded"], 16)
            bank = c2.enter_context(nc.psum_tensor(f"{tag}_psw", [P, 4, 512], F32))
            turn_weights(nc, core, ctx, tag, [(rows[:, n, :], wqkv[:, n * D:(n + 1) * D] if n < 3 else wo[:], P)
                                         for n in range(4)], S["loaded"], 144, bank)

        with ExitStack() as c2:
            def sb2(name, shape, dt=F32):
                return c2.enter_context(nc.sbuf_tensor(f"{tag}_{name}", shape, dt))

            bank = c2.enter_context(nc.psum_tensor(f"{tag}_psa", [P, 6, 512], F32))
            bank16 = c2.enter_context(nc.psum_tensor(f"{tag}_ps16", [P, 2, 1024], F16))
            y = sb2("y", [P, 2, GROUP, D])
            yT = sb2("yT", [P, 2, GROUP * P])
            qk = sb2("qk", [P, 2, GROUP, 2 * D])
            sq = sb2("sq", [P, GROUP, 2 * D])
            ss = sb2("ss", [P, 2, GROUP * 2 * NH])
            rn = sb2("rn", [P, 2, GROUP * 2 * NH])
            split = sb2("split", [P, 2, GROUP, 2, NH, SPLIT, DK], F16)
            ps_y = [bank[:, i, :] for i in (0, 5)]
            ps_qkv = bank[:, 1:5, 0:3 * D]
            PAIRS = GROUPS // 2

            with nc.Block() as block:
                @block.gpsimd
                def _(pool):
                    core.ln_rsqrt(pool, S["var_ready"], S["rstd_ready"])

                @block.vector
                def _(dve):
                    dve.sem_inc(S["yT_ready"], 2)
                    chain = Chain(dve, S["dve_chain"])
                    core.ln_stats(dve, chain, S["stat_done"], S["var_ready"], S["rstd_ready"])
                    before = chain.n

                    def normalize(g, par):
                        dve.wait_ge(S["yT_ready"], g + 1)
                        dve.sem_inc(core.passed, 1)
                        for j in range(GROUP):
                            ins = core.normalize(y[:, par, j, :], g * GROUP + j)
                        ins.then_inc(S["y_ready"], 1)

                    def lengths(g, par):
                        dve.wait_ge(S["qk_ready"], g + 2)
                        dve.sem_inc(core.passed, 1)
                        chain.link(v.tensor_tensor(sq[:], qk[:, par], qk[:, par], ALU.mult))
                        chain.link(v.tensor_reduce(ss[:, par], sq[:].rearrange("p j (h d) -> p (j h) d", d=DK), AX_X, ALU.add))
                        v.tensor_scalar(ss[:, par], ss[:, par], 1e-16, None, ALU.max).then_inc(S["ss_ready"], 1)

                    def units(g, par):
                        dve.wait_ge(S["norm_ready"], g + 1)
                        dve.sem_inc(core.passed, 1)
                        chain.link(v.reciprocal(rn[:, par], ss[:, par]))
                        qkh = qk[:, par].rearrange("p j (h d) -> p (j h) d", d=DK)
                        v.scalar_tensor_tensor(qkh, qkh, UNIT, rn[:, par].unsqueeze(2).broadcast_to([P, GROUP * 2 * NH, DK]),
                                               ALU.mult, ALU.mult).then_inc(S["qn_ready"], 1)

                    def low_halves(g, par):
                        dve.wait_ge(S["hi_ready"], 4 * g + 4)
                        dve.sem_inc(core.passed, 1)
                        for n in range(2):
                            qn = qk[:, par].rearrange("p j (n h d) -> p j n h d", n=2, d=DK)[:, :, n]
                            for m in range(2):
                                hi, lo = ((m, 2 + m) if n == 0 else (2 * m, 2 * m + 1))
                                ins = v.tensor_tensor(split[:, par, :, n, :, lo, :], qn, split[:, par, :, n, :, hi, :], ALU.subtract)
                        ins.then_inc(S["lo_ready"], 1)

                    def pair(g2, ahead):
                        for par in range(2):
                            g = g2 * 2 + par
                            lengths(g, par)
                            if ahead:
                                normalize(g + 2, par)
                            units(g, par)
                            low_halves(g, par)

                    normalize(0, 0)
                    normalize(1, 1)
                    with dve.Fori(0, PAIRS - 1) as g2:
                        chain.enter(before, g2, 6)
                        pair(g2, True)
                    chain.leave(before, PAIRS - 1)
                    pair(PAIRS - 1, False)

                @block.scalar
                def _(act):
                    def move_out(b, g, par):
                        act.wait_ge(S["y_turned"], g + 1)
                        act.sem_inc(core.passed, 1)
                        s.copy(yT[:, par, :], ps_y[par]).then_inc(S["yT_ready"], 1)
                        act.wait_ge(S["proj_done"], g + 1)
                        act.sem_inc(core.passed, 1)
                        for j in range(GROUP):
                            s.copy(V[:, bass.ds(b * HG, HG), par * GROUP + j, :, 0:DK],
                                   ps_qkv[:, j, 2 * D:3 * D].rearrange("p (g h d) -> p g h d", h=HG, d=DK)).then_inc(S["v_ready"], 1)
                        s.copy(qk[:, par], ps_qkv[:, :, 0:2 * D]).then_inc(S["qk_ready"], 1)

                    def norms(g, par):
                        act.wait_ge(S["ss_ready"], g + 1)
                        act.sem_inc(core.passed, 1)
                        s.activation(ss[:, par], ss[:, par], ACT.Sqrt).then_inc(S["norm_ready"], 1)

                    def high_halves(g, par):
                        act.wait_ge(S["qn_ready"], g + 1)
                        act.sem_inc(core.passed, 1)
                        for n in range(2):
                            qn = qk[:, par].rearrange("p j (n h d) -> p j n h d", n=2, d=DK)[:, :, n]
                            for m in range(2):
                                s.copy(split[:, par, :, n, :, m if n == 0 else 2 * m, :], qn).then_inc(S["hi_ready"], 1)

                    def store_turned(b, g, par):
                        for j in range(GROUP):
                            act.wait_ge(S["split_turned"], g * GROUP + j + 1)
                            act.sem_inc(core.passed, 1)
                            tokens = slice((par * GROUP + j) * P, (par * GROUP + j + 1) * P)
                            s.copy(qkT[:, bass.ds(b * HG, HG), :, tokens].rearrange("p g n c -> p n g c"),
                                   bank16[:, j % 2, :].rearrange("p (n g c) -> p n g c", n=2, g=HG)).then_inc(S["qkT_ready"], 1)

                    s.activation(core.warm[:], core.minus_half[:, 0:1], ACT.Sqrt, scale=-1.0).then_inc(core.passed, 1)
                    with act.Fori(0, PAIRS) as b:
                        for par in range(2):
                            move_out(b, b * 2 + par, par)
                        for par in range(2):
                            norms(b * 2 + par, par)
                            high_halves(b * 2 + par, par)
                            store_turned(b, b * 2 + par, par)

                @block.tensor
                def _(pe):
                    pe.sem_inc(S["qkT_ready"], 2)
                    pe.sem_inc(S["qk_ready"], 1)
                    with pe.Fori(0, PAIRS) as b:
                        for par in range(2):
                            g = b * 2 + par
                            pe.wait_ge(S["y_ready"], g + 1)
                            pe.sem_inc(core.passed, 1)
                            for j in range(GROUP):
                                ins = t_.transpose(ps_y[par][:, j * P:(j + 1) * P], y[:, par, j, :], core.ident[:])
                            ins.then_inc(S["y_turned"], 1)
                            pe.wait_ge(S["yT_ready"], g + 3)
                            pe.sem_inc(core.passed, 1)
                            pe.wait_ge(S["qk_ready"], g + 1)
                            pe.sem_inc(core.passed, 1)
                            for j in range(GROUP):
                                t_.matmul(ps_qkv[:, j, :], yT[:, par, j * P:(j + 1) * P], wqkv[:], start=True, stop=False)
                                ins = t_.matmul(ps_qkv[:, j, :], ones[:], bias[:, 0:3 * D], start=False, stop=True)
                            ins.then_inc(S["proj_done"], 1)
                        for par in range(2):
                            g = b * 2 + par
                            pe.wait_ge(S["lo_ready"], g + 1)
                            pe.sem_inc(core.passed, 1)
                            for j in range(GROUP):
                                pe.wait_ge(S["qkT_ready"], g * GROUP + j + 1)
                                pe.sem_inc(core.passed, 1)
                                for n in range(2 * HG):
                                    ins = t_.transpose(bank16[:, j % 2, n * P:(n + 1) * P],
                                                       split[:, par, j, n // HG, n % HG * HG:n % HG * HG + HG]
                                                       .rearrange("p h x d -> p (h x d)"), ident16[:])
                                ins.then_inc(S["split_turned"], 1)

        with ExitStack() as c2:
            def sb2(name, shape, dt=F32):
                return c2.enter_context(nc.sbuf_tensor(f"{tag}_{name}", shape, dt))

            SLOTS, PSLOTS = 3, 9
            STAGED = HG + 2
            VP = 32
            bank = c2.enter_context(nc.psum_tensor(f"{tag}_psb", [P, 8, 512], F32))
            qs = sb2("qs", [P, T], F16)
            ks = sb2("ks", [P, HG, T], F16)
            vs = sb2("vs", [P, BATCH_TILES, HG, VP])
            probs = sb2("probs", [P, PSLOTS, 1024])
            oTs = sb2("oTs", [P, T])
            rec = sb2("rec", [P, BATCH_TILES * HG])
            ps_s = [bank[:, 2 * i:2 * i + 2, :].rearrange("p b c -> p (b c)") for i in range(SLOTS)]
            ps_o = bank[:, 6:8, :].rearrange("p b c -> p (b c)")
            works, flushes = [], {}
            for k in range(BATCH_TILES // 2):
                for h in range(HG):
                    works.append([(h, 0, 0)] if k == 0 else [(h, k, 0), (h, BATCH_TILES - k, (BATCH_TILES - k) * P)])
                flushes[len(works) - 1] = [k] if k == 0 else [k, BATCH_TILES - k]
            k = BATCH_TILES // 2
            works += [[(0, k, 0), (1, k, 512)], [(2, k, 0), (3, k, 512)]]
            flushes[len(works) - 1] = [k]
            NW = len(works)
            assert NW % SLOTS == 0 and NW % PSLOTS == 0
            NF = len(flushes)
            flush_of = [sum(f < n for f in flushes) for n in range(NW)]
            place = {(h, kb): (n, at) for n, work in enumerate(works) for h, kb, at in work}

            with nc.Block() as block:
                @block.vector
                def _(dve):
                    v.memset(vs[:], 0.0).then_inc(S["zeroed"], 1)
                    v.memset(ks[:], 0.0).then_inc(S["zeroed"], 1)
                    dve.wait_ge(S["zeroed"], 2)

                    def stage(it):
                        step = qkT[:, bass.ds(it, 1)].rearrange("p a n c -> p (a n) c")
                        v.tensor_copy(qs[:], step[:, 0]).then_inc(S["staged"], 1)
                        for h in range(HG):
                            r = slice(h * 32, h * 32 + 32)
                            v.tensor_copy(ks[r, h, :], step[r, 1]).then_inc(S["staged"], 1)

                    def stage_v(it):
                        v.tensor_copy(vs[:, :, :, 0:VW], V[:, bass.ds(it, 1)].rearrange("p a t h d -> p (a t) h d")).then_inc(S["staged"], 1)

                    def mask(it, n):
                        dve.wait_ge(S["e_done"], it * NW + n + 1)
                        dve.sem_inc(core.passed, 1)
                        for _, _, at in works[n]:
                            p = probs[:, n % PSLOTS, at:at + P]
                            ins = v.tensor_tensor(p, p, tri[:], ALU.mult)
                        ins.then_inc(S["m_done"], 1)

                    def close(it):
                        dve.wait_ge(S["pv_done"], (it + 2) * NF)
                        dve.sem_inc(core.passed, 1)
                        v.tensor_copy(oTs[:], ps_o).then_inc(S["oT_read"], 1)
                        dve.wait_ge(S["sums_turned"], it + 1)
                        dve.sem_inc(core.passed, 1)
                        o = ps_o.rearrange("p (t h d) -> p t h d", t=BATCH_TILES, h=HG)
                        v.reciprocal(rec[:].rearrange("p (t h) -> p t h", h=HG).unsqueeze(3), o[:, :, :, DK:VW]).then_inc(S["rec_ready"], 1)
                        dve.wait_ge(S["rec_ready"], it + 1)
                        dve.sem_inc(core.passed, 1)
                        v.tensor_tensor(O[:, bass.ds(it, 1)].rearrange("p a t (h d) -> p (a t) h d", d=DK), o[:, :, :, 0:DK],
                                        rec[:].rearrange("p (t h) -> p t h", h=HG).unsqueeze(3)
                                        .broadcast_to([P, BATCH_TILES, HG, DK]), ALU.mult).then_inc(S["o_read"], 1)

                    def step(it, ahead):
                        for n in range(NW):
                            if ahead and n == NW - 2:
                                dve.wait_ge(S["s_done"], (it + 1) * NW)
                                dve.sem_inc(core.passed, 1)
                                stage(it + 1)
                            mask(it, n)
                        close(it)
                        if ahead:
                            stage_v(it + 1)

                    stage(0)
                    stage_v(0)
                    with dve.Fori(0, STEPS - 1) as it:
                        step(it, True)
                    step(STEPS - 1, False)

                @block.scalar
                def _(act):
                    s.activation(core.warm[:], core.minus_half[:, 0:1], ACT.Exp).then_inc(core.passed, 1)
                    act.sem_inc(S["pv_done"], NF)
                    with act.Fori(0, STEPS) as it:
                        for n in range(NW):
                            act.wait_ge(S["pv_done"], it * NF + (flush_of[n - PSLOTS] + NF if n >= PSLOTS else flush_of[n + PSLOTS]) + 1)
                            act.sem_inc(core.passed, 1)
                            act.wait_ge(S["s_done"], it * NW + n + 1)
                            act.sem_inc(core.passed, 1)
                            s.activation(probs[:, n % PSLOTS, :], ps_s[n % SLOTS], ACT.Exp,
                                         scale=SCALE / (UNIT * UNIT)).then_inc(S["e_done"], 1)

                @block.tensor
                def _(pe):
                    pe.sem_inc(S["o_read"], 1)

                    def score(it, n):
                        for h, kb, at in works[n]:
                            width, q0 = T - kb * P, kb * P
                            while width:
                                w = min(width, 512 - at % 512)
                                ins = t_.matmul(ps_s[n % SLOTS][:, at:at + w], ks[:, h, kb * P:(kb + 1) * P],
                                                qs[:, q0:q0 + w], start=True, stop=True, skip_group_check=True)
                                at, q0, width = at + w, q0 + w, width - w
                        ins.then_inc(S["s_done"], 1)

                    def gather(it, n):
                        pe.wait_ge(S["m_done"], it * NW + n + 1)
                        pe.sem_inc(core.passed, 1)
                        for kb in flushes[n]:
                            for half in range(kb // 4, 2):
                                q0 = max(kb * P, half * 512)
                                for h in range(HG):
                                    w, at = place[(h, kb)]
                                    at += q0 - kb * P
                                    ins = t_.matmul(ps_o[VP * h:VP * h + VP, q0:half * 512 + 512],
                                                    vs[:, kb, h, :], probs[:, w % PSLOTS, at:at + half * 512 + 512 - q0],
                                                    start=(kb == 0), stop=(kb == 4), skip_group_check=True)
                        return ins

                    def step(it, ahead):
                        for n in range(NW):
                            m = n + SLOTS
                            if m < NW:
                                pe.wait_ge(S["e_done"], it * NW + n + 1)
                                pe.sem_inc(core.passed, 1)
                                score(it, m)
                            elif ahead:
                                if m == NW:
                                    pe.wait_ge(S["staged"], STAGED * (it + 1) + HG + 1)
                                    pe.sem_inc(core.passed, 1)
                                pe.wait_ge(S["e_done"], it * NW + n + 1)
                                pe.sem_inc(core.passed, 1)
                                score(it + 1, m - NW)
                            if n in flushes:
                                if n == min(flushes):
                                    pe.wait_ge(S["staged"], STAGED * (it + 1))
                                    pe.sem_inc(core.passed, 1)
                                    pe.wait_ge(S["o_read"], it + 1)
                                    pe.sem_inc(core.passed, 1)
                                gather(it, n).then_inc(S["pv_done"], 1)
                        pe.wait_ge(S["oT_read"], it + 1)
                        pe.sem_inc(core.passed, 1)
                        for t in range(BATCH_TILES):
                            ins = t_.transpose(ps_o[:, t * P:(t + 1) * P], oTs[:, t * P:(t + 1) * P], core.ident[:])
                        ins.then_inc(S["sums_turned"], 1)

                    pe.wait_ge(S["staged"], HG + 1)
                    for n in range(SLOTS):
                        score(0, n)
                    with pe.Fori(0, STEPS - 1) as it:
                        step(it, True)
                    step(STEPS - 1, False)

        ostage = sb("ostage", [P, 2, GROUP, D])
        oT = sb("oT", [P, 2, GROUP * P])
        bank = ctx.enter_context(nc.psum_tensor(f"{tag}_psc", [P, 4, 512], F32))
        ps_t = [bank[:, i, :] for i in (0, 1)]
        ps_f = [bank[:, i, :].rearrange("p (j d) -> p j d", j=GROUP) for i in (2, 3)]
        with nc.Block() as block:
            @block.vector
            def _(dve):
                dve.sem_inc(S["oT_ready"], 2)
                with dve.Fori(0, GROUPS // 2) as g2:
                    for par in range(2):
                        g = g2 * 2 + par
                        dve.wait_ge(S["oT_ready"], g + 1)
                        dve.sem_inc(core.passed, 1)
                        v.tensor_copy(ostage[:, par].rearrange("p t (g c) -> p t g c", g=HG),
                                      O[:, bass.ds(g2 * HG, HG), par * GROUP:(par + 1) * GROUP, :]
                                      .rearrange("p g t c -> p t g c")).then_inc(S["ost_ready"], 1)
                        dve.wait_ge(S["out_done"], g + 1)
                        dve.sem_inc(core.passed, 1)
                        xg = core.x[:, bass.ds(g * GROUP, GROUP), :]
                        v.scalar_tensor_tensor(xg, ps_f[par], 0.5, xg, ALU.mult, ALU.add).then_inc(S["added"], 1)

            @block.tensor
            def _(pe):
                with pe.Fori(0, GROUPS // 2) as g2:
                    for par in range(2):
                        g = g2 * 2 + par
                        pe.wait_ge(S["ost_ready"], g + 1)
                        pe.sem_inc(core.passed, 1)
                        for j in range(GROUP):
                            ins = t_.transpose(ps_t[par][:, j * P:(j + 1) * P], ostage[:, par, j, :], core.ident[:])
                        ins.then_inc(S["o_turned"], 1)
                        pe.wait_ge(S["oT_ready"], g + 3)
                        pe.sem_inc(core.passed, 1)
                        for j in range(GROUP):
                            t_.matmul(ps_f[par][:, j, :], oT[:, par, j * P:(j + 1) * P], wo[:], start=True, stop=False)
                            ins = t_.matmul(ps_f[par][:, j, :], ones[:], bias[:, 3 * D:4 * D], start=False, stop=True)
                        ins.then_inc(S["out_done"], 1)

            @block.scalar
            def _(act):
                with act.Fori(0, GROUPS // 2) as g2:
                    for par in range(2):
                        g = g2 * 2 + par
                        act.wait_ge(S["o_turned"], g + 1)
                        act.sem_inc(core.passed, 1)
                        s.copy(oT[:, par, :], ps_t[par]).then_inc(S["oT_ready"], 1)
        core.clear()


def transformer(nc, a, consts, out, stages):
    with ExitStack() as ctx:
        core = Core(nc, ctx, a["L0_attn_x"], consts)
        ffn = (a["L0_ffn_Wg"], a["L0_ffn_bg"], a["L0_ffn_W1"], a["L0_ffn_b1"], a["L0_ffn_W2"], a["L0_ffn_b2"],
               consts["order"])
        lora = (a["L1_ffn_base_w"], a["L1_ffn_base_b"], a["L1_ffn_gate_w"], a["L1_ffn_lora_A"], a["L1_ffn_lora_B"],
                consts["order"])
        steps = [lambda: moe_ffn(core, "ffn1", *ffn),
                 lambda: ssm(core, "ssm", a, consts),
                 lambda: moe_ffn(core, "ffn2", *ffn),
                 lambda: lora_ffn(core, "lora1", *lora),
                 lambda: attention(core, "attn", a, consts),
                 lambda: lora_ffn(core, "lora2", *lora)]
        for n in stages:
            steps[n]()
        stored = core.sem("stored")
        with nc.Block() as block:
            @block.sync
            def _(sp):
                sp.dma_start(out.rearrange("b (t p) d -> p (b t) d", p=P), core.x[:]).then_inc(stored, 16)
                sp.wait_ge(stored, 16)


_INS = ['L0_attn_x', 'L0_attn_W_in', 'L0_attn_A_log', 'L0_attn_dt_bias', 'L0_attn_B_norm_bias', 'L0_attn_C_norm_bias',
        'L0_attn_W_out', 'L0_ffn_Wg', 'L0_ffn_bg', 'L0_ffn_W1', 'L0_ffn_b1', 'L0_ffn_W2', 'L0_ffn_b2', 'L1_attn_Wq',
        'L1_attn_bq', 'L1_attn_Wk', 'L1_attn_bk', 'L1_attn_Wv', 'L1_attn_bv', 'L1_attn_Wo', 'L1_attn_bo',
        'L1_ffn_base_w', 'L1_ffn_base_b', 'L1_ffn_gate_w', 'L1_ffn_lora_A', 'L1_ffn_lora_B']
STAGES = (0, 1, 2, 3, 4, 5)


def constants():
    c = {"ident": np.eye(P, dtype=np.float32),
         "order": np.tile(np.arange(16, 0, -1, dtype=np.float32), (P, 1))}
    c["tri"] = np.triu(np.ones((P, P), np.float32))
    c.update(ssm_constants())
    return c


def kernel(**inputs):
    import numpy as _np
    import concourse.bacc as _bacc
    from concourse.bass_utils import run_bass_kernel_spmd as _run

    nc = _bacc.Bacc("TRN2", target_bir_lowering=False, num_devices=1)
    arrays, args, consts = {}, {}, {}
    for name in _INS:
        a = _np.ascontiguousarray(inputs[name])
        arrays[f"in_{name}"] = a
        args[name] = nc.dram_tensor(f"in_{name}", a.shape, mybir.dt.from_np(a.dtype), kind="ExternalInput").ap()
    for name, a in constants().items():
        arrays[f"const_{name}"] = a
        consts[name] = nc.dram_tensor(f"const_{name}", a.shape, mybir.dt.from_np(a.dtype), kind="ExternalInput").ap()
    out = nc.dram_tensor("out_x", (BATCHES, TIME, D), F32, kind="ExternalOutput").ap()
    transformer(nc, args, consts, out, STAGES)
    r = _run(nc, [arrays], core_ids=[0])
    return r.results[0]["out_x"]
```

```python
from contextlib import ExitStack

import numpy as np

import concourse.bass as bass
from concourse import mybir

ALU = mybir.AluOpType
ACT = mybir.ActivationFunctionType
F32 = mybir.dt.float32
F16 = mybir.dt.float16
F32R = mybir.dt.float32r
AX_X = mybir.AxisListType.X

P = 128
D = 128
BATCHES, TIME = 4, 1024
TILES = BATCHES * TIME // P
BATCH_TILES = TIME // P
GROUP = 4
GROUPS = TILES // GROUP
LN_EPS = 1e-5


class Chain:

    def __init__(self, eng, sem):
        self.eng, self.sem, self.base, self.n = eng, sem, 0, 0

    def link(self, ins):
        ins.then_inc(self.sem, 1)
        self.n += 1
        self.eng.wait_ge(self.sem, self.base + self.n)

    def enter(self, before, i, per):
        self.base, self.n, self.per = i * per + before, 0, per

    def leave(self, before, count):
        assert self.n == self.per, (self.n, self.per)
        self.base, self.n = 0, before + count * self.per


class Core:

    def __init__(self, nc, ctx, x_in, consts):
        self.nc, self.ctx, self.used = nc, ctx, []
        self.x = ctx.enter_context(nc.sbuf_tensor("x_res", [P, TILES, D], F32))
        self.ident = ctx.enter_context(nc.sbuf_tensor("ident", [P, P], F32))
        self.stats = ctx.enter_context(nc.sbuf_tensor("ln_stats", [P, TILES, 6], F32))
        self.mean = ctx.enter_context(nc.sbuf_tensor("ln_mean", [P, TILES], F32))
        self.rstd = ctx.enter_context(nc.sbuf_tensor("ln_rstd", [P, TILES], F32))
        self.tmp1 = ctx.enter_context(nc.sbuf_tensor("ln_tmp1", [P, TILES], F32))
        self.tmp2 = ctx.enter_context(nc.sbuf_tensor("ln_tmp2", [P, TILES], F32))
        self.minus_half = ctx.enter_context(nc.sbuf_tensor("minus_half", [P, 256], F32))
        self.warm = ctx.enter_context(nc.sbuf_tensor("warm", [P, 1], F32))
        self.x_loaded = [self.sem(f"x_loaded{b}") for b in range(BATCHES)]
        self.ident_loaded = self.sem("ident_loaded")
        self.tiles_counted, self.counted = self.sem("tiles_counted"), 0
        self.half_ready = self.sem("half_ready")
        self.passed = self.sem("waits_passed")
        with nc.Block() as block:
            @block.gpsimd
            def _(pool):
                nc.gpsimd.memset(self.minus_half[:], -0.5).then_inc(self.half_ready, 1)

            @block.sync
            def _(sp):
                for b in range(BATCHES):
                    sp.dma_start(self.x[:, b * BATCH_TILES:(b + 1) * BATCH_TILES],
                                 x_in[b].rearrange("(t p) d -> p t d", p=P)).then_inc(self.x_loaded[b], 16)
                sp.dma_start(self.ident[:], consts["ident"]).then_inc(self.ident_loaded, 16)
                sp.wait_ge(self.ident_loaded, 16)
                sp.wait_ge(self.half_ready, 1)

            @block.vector
            def _(dve):
                for b in range(BATCHES):
                    dve.wait_ge(self.x_loaded[b], 16)
                    for t in range(BATCH_TILES):
                        self.count(b * BATCH_TILES + t)

    def sem(self, name):
        return self.ctx.enter_context(self.nc.semaphore(name))

    def scoped_sem(self, ctx, name):
        handle = ctx.enter_context(self.nc.semaphore(name))
        self.used.append(handle)
        return handle

    def clear(self):
        with self.nc.Block() as block:
            @block.gpsimd
            def _(pool):
                for handle in self.used:
                    pool.sem_clear(handle)
        self.used = []

    def count(self, t):
        tile = bass.ds(t, 1)
        self.nc.vector.bn_stats(flat(self.stats[:, tile, :]), flat(self.x[:, tile, :])).then_inc(self.tiles_counted, 1)

    def ln_stats(self, dve, chain, var_ready, rstd_ready):
        v = self.nc.vector
        self.counted += TILES
        dve.wait_ge(self.tiles_counted, self.counted)
        ts = slice(0, TILES)
        even, odd = self.stats[:, ts, 1], self.stats[:, ts, 4]
        half, var = self.tmp1[:, ts], self.tmp2[:, ts]
        v.tensor_tensor(half, even, odd, ALU.subtract).then_inc(chain.sem, 1)
        v.tensor_tensor(self.mean[:, ts], even, odd, ALU.add).then_inc(chain.sem, 1)
        chain.n += 2
        chain.link(v.tensor_tensor(var, self.stats[:, ts, 2], self.stats[:, ts, 5], ALU.add))
        chain.link(v.tensor_tensor(half, half, half, ALU.mult))
        v.tensor_scalar(self.mean[:, ts], self.mean[:, ts], 0.5, None, ALU.mult).then_inc(chain.sem, 1)
        chain.n += 1
        chain.link(v.tensor_scalar(var, var, 1.0 / D, LN_EPS, ALU.mult, ALU.add))
        v.scalar_tensor_tensor(var, half, 0.25, var, ALU.mult, ALU.add).then_inc(var_ready, 1)
        dve.wait_ge(rstd_ready, 1)

    def ln_rsqrt(self, pool, var_ready, rstd_ready):
        pool.wait_ge(var_ready, 1)
        self.nc.gpsimd.tensor_tensor(self.rstd[:], self.tmp2[:], self.minus_half[:, 0:TILES], ALU.pow).then_inc(rstd_ready, 1)

    def normalize(self, out, t):
        return self.nc.vector.tensor_scalar(out, self.x[:, bass.ds(t, 1), :].rearrange("p a b -> p (a b)"),
                                            self.mean[:, bass.ds(t, 1)], self.rstd[:, bass.ds(t, 1)],
                                            ALU.subtract, ALU.mult)


def flat(ap):
    return ap.rearrange("p a b -> p (a b)")


def select_top2(nc, chain, logits, both, left, eq, key, top, order, E, left_ready):
    v = nc.vector
    shape = [P, TILES, E]
    order_b = order.unsqueeze(1).broadcast_to(shape)

    def pick(values):
        chain.link(v.tensor_reduce(top[:], values, AX_X, ALU.max))
        chain.link(v.tensor_tensor(eq, values, top[:].unsqueeze(2).broadcast_to(shape), ALU.is_equal))
        chain.link(v.tensor_tensor(key, eq, order_b, ALU.mult))

    pick(logits)
    v.tensor_tensor(left, logits, top[:].unsqueeze(2).broadcast_to(shape), ALU.subtract).then_inc(left_ready, 1)
    chain.eng.wait_ge(left_ready, 1)
    chain.link(v.tensor_reduce(top[:], key, AX_X, ALU.max))
    chain.link(v.tensor_tensor(both, key, top[:].unsqueeze(2).broadcast_to(shape), ALU.is_equal))
    chain.link(v.scalar_tensor_tensor(flat(logits), flat(both), -1e30, flat(logits), ALU.mult, ALU.add))
    pick(logits)
    chain.link(v.tensor_reduce(top[:], key, AX_X, ALU.max))
    chain.link(v.tensor_tensor(key, key, top[:].unsqueeze(2).broadcast_to(shape), ALU.is_equal))
    chain.link(v.tensor_tensor(both, both, key, ALU.add))


def moe_ffn(core, tag, Wg, bg, W1, b1, W2, b2, order_in):
    nc = core.nc
    v, s, t, g_ = nc.vector, nc.scalar, nc.tensor, nc.gpsimd
    E, _, H = W1.shape
    HC = H // P
    SPLITS = 5
    with ExitStack() as ctx:
        def sb(name, shape, dt=F32):
            return ctx.enter_context(nc.sbuf_tensor(f"{tag}_{name}", shape, dt))

        def ps(name, shape, dt=F32):
            return ctx.enter_context(nc.psum_tensor(f"{tag}_{name}", shape, dt))

        def sem(name):
            return core.scoped_sem(ctx, f"{tag}_{name}")

        yTh = sb("yTh", [P, TILES * P], F32R)
        yTl = sb("yTl", [P, TILES * P], F32R)
        accT = sb("accT", [P, TILES * P])
        gT = sb("gT", [2 * E, TILES * P], F32R)
        b1T = sb("b1T", [P, E * HC])
        b2T = sb("b2T", [P, E])
        w_raw = sb("w_raw", [P, 2, 2, H])
        w_high = sb("w_high", [P, 2, 2, H], F32R)
        w_low = sb("w_low", [P, 2, 2, H], F32R)
        select = sb("select", [2 * E, 2, P], F32R)
        w_loaded = [sem("w_loaded0"), sem("w_loaded1")]
        w_split = sem("w_split")

        def load_weights(sp, e):
            sp.dma_start(w_raw[:, e % 2, 0, :], W1[e]).then_inc(w_loaded[e % 2], 16)
            sp.dma_start(w_raw[:, e % 2, 1, :].rearrange("p (c d) -> p c d", c=HC),
                         W2[e].rearrange("(c h) d -> h c d", c=HC)).then_inc(w_loaded[e % 2], 16)

        def split_weights(pool, e):
            slot = e % 2
            pool.wait_ge(w_loaded[slot], 32 * (e // 2) + 32)
            for w in range(2):
                g_.tensor_copy(w_high[:, slot, w, :], w_raw[:, slot, w, :]).then_inc(w_split, 1)
            g_.tensor_tensor(select[:, slot, :], core.ident[0:2 * E, e:e + 1].broadcast_to([2 * E, P]),
                             core.ident[0:2 * E, E + e:E + e + 1].broadcast_to([2 * E, P]), ALU.add).then_inc(w_split, 1)
            pool.wait_ge(w_split, SPLITS * e + 3)
            for w in range(2):
                g_.tensor_tensor(w_low[:, slot, w, :], w_raw[:, slot, w, :], w_high[:, slot, w, :].bitcast(F32),
                                 ALU.subtract).then_inc(w_split, 1)

        with ExitStack() as rctx:
            def rsb(name, shape, dt=F32):
                return rctx.enter_context(nc.sbuf_tensor(f"{tag}_{name}", shape, dt))

            def rps(name, shape, dt=F32):
                return rctx.enter_context(nc.psum_tensor(f"{tag}_{name}", shape, dt))

            y = rsb("y", [P, 2, GROUP, D])
            yT = rsb("yT", [P, 2, GROUP * P])
            wg = rsb("wg", [P, E])
            bg_all = rsb("bg", [P, E])
            b1_rows = rsb("b1_rows", [E * HC, P])
            b2_rows = rsb("b2_rows", [E, D])
            order = rsb("order", [P, E])
            gates = rsb("gates", [P, TILES, E])
            g_high = rsb("g_high", [P, TILES, E], F32R)
            g_low = rsb("g_low", [P, TILES, E])
            gstage = rsb("gstage", [P, 2, GROUP, 2, E])
            logits = rsb("logits", [P, TILES, E])
            left = rsb("left", [P, TILES, E])
            eq = rsb("eq", [P, TILES, E])
            key = rsb("key", [P, TILES, E])
            both = rsb("both", [P, TILES, E])
            top = rsb("top", [P, TILES])
            ps_y = rps("ps_y", [P, 2, GROUP * P])
            ps_l = rps("ps_l", [P, 2, 512])
            ps_g = rps("ps_g", [P, 2, 512])
            small_loaded = sem("small_loaded")
            dve_chain = sem("dve_chain")
            var_ready = sem("var_ready")
            rstd_ready = sem("rstd_ready")
            y_ready = sem("y_ready")
            y_turned = sem("y_turned")
            yT_ready = sem("yT_ready")
            yTh_ready = sem("yTh_ready")
            yTl_ready = sem("yTl_ready")
            lg_done = sem("lg_done")
            logits_ready = sem("logits_ready")
            left_ready = sem("left_ready")
            exp_ready = sem("exp_ready")
            b_turned = sem("b_turned")
            bT_ready = sem("bT_ready")
            acc_cleared = sem("acc_cleared")
            gstage_ready = sem("gstage_ready")
            g_turned = sem("g_turned")
            gT_ready = sem("gT_ready")

            with nc.Block() as block:
                @block.gpsimd
                def _(pool):
                    core.ln_rsqrt(pool, var_ready, rstd_ready)
                    g_.memset(accT[:], 0.0).then_inc(acc_cleared, 1)
                    for e in range(2):
                        split_weights(pool, e)
                    pool.wait_ge(acc_cleared, 1)

                @block.sync
                def _(sp):
                    sp.dma_start(wg[:], Wg).then_inc(small_loaded, 16)
                    sp.dma_start(bg_all[:], bg.unsqueeze(0).broadcast_to([P, E])).then_inc(small_loaded, 16)
                    sp.dma_start(b1_rows[:], b1.rearrange("e (c h) -> (e c) h", c=HC)).then_inc(small_loaded, 16)
                    sp.dma_start(b2_rows[:], b2).then_inc(small_loaded, 16)
                    sp.dma_start(order[:], order_in[:, 0:E]).then_inc(small_loaded, 16)
                    for e in range(2):
                        load_weights(sp, e)

                @block.vector
                def _(dve):
                    chain = Chain(dve, dve_chain)
                    core.ln_stats(dve, chain, var_ready, rstd_ready)

                    def normalize(g, par):
                        dve.wait_ge(yT_ready, g + 1)
                        dve.sem_inc(core.passed, 1)
                        for j in range(GROUP):
                            ins = core.normalize(y[:, par, j, :], g * GROUP + j)
                        ins.then_inc(y_ready, 1)

                    def after(g, par):
                        dve.wait_ge(yTh_ready, g + 3)
                        dve.sem_inc(core.passed, 1)
                        tokens = bass.ds(g * GROUP * P, GROUP * P)
                        v.tensor_tensor(yTl[:, tokens], yT[:, par, :], yTh[:, tokens].bitcast(F32),
                                        ALU.subtract).then_inc(yTl_ready, 1)
                        dve.wait_ge(lg_done, g + 3)
                        dve.sem_inc(core.passed, 1)
                        v.tensor_tensor(logits[:, bass.ds(g * GROUP, GROUP), :],
                                        ps_l[:, par, 0:GROUP * E].rearrange("p (t e) -> p t e", t=GROUP),
                                        bg_all[:].unsqueeze(1).broadcast_to([P, GROUP, E]), ALU.add).then_inc(logits_ready, 1)

                    dve.sem_inc(yT_ready, 2)
                    dve.wait_ge(small_loaded, 80)
                    for par in range(2):
                        normalize(par, par)
                    with dve.Fori(0, GROUPS // 2 - 1) as g2:
                        for par in range(2):
                            normalize(g2 * 2 + par + 2, par)
                            after(g2 * 2 + par, par)
                    for par in range(2):
                        after(GROUPS - 2 + par, par)
                    dve.wait_ge(logits_ready, GROUPS + 2)
                    select_top2(nc, chain, logits[:], both[:], left[:], eq[:], key[:], top, order[:], E, left_ready)
                    dve.wait_ge(exp_ready, 1)
                    chain.link(v.tensor_tensor(gates[:], left[:], both[:], ALU.mult))
                    chain.link(v.tensor_reduce(top[:], gates[:], AX_X, ALU.add))
                    chain.link(v.tensor_scalar(top[:], top[:], 1e-12, 2.0, ALU.max, ALU.mult))
                    chain.link(v.reciprocal(top[:], top[:]))
                    chain.link(v.tensor_tensor(gates[:], gates[:], top[:].unsqueeze(2).broadcast_to([P, TILES, E]), ALU.mult))
                    chain.link(v.tensor_copy(g_high[:], gates[:]))
                    chain.link(v.tensor_tensor(g_low[:], gates[:], g_high[:].bitcast(F32), ALU.subtract))
                    dve.sem_inc(gT_ready, 2)
                    with dve.Fori(0, GROUPS // 2) as g2:
                        for par in range(2):
                            g = g2 * 2 + par
                            dve.wait_ge(g_turned, g + 1)
                            dve.sem_inc(core.passed, 1)
                            tiles = bass.ds(g * GROUP, GROUP)
                            v.tensor_copy(gstage[:, par, :, 0, :], g_high[:, tiles, :].bitcast(F32)).then_inc(gstage_ready, 1)
                            v.tensor_copy(gstage[:, par, :, 1, :], g_low[:, tiles, :]).then_inc(gstage_ready, 1)

                @block.tensor
                def _(pe):
                    def turn(g, par):
                        pe.wait_ge(y_ready, g + 1)
                        pe.sem_inc(core.passed, 1)
                        pe.wait_ge(yTh_ready, g + 1)
                        pe.sem_inc(core.passed, 1)
                        for j in range(GROUP):
                            ins = t.transpose(ps_y[:, par, j * P:(j + 1) * P], y[:, par, j, :], core.ident[:])
                        ins.then_inc(y_turned, 1)

                    def score(g, par):
                        pe.wait_ge(yT_ready, g + 3)
                        pe.sem_inc(core.passed, 1)
                        pe.wait_ge(logits_ready, g + 1)
                        pe.sem_inc(core.passed, 1)
                        for j in range(GROUP):
                            ins = t.matmul(ps_l[:, par, j * E:(j + 1) * E], yT[:, par, j * P:(j + 1) * P], wg[:],
                                           start=True, stop=True)
                        ins.then_inc(lg_done, 1)

                    pe.wait_ge(small_loaded, 80)
                    t.transpose(ps_g[:, 0, 0:E * HC], b1_rows[:], core.ident[0:E * HC, 0:E * HC]).then_inc(b_turned, 1)
                    t.transpose(ps_g[:, 1, 0:E], b2_rows[:], core.ident[0:E, 0:E]).then_inc(b_turned, 1)
                    pe.wait_ge(bT_ready, 2)
                    turn(0, 0)
                    with pe.Fori(0, GROUPS // 2 - 1) as g2:
                        for par in range(2):
                            turn(g2 * 2 + par + 1, 1 - par)
                            score(g2 * 2 + par, par)
                    turn(GROUPS - 1, 1)
                    score(GROUPS - 2, 0)
                    score(GROUPS - 1, 1)
                    pe.sem_inc(g_turned, 2)
                    with pe.Fori(0, GROUPS // 2) as g2:
                        for par in range(2):
                            g = g2 * 2 + par
                            pe.wait_ge(gstage_ready, 2 * g + 2)
                            pe.sem_inc(core.passed, 1)
                            pe.wait_ge(gT_ready, g + 1)
                            pe.sem_inc(core.passed, 1)
                            for j in range(GROUP):
                                ins = t.transpose(ps_g[0:2 * E, par, j * P:(j + 1) * P], gstage[:, par, j]
                                                  .rearrange("p n e -> p (n e)"), core.ident[:])
                            ins.then_inc(g_turned, 1)

                @block.scalar
                def _(act):
                    act.wait_ge(b_turned, 2)
                    s.copy(b1T[:], ps_g[:, 0, 0:E * HC]).then_inc(bT_ready, 1)
                    s.copy(b2T[:], ps_g[:, 1, 0:E]).then_inc(bT_ready, 1)
                    act.sem_inc(yTh_ready, 2)
                    act.sem_inc(logits_ready, 2)
                    act.sem_inc(yTl_ready, 2)
                    act.sem_inc(lg_done, 2)
                    with act.Fori(0, GROUPS // 2) as g2:
                        for par in range(2):
                            g = g2 * 2 + par
                            act.wait_ge(y_turned, g + 1)
                            act.sem_inc(core.passed, 1)
                            act.wait_ge(yTl_ready, g + 1)
                            act.sem_inc(core.passed, 1)
                            act.wait_ge(lg_done, g + 1)
                            act.sem_inc(core.passed, 1)
                            s.copy(yT[:, par, :], ps_y[:, par, :]).then_inc(yT_ready, 1)
                            s.copy(yTh[:, bass.ds(g * GROUP * P, GROUP * P)], ps_y[:, par, :]).then_inc(yTh_ready, 1)
                    act.wait_ge(left_ready, 1)
                    s.activation(flat(left[:]), flat(left[:]), ACT.Exp).then_inc(exp_ready, 1)
                    with act.Fori(0, GROUPS // 2) as g2:
                        for par in range(2):
                            g = g2 * 2 + par
                            act.wait_ge(g_turned, g + 3)
                            act.sem_inc(core.passed, 1)
                            s.copy(gT[:, bass.ds(g * GROUP * P, GROUP * P)], ps_g[0:2 * E, par, :]).then_inc(gT_ready, 1)

        with ExitStack() as ectx:
            hT = ectx.enter_context(nc.sbuf_tensor(f"{tag}_hT", [P, 2, HC, GROUP * P], F32))
            h_high = ectx.enter_context(nc.sbuf_tensor(f"{tag}_h_high", [P, 2, HC, GROUP * P], F32R))
            h_low = ectx.enter_context(nc.sbuf_tensor(f"{tag}_h_low", [P, 2, HC, GROUP * P], F32R))
            weighted = ectx.enter_context(nc.sbuf_tensor(f"{tag}_weighted", [P, 2, GROUP * P], F32))
            ps_h = ectx.enter_context(nc.psum_tensor(f"{tag}_ps_h", [P, HC, GROUP * P], F32))
            ps_o = ectx.enter_context(nc.psum_tensor(f"{tag}_ps_o", [P, 2, GROUP * P], F32))
            ps_w = ectx.enter_context(nc.psum_tensor(f"{tag}_ps_w", [P, 2, GROUP * P], F32))
            gate = ectx.enter_context(nc.sbuf_tensor(f"{tag}_gate", [P, 2, GROUP * P], F32))
            gate_done = sem("gate_done")
            gate_ready = sem("gate_ready")
            h_done = sem("h_done")
            h_ready = sem("h_ready")
            high_ready = sem("high_ready")
            high2_ready = sem("high2_ready")
            low_ready = sem("low_ready")
            out_done = sem("out_done")
            weighted_ready = sem("weighted_ready")
            added = sem("added")
            PAIRS = GROUPS // 2
            HALF = HC // 2

            with nc.Block() as block:
                @block.sync
                def _(sp):
                    for e in range(2, E):
                        sp.wait_ge(w_split, SPLITS * (e - 1))
                        load_weights(sp, e)

                @block.gpsimd
                def _(pool):
                    for e in range(2, E):
                        pool.wait_ge(out_done, 2 + (e - 1) * GROUPS)
                        split_weights(pool, e)

                @block.tensor
                def _(pe):
                    def tokens(g):
                        return bass.ds(g * GROUP * P, GROUP * P)

                    def first(slot, k, g, par):
                        pe.wait_ge(gate_ready, k + 1)
                        pe.sem_inc(core.passed, 1)
                        t.matmul(ps_w[:, par, :], select[:, slot, :], gT[:, tokens(g)], start=True, stop=True).then_inc(gate_done, 1)
                        for c in range(HC):
                            pe.wait_ge(h_ready, k * HC + c + 1)
                            pe.sem_inc(core.passed, 1)
                            cols = slice(c * P, (c + 1) * P)
                            t.matmul(ps_h[:, c, :], w_high[:, slot, 0, cols], yTh[:, tokens(g)], start=True, stop=False)
                            t.matmul(ps_h[:, c, :], w_high[:, slot, 0, cols], yTl[:, tokens(g)], start=False, stop=False)
                            t.matmul(ps_h[:, c, :], w_low[:, slot, 0, cols], yTh[:, tokens(g)],
                                     start=False, stop=True).then_inc(h_done, 1)

                    def second(slot, k, g, par):
                        pe.wait_ge(weighted_ready, k + 1)
                        pe.sem_inc(core.passed, 1)
                        for c in range(HC):
                            if c % HALF == 0:
                                pe.wait_ge(low_ready, 2 * k + 5 + c // HALF)
                                pe.sem_inc(core.passed, 1)
                            cols = slice(c * P, (c + 1) * P)
                            t.matmul(ps_o[:, par, :], w_high[:, slot, 1, cols], h_high[:, par, c, :],
                                     start=(c == 0), stop=False)
                            t.matmul(ps_o[:, par, :], w_high[:, slot, 1, cols], h_low[:, par, c, :], start=False, stop=False)
                            ins = t.matmul(ps_o[:, par, :], w_low[:, slot, 1, cols], h_high[:, par, c, :],
                                           start=False, stop=(c == HC - 1))
                        ins.then_inc(out_done, 1)

                    def expert(e, slot, ahead):
                        k0 = e * GROUPS
                        with pe.Fori(0, PAIRS - 1) as g2:
                            for par in range(2):
                                g = g2 * 2 + par
                                first(slot, k0 + g + 1, g + 1, 1 - par)
                                second(slot, k0 + g, g, par)
                        first(slot, k0 + GROUPS - 1, GROUPS - 1, 1)
                        second(slot, k0 + GROUPS - 2, GROUPS - 2, 0)
                        if ahead:
                            pe.wait_ge(w_split, SPLITS * e + 2 * SPLITS)
                            pe.sem_inc(core.passed, 1)
                            first(1 - slot, k0 + GROUPS, 0, 0)
                        second(slot, k0 + GROUPS - 1, GROUPS - 1, 1)

                    pe.wait_ge(w_split, SPLITS)
                    first(0, 0, 0, 0)
                    with pe.Fori(0, E // 2 - 1) as e2:
                        for slot in range(2):
                            expert(e2 * 2 + slot, slot, True)
                    expert(E - 2, 0, True)
                    expert(E - 1, 1, False)

                @block.scalar
                def _(act):
                    act.sem_inc(h_ready, HC)
                    act.sem_inc(low_ready, 4)
                    act.sem_inc(out_done, 2)
                    act.sem_inc(gate_ready, 2)
                    s.activation(core.warm[:], core.minus_half[:, 0:1], ACT.Gelu).then_inc(core.passed, 1)
                    with act.Fori(0, E) as e:
                        with act.Fori(0, PAIRS) as g2:
                            for par in range(2):
                                k = e * GROUPS + g2 * 2 + par
                                act.wait_ge(low_ready, 2 * k + 2)
                                act.sem_inc(core.passed, 1)
                                for c in range(HC):
                                    act.wait_ge(h_done, k * HC + c + 1)
                                    act.sem_inc(core.passed, 1)
                                    s.activation(hT[:, par, c, :], ps_h[:, c, :], ACT.Gelu,
                                                 bias=b1T[:, bass.ds(e * HC + c, 1)]).then_inc(h_ready, 1)
                                act.wait_ge(out_done, k + 1)
                                act.sem_inc(core.passed, 1)
                                act.wait_ge(h_ready, (k + 2) * HC)
                                act.sem_inc(core.passed, 1)
                                s.copy(h_high[:, par, HALF:, :], hT[:, par, HALF:, :]).then_inc(high2_ready, 1)
                                act.wait_ge(gate_done, k + 1)
                                act.sem_inc(core.passed, 1)
                                act.wait_ge(weighted_ready, k + 1)
                                act.sem_inc(core.passed, 1)
                                s.copy(gate[:, par, :], ps_w[:, par, :]).then_inc(gate_ready, 1)

                @block.vector
                def _(dve):
                    def halves(k, par):
                        dve.wait_ge(h_ready, (k + 1) * HC + HALF)
                        dve.sem_inc(core.passed, 1)
                        dve.wait_ge(out_done, k + 1)
                        dve.sem_inc(core.passed, 1)
                        v.tensor_copy(h_high[:, par, 0:HALF, :], hT[:, par, 0:HALF, :]).then_inc(high_ready, 1)
                        dve.wait_ge(high_ready, k + 1)
                        dve.sem_inc(core.passed, 1)
                        v.tensor_tensor(h_low[:, par, 0:HALF, :], hT[:, par, 0:HALF, :],
                                        h_high[:, par, 0:HALF, :].bitcast(F32), ALU.subtract).then_inc(low_ready, 1)
                        dve.wait_ge(high2_ready, k + 1)
                        dve.sem_inc(core.passed, 1)
                        v.tensor_tensor(h_low[:, par, HALF:, :], hT[:, par, HALF:, :],
                                        h_high[:, par, HALF:, :].bitcast(F32), ALU.subtract).then_inc(low_ready, 1)

                    def weigh(e, k, par):
                        dve.wait_ge(out_done, k + 3)
                        dve.sem_inc(core.passed, 1)
                        dve.wait_ge(added, k + 1)
                        dve.sem_inc(core.passed, 1)
                        dve.wait_ge(gate_ready, k + 3)
                        dve.sem_inc(core.passed, 1)
                        v.scalar_tensor_tensor(weighted[:, par, :], ps_o[:, par, :], b2T[:, bass.ds(e, 1)], gate[:, par, :],
                                               ALU.add, ALU.mult).then_inc(weighted_ready, 1)

                    def add(k, g, par):
                        dve.wait_ge(weighted_ready, k + 3)
                        dve.sem_inc(core.passed, 1)
                        a = accT[:, bass.ds(g * GROUP * P, GROUP * P)]
                        v.tensor_tensor(a, a, weighted[:, par, :], ALU.add).then_inc(added, 1)

                    def step(e, g2, ahead):
                        for par in range(2):
                            g = g2 * 2 + par
                            k = e * GROUPS + g
                            weigh(e, k, par)
                            if ahead:
                                halves(k + 2, par)
                            add(k, g, par)

                    dve.sem_inc(weighted_ready, 2)
                    dve.sem_inc(added, 2)
                    for par in range(2):
                        halves(par, par)
                    with dve.Fori(0, E - 1) as e:
                        with dve.Fori(0, PAIRS) as g2:
                            step(e, g2, True)
                    with dve.Fori(0, PAIRS - 1) as g2:
                        step(E - 1, g2, True)
                    step(E - 1, PAIRS - 1, False)

        ps_t = ps("ps_t", [P, 2, GROUP * P])
        turn_in = sb("turn_in", [P, 2, GROUP * P])
        staged = sem("staged")
        turned = sem("turned")
        x_added = sem("x_added")
        with nc.Block() as block:
            @block.scalar
            def _(act):
                with act.Fori(0, GROUPS // 2) as g2:
                    for par in range(2):
                        g = g2 * 2 + par
                        act.wait_ge(turned, g + 1)
                        act.sem_inc(core.passed, 1)
                        s.copy(turn_in[:, par, :], accT[:, bass.ds(g * GROUP * P, GROUP * P)]).then_inc(staged, 1)

            @block.tensor
            def _(pe):
                pe.sem_inc(turned, 2)
                with pe.Fori(0, GROUPS // 2) as g2:
                    for par in range(2):
                        g = g2 * 2 + par
                        pe.wait_ge(staged, g + 1)
                        pe.sem_inc(core.passed, 1)
                        pe.wait_ge(x_added, g + 1)
                        pe.sem_inc(core.passed, 1)
                        for j in range(GROUP):
                            ins = t.transpose(ps_t[:, par, j * P:(j + 1) * P], turn_in[:, par, j * P:(j + 1) * P], core.ident[:])
                        ins.then_inc(turned, 1)

            @block.vector
            def _(dve):
                dve.sem_inc(x_added, 2)
                with dve.Fori(0, GROUPS // 2) as g2:
                    for par in range(2):
                        g = g2 * 2 + par
                        dve.wait_ge(turned, g + 3)
                        dve.sem_inc(core.passed, 1)
                        xg = core.x[:, bass.ds(g * GROUP, GROUP), :]
                        v.tensor_tensor(xg, xg, ps_t[:, par, :].rearrange("p (t d) -> p t d", t=GROUP), ALU.add).then_inc(x_added, 1)
                        dve.wait_ge(x_added, g + 3)
                        dve.sem_inc(core.passed, 1)
                        for j in range(GROUP):
                            core.count(g * GROUP + j)
        core.clear()


LEAF = 8
LEVELS = (8, 16, 32, 64)
LEAF_FLOOR = -18.0
TWO_PI = 2 * np.pi
PI_F32 = float(np.nextafter(np.float32(np.pi), np.float32(0)))
TWO_PI_HI = float(np.float32(6.28125))
TWO_PI_LO = float(np.float32(TWO_PI - 6.28125))
ROUND_MAGIC = 1.5 * 2.0 ** 23
DVE_LINKS = 49
RMS_EPS = 1e-6


def ssm_constants():
    k, t = np.meshgrid(np.arange(P), np.arange(P), indexing="ij")
    sums = np.zeros((P, 8, P), np.float32)
    mid = (t // LEAF) * LEAF + LEAF // 2 - 1
    sums[:, 0] = ((mid < k) & (k <= t)).astype(np.float32) - ((t < k) & (k <= mid)).astype(np.float32)
    for n, size in enumerate(LEVELS):
        mid = (t // (2 * size)) * 2 * size + size - 1
        sums[:, 1 + n] = ((mid < k) & (k <= t)) | ((t < k) & (k <= mid))
    sums[:, 5] = k <= t
    sums[:, 6] = k > t
    sums[:, 7] = 1
    shift = np.zeros((P, 2, P), np.float32)
    shift[:, 0] = k == t + 1
    shift[:, 1] = (k == 0) & (t == P - 1)
    m, l = k, t
    masks = np.zeros((P, 6, P), np.float32)
    same = m // LEAF == l // LEAF
    masks[:, 0] = same & (m <= l)
    masks[:, 1] = same & (m < l)
    for n, size in enumerate(LEVELS):
        masks[:, 2 + n] = (m // (2 * size) == l // (2 * size)) & (m // size % 2 == 0) & (l // size % 2 == 1)
    return {"sums": sums, "shift": shift, "masks": masks}


def ssm(core, tag, a, consts):
    nc = core.nc
    NT, H, N, R, PD = BATCH_TILES, 32, 64, 2, 8
    DI = H * PD
    XR = DI * R
    K_OUT, K_X = 6, 7
    K_V = 5
    SCALE = float((N * R) ** -0.5)
    W_in, W_out = a["L0_attn_W_in"], a["L0_attn_W_out"]
    DP = W_in.shape[1]
    v, s, t_, g_ = nc.vector, nc.scalar, nc.tensor, nc.gpsimd
    with ExitStack() as ctx:
        def sb(name, shape, dt=F32):
            return ctx.enter_context(nc.sbuf_tensor(f"{tag}_{name}", shape, dt))

        def sem(name):
            return core.scoped_sem(ctx, f"{tag}_{name}")

        win = sb("win", [P, DP])
        wout = sb("wout", [P, 2, D])
        sums = sb("sums", [P, 8, P])
        shift = sb("shift", [P, 2, P])
        masks = sb("masks", [P, 6, P])
        A_b = sb("A_b", [P, H])
        bias_b = sb("bias_b", [P, H])
        norm_b = sb("norm_b", [P, 3, N])
        y = sb("y", [P, 2, D])
        yT = sb("yT", [P, 2, P])
        zx = sb("zx", [P, NT, DI + XR])
        raw = sb("raw", [P, NT, 288])
        rot = sb("rot", [P, NT, 3, N])
        half = [sb(f"half{i}", [P, NT, 3, N // 2]) for i in range(2)]
        sm = {n: sb(n, [P, NT, H]) for n in ("u", "e", "dt", "lam", "g", "vn", "w", "ld", "ldf", "thm", "ang",
                                             "turn", "sin", "cos", "leafx", "carry", "el")}
        dtm = sb("dtm", [P, NT])
        ss = sb("ss", [P, NT * 3])
        rs = sb("rs", [P, NT * 3])
        outp = sb("outp", [P, NT, 8, H])
        xw = sb("xw", [P, NT, K_X, H])
        X = sb("X", [P, 2, K_X, XR])
        SM = sb("SM", [P, 2, 6, 2, P])
        Y6 = sb("Y6", [P, K_OUT, DI])
        ysum = sb("ysum", [P, DI])
        u = sb("u_out", [P, 2, DI])
        usq = sb("usq", [P, 2, DI])
        uT = sb("uT", [P, 2, 2, P])
        uss = sb("uss", [P, 2])
        ums = sb("ums", [P, 2])
        urs = sb("urs", [P, 2])
        bct = sb("bct", [N, 2, 3, P])
        state = sb("state", [N, 2, DI])
        bank = ctx.enter_context(nc.psum_tensor(f"{tag}_ps", [P, 8, 512], F32))
        ps_y = [bank[:, i, 0:P] for i in (0, 7)]
        ps_theta = [bank[:, i, 0:H] for i in (5, 6)]
        ps_exp = bank[:, 1:5, :].rearrange("p b c -> p (b c)")
        ps_ang = bank[:, 5, 0:256]
        ps_tot = bank[:, 5, 256:512]
        ps_vn = bank[:, 6, 0:256]
        ps_t = [bank[0:N, i, 0:3 * P].rearrange("p (j d) -> p j d", j=3) for i in (0, 7)]
        ps_s = bank[:, 6, :].rearrange("p (s r l) -> p s r l", s=2, r=2)
        ps_o = bank[:, 1:4, :].rearrange("p b c -> p (b c)")
        ps_st = bank[0:N, 4, 0:DI]
        ps_u = bank[:, 5, 0:256].rearrange("p (i d) -> p i d", i=2)
        ps_r = bank[:, 5, 256:384]

        names = ("loaded dve_chain var_ready rstd_ready setup A_ready y_ready y_turned yT_ready proj_done "
                 "silu_done raw_done dt_in_ready dt_exp lam_in_ready lam_exp sp_ready ln_done coef_in sums_done v_ready "
                 "v_done exp_ready leafx_ready thm_ready ang_done r_ready sin_ready ss_ready rs_ready rot_ready "
                 "bc_turned bct_ready s_done sm_ready x_ready x2_ready halved partial outs_done st_done scaled state_ready u_ready u_turned uT_ready "
                 "uss_ready urs_ready r_done added ums_ready w_ready").split()
        S = {n: sem(n) for n in names}

        class Eng:

            def __init__(self, eng, b):
                self.eng, self.b = eng, b

            def wait(self, name, n, per, extra=0):
                self.eng.wait_ge(S[name], self.b * per + (n + extra))
                self.eng.sem_inc(core.passed, 1)

        with nc.Block() as block:
            @block.sync
            def _(sp):
                for dst, src in ((win[:], W_in), (wout[:], W_out.rearrange("(i p) d -> p i d", p=P)),
                                 (sums[:], consts["sums"]), (shift[:], consts["shift"]), (masks[:], consts["masks"]),
                                 (A_b[:], a["L0_attn_A_log"].unsqueeze(0).broadcast_to([P, H])),
                                 (bias_b[:], a["L0_attn_dt_bias"].unsqueeze(0).broadcast_to([P, H])),
                                 (norm_b[:, 0, :], a["L0_attn_B_norm_bias"].broadcast_to([P, N])),
                                 (norm_b[:, 1, :], a["L0_attn_B_norm_bias"].broadcast_to([P, N])),
                                 (norm_b[:, 2, :], a["L0_attn_C_norm_bias"].broadcast_to([P, N]))):
                    sp.dma_start(dst, src).then_inc(S["loaded"], 16)

            LOADS = 160

            @block.gpsimd
            def _(pool):
                core.ln_rsqrt(pool, S["var_ready"], S["rstd_ready"])
                with pool.Fori(0, BATCHES) as b:
                    E = Eng(pool, b)
                    E.wait("ss_ready", 1, 1)
                    g_.tensor_tensor(rs[:], ss[:], core.minus_half[:, 0:NT * 3], ALU.pow).then_inc(S["rs_ready"], 1)

                    def weigh(i):
                        if i >= 2:
                            E.wait("outs_done", i - 1, NT)
                        xin = zx[:, i, 256:768].rearrange("p (h d) -> p h d", h=H).unsqueeze(1).broadcast_to([P, K_X - K_V, H, 16])
                        g_.tensor_tensor(X[:, i % 2, K_V:].rearrange("p k (h d) -> p k h d", h=H), xin,
                                         xw[:, i, K_V:].unsqueeze(3).broadcast_to([P, K_X - K_V, H, 16]),
                                         ALU.mult).then_inc(S["x2_ready"], 1)

                    E.wait("w_ready", 1, 1)
                    def inverse_rms(j):
                        E.wait("uss_ready", j + 1, NT)
                        g_.tensor_scalar(ums[:, j % 2:j % 2 + 1], uss[:, j % 2:j % 2 + 1], 1.0 / DI, RMS_EPS,
                                         ALU.mult, ALU.add).then_inc(S["ums_ready"], 1)
                        E.wait("ums_ready", j + 1, NT)
                        g_.tensor_tensor(urs[:, j % 2:j % 2 + 1], ums[:, j % 2:j % 2 + 1], core.minus_half[:, 0:1],
                                         ALU.pow).then_inc(S["urs_ready"], 1)

                    def sum_up(i):
                        E.wait("halved", i + 1, NT)
                        g_.tensor_tensor(ysum[:], Y6[:, 0], Y6[:, 1], ALU.add).then_inc(S["partial"], 1)
                        E.wait("partial", 2 * i + 1, 2 * NT)
                        g_.tensor_tensor(ysum[:], ysum[:], Y6[:, 2], ALU.add).then_inc(S["partial"], 1)
                        E.wait("partial", 2 * i + 2, 2 * NT)
                        if i >= 2:
                            E.wait("uss_ready", i - 1, NT)
                            E.wait("u_turned", i - 1, NT)
                        g_.tensor_tensor(u[:, i % 2, :], ysum[:], zx[:, i, 0:256], ALU.mult).then_inc(S["u_ready"], 1)

                    weigh(0)
                    weigh(1)
                    for i in range(NT):
                        if i + 2 < NT:
                            weigh(i + 2)
                        if i >= 1:
                            inverse_rms(i - 1)
                        sum_up(i)
                    inverse_rms(NT - 1)

            @block.scalar
            def _(act):
                act.wait_ge(S["loaded"], LOADS)
                s.activation(A_b[:], A_b[:], ACT.Exp).then_inc(S["A_ready"], 1)
                with act.Fori(0, BATCHES) as b:
                    E = Eng(act, b)
                    E.wait("added", 1, NT)
                    for i in range(NT + 1):
                        if i < NT:
                            E.wait("y_turned", i + 1, NT)
                            s.copy(yT[:, i % 2, :], ps_y[i % 2]).then_inc(S["yT_ready"], 1)
                        if i == 0:
                            continue
                        i -= 1
                        E.wait("proj_done", i + 1, NT)
                        s0 = 1 + 2 * (i % 2)
                        s.activation(zx[:, i, 0:512], bank[:, s0, :], ACT.Silu).then_inc(S["silu_done"], 1)
                        s.activation(zx[:, i, 512:768], bank[:, s0 + 1, 0:256], ACT.Silu).then_inc(S["silu_done"], 1)
                    E.wait("dt_in_ready", 1, 1)
                    s.activation(sm["e"][:], sm["u"][:], ACT.Exp).then_inc(S["dt_exp"], 1)
                    E.wait("lam_in_ready", 1, 1)
                    s.activation(sm["el"][:], sm["lam"][:], ACT.Exp, scale=-1.0).then_inc(S["lam_exp"], 1)
                    E.wait("dt_exp", 1, 1)
                    s.activation(sm["u"][:], sm["e"][:], ACT.Ln, bias=1.0).then_inc(S["ln_done"], 1)
                    E.wait("sums_done", 1, 1)
                    s.activation(outp[:].rearrange("p t k h -> p k t h"),
                                 ps_exp.rearrange("p (k t h) -> p k t h", k=8, t=NT), ACT.Exp).then_inc(S["exp_ready"], 1)
                    s.activation(sm["leafx"][:], ps_exp[:, 0:256].rearrange("p (t h) -> p t h", t=NT), ACT.Exp,
                                 scale=-1.0).then_inc(S["leafx_ready"], 1)
                    E.wait("r_ready", 1, 1)
                    s.activation(sm["sin"][:], sm["ang"][:], ACT.Sin).then_inc(S["sin_ready"], 1)
                    s.activation(sm["cos"][:], sm["ang"][:], ACT.Sin, scale=0.5).then_inc(S["sin_ready"], 1)
                    def copy_bct(i):
                        E.wait("bc_turned", i + 1, NT)
                        s.copy(bct[:, i % 2], ps_t[i % 2]).then_inc(S["bct_ready"], 1)

                    def turn_u(j):
                        E.wait("u_ready", j + 1, NT)
                        if j >= 2:
                            E.wait("urs_ready", j - 1, NT)
                        s.activation(usq[:, j % 2, :], u[:, j % 2, :], ACT.Square,
                                     accum_out=uss[:, j % 2:j % 2 + 1]).then_inc(S["uss_ready"], 1)
                        E.wait("u_turned", j + 1, NT)
                        s.copy(uT[:, j % 2], ps_u).then_inc(S["uT_ready"], 1)

                    copy_bct(0)
                    copy_bct(1)
                    for i in range(NT):
                        if i + 2 < NT:
                            copy_bct(i + 2)
                        if i >= 1:
                            turn_u(i - 1)
                    turn_u(NT - 1)

            @block.tensor
            def _(pe):
                pe.wait_ge(S["loaded"], LOADS)
                with pe.Fori(0, BATCHES) as b:
                    E = Eng(pe, b)
                    E.wait("added", 1, NT)
                    for i in range(NT + 1):
                        if i < NT:
                            E.wait("y_ready", i + 1, NT)
                            t_.transpose(ps_y[i % 2], y[:, i % 2, :], core.ident[:]).then_inc(S["y_turned"], 1)
                        if i == 0:
                            continue
                        i -= 1
                        E.wait("yT_ready", i + 1, NT)
                        if i >= 2:
                            E.wait("silu_done", 2 * (i - 1), 2 * NT)
                            E.wait("raw_done", 2 * (i - 1), 2 * NT)
                        s0 = 1 + 2 * (i % 2)
                        lhsT = yT[:, i % 2, :]
                        t_.matmul(bank[:, s0, :], lhsT, win[:, 0:512], start=True, stop=True)
                        t_.matmul(bank[:, s0 + 1, :], lhsT, win[:, 512:1024], start=True, stop=True)
                        t_.matmul(ps_theta[i % 2], lhsT, win[:, 1024:DP], start=True,
                                  stop=True).then_inc(S["proj_done"], 1)
                    E.wait("coef_in", 1, 1)
                    E.wait("silu_done", 2 * NT, 2 * NT)
                    E.wait("raw_done", 2 * NT, 2 * NT)
                    for k in range(8):
                        ins = t_.matmul(ps_exp[:, k * 256:(k + 1) * 256], sums[:, k, :],
                                        (sm["ldf"] if k == 0 else sm["ld"])[:].rearrange("p t h -> p (t h)"),
                                        start=True, stop=True)
                    ins.then_inc(S["sums_done"], 1)
                    thm = sm["thm"][:].rearrange("p t h -> p (t h)")
                    t_.matmul(ps_ang, sums[:, 5, :], thm, start=True, stop=True)
                    t_.matmul(ps_tot, sums[:, 7, :], thm, start=True, stop=True).then_inc(S["ang_done"], 1)
                    vn = sm["vn"][:].rearrange("p t h -> p (t h)")
                    t_.matmul(ps_vn, shift[:, 0, :], vn, start=True, stop=False, skip_group_check=True)
                    t_.matmul(ps_vn[:, 0:(NT - 1) * H], shift[:, 1, :], vn[:, H:NT * H], start=False, stop=True,
                              skip_group_check=True).then_inc(S["v_done"], 1)
                    E.wait("rot_ready", 1, 1)
                    E.wait("w_ready", 1, 1)

                    def turn(i):
                        if i >= 2:
                            E.wait("bct_ready", i - 1, NT)
                        for j in range(3):
                            ins = t_.transpose(ps_t[i % 2][:, j, :], rot[:, i, j, :], core.ident[:])
                        ins.then_inc(S["bc_turned"], 1)

                    def dots(i):
                        E.wait("bct_ready", i + 1, NT)
                        if i >= 1:
                            E.wait("sm_ready", i, NT)
                        for r in range(R):
                            ins = t_.matmul(ps_s[:, i % 2, r, :], bct[:, i % 2, r, :], bct[:, i % 2, 2, :],
                                            start=True, stop=True)
                        ins.then_inc(S["s_done"], 1)

                    def xr(i, k, r):
                        return X[:, i % 2, k, :].rearrange("p (h r d) -> p h r d", h=H, r=R)[:, :, r, :]

                    def close(j):
                        E.wait("u_ready", j + 1, NT)
                        if j >= 1:
                            E.wait("added", j, NT, 1)
                        for i2 in range(2):
                            ins = t_.transpose(ps_u[:, i2, :], u[:, j % 2, i2 * P:(i2 + 1) * P], core.ident[:])
                        ins.then_inc(S["u_turned"], 1)
                        E.wait("uT_ready", j + 1, NT)
                        for i2 in range(2):
                            ins = t_.matmul(ps_r, uT[:, j % 2, i2, :], wout[:, i2, :], start=(i2 == 0), stop=(i2 == 1))
                        ins.then_inc(S["r_done"], 1)

                    turn(0)
                    turn(1)
                    dots(0)
                    dots(1)
                    for i in range(NT):
                        E.wait("x_ready", i + 1, NT)
                        E.wait("x2_ready", i + 1, NT)
                        E.wait("sm_ready", i + 1, NT)
                        if i >= 1:
                            E.wait("scaled", i, NT)
                            E.wait("state_ready", i, NT)
                        else:
                            E.wait("exp_ready", 1, 1)
                            E.wait("leafx_ready", 1, 1)
                        for k in range(6):
                            o = 0 if k < 2 else k - 1
                            for r in range(R):
                                t_.matmul(ps_o[:, o * DI:(o + 1) * DI], SM[:, i % 2, k, r, :], xr(i, k, r),
                                          start=(k != 1 and r == 0), stop=(k != 0 and r == 1), skip_group_check=True)
                        for r in range(R):
                            ins = t_.matmul(ps_st, rot[:, i, r, :], xr(i, 6, r), start=(r == 0), stop=(r == 1))
                        ins.then_inc(S["st_done"], 1)
                        t_.matmul(ps_o[:, 5 * DI:6 * DI], bct[:, i % 2, 2, :], state[:, i % 2, :],
                                  start=True, stop=True).then_inc(S["outs_done"], 1)
                        if i + 2 < NT:
                            turn(i + 2)
                        if i >= 1:
                            close(i - 1)
                        if i + 2 < NT:
                            dots(i + 2)
                    close(NT - 1)

            @block.vector
            def _(dve):
                dve.sem_inc(S["added"], 1)
                chain = Chain(dve, S["dve_chain"])
                core.ln_stats(dve, chain, S["var_ready"], S["rstd_ready"])
                dve.wait_ge(S["loaded"], LOADS)
                dve.wait_ge(S["A_ready"], 1)
                chain.link(v.tensor_scalar(A_b[:], A_b[:], -1.0, None, ALU.mult))
                v.memset(sm["carry"][:, 0, :], 0.0).then_inc(S["dve_chain"], 1)
                chain.n += 1
                chain.link(v.tensor_scalar(norm_b[:, 2, :], norm_b[:, 2, :], SCALE, None, ALU.mult))
                before = chain.n
                with dve.Fori(0, BATCHES) as b:
                    E = Eng(dve, b)
                    chain.enter(before, b, DVE_LINKS)
                    for i in range(NT + 2):
                        if i < NT:
                            if i >= 2:
                                E.wait("y_turned", i - 1, NT)
                            core.normalize(y[:, i % 2, :], b * NT + i).then_inc(S["y_ready"], 1)
                        if i >= 2:
                            j = i - 2
                            E.wait("silu_done", 2 * (j + 1), 2 * NT)
                            v.tensor_copy(raw[:, j, 0:256], bank[:, 2 + 2 * (j % 2), 256:512]).then_inc(S["raw_done"], 1)
                            v.tensor_copy(raw[:, j, 256:288], ps_theta[j % 2]).then_inc(S["raw_done"], 1)
                    E.wait("raw_done", 2 * NT, 2 * NT)
                    T3 = [P, NT, H]
                    c = {n: x[:] for n, x in sm.items()}
                    chain.link(v.tensor_tensor(c["u"], raw[:, :, 192:224], bias_b[:].unsqueeze(1).broadcast_to(T3), ALU.add))
                    v.tensor_scalar(c["u"], c["u"], 30.0, None, ALU.min).then_inc(S["dt_in_ready"], 1)
                    v.tensor_scalar(c["lam"], raw[:, :, 224:256], -80.0, None, ALU.max).then_inc(S["lam_in_ready"], 1)
                    chain.link(v.tensor_tensor(rot[:].rearrange("p t j n -> p t (j n)"), raw[:, :, 0:192], raw[:, :, 0:192], ALU.mult))
                    chain.link(v.tensor_reduce(ss[:], rot[:].rearrange("p t j n -> p (t j) n"), AX_X, ALU.add))
                    v.tensor_scalar(ss[:], ss[:], 1.0 / N, RMS_EPS, ALU.mult, ALU.add).then_inc(S["ss_ready"], 1)
                    E.wait("ln_done", 1, 1)
                    chain.link(v.tensor_scalar(c["dt"], c["u"], 0.5, 0.0001, ALU.min, ALU.max))
                    E.wait("lam_exp", 1, 1)
                    chain.link(v.tensor_scalar(c["el"], c["el"], 1.0, None, ALU.add))
                    chain.link(v.reciprocal(c["lam"], c["el"]))
                    chain.link(v.tensor_tensor(c["ld"], c["dt"], A_b[:].unsqueeze(1).broadcast_to(T3), ALU.mult))
                    chain.link(v.tensor_scalar(c["ldf"], c["ld"], LEAF_FLOOR, None, ALU.max))
                    chain.link(v.tensor_tensor(c["g"], c["lam"], c["dt"], ALU.mult))
                    chain.link(v.tensor_scalar(c["lam"], c["lam"], -1.0, 1.0, ALU.mult, ALU.add))
                    chain.link(v.tensor_tensor(c["vn"], c["lam"], c["dt"], ALU.mult))
                    chain.link(v.tensor_reduce(dtm[:], c["dt"], AX_X, ALU.add))
                    chain.link(v.tensor_scalar(dtm[:], dtm[:], 1.0 / H, None, ALU.mult))
                    v.tensor_tensor(c["thm"], raw[:, :, 256:288], dtm[:].unsqueeze(2).broadcast_to(T3),
                                    ALU.mult).then_inc(S["coef_in"], 1)
                    E.wait("rs_ready", 1, 1)
                    bc3 = raw[:, :, 0:192].rearrange("p t (j n) -> p t j n", j=3)
                    chain.link(v.tensor_tensor(bc3, bc3, rs[:].rearrange("p (t j) -> p t j", j=3).unsqueeze(3)
                                               .broadcast_to([P, NT, 3, N]), ALU.mult))
                    chain.link(v.tensor_tensor(raw[:, :, 0:192], raw[:, :, 0:192],
                                               norm_b[:].rearrange("p j n -> p (j n)").unsqueeze(1)
                                               .broadcast_to([P, NT, 3 * N]), ALU.mult))
                    E.wait("ang_done", 1, 1)
                    tot = ps_tot.rearrange("p (t h) -> p t h", t=NT)
                    for i in range(1, NT):
                        chain.link(v.tensor_tensor(c["carry"][:, i, :], c["carry"][:, i - 1, :], tot[:, i - 1, :], ALU.add))
                    chain.link(v.tensor_tensor(c["ang"], c["carry"], ps_ang.rearrange("p (t h) -> p t h", t=NT), ALU.add))
                    chain.link(v.tensor_scalar(c["turn"], c["ang"], 1.0 / TWO_PI, ROUND_MAGIC, ALU.mult, ALU.add))
                    chain.link(v.tensor_scalar(c["turn"], c["turn"], ROUND_MAGIC, None, ALU.subtract))
                    chain.link(v.scalar_tensor_tensor(c["ang"], c["turn"], -TWO_PI_HI, c["ang"], ALU.mult, ALU.add))
                    chain.link(v.scalar_tensor_tensor(c["ang"], c["turn"], -TWO_PI_LO, c["ang"], ALU.mult, ALU.add))
                    v.tensor_scalar(c["ang"], c["ang"], PI_F32, -PI_F32, ALU.min, ALU.max).then_inc(S["r_ready"], 1)
                    E.wait("v_done", 1, 1)
                    E.wait("exp_ready", 1, 1)
                    E.wait("leafx_ready", 1, 1)
                    vn = ps_vn.rearrange("p (t h) -> p t h", t=NT)
                    chain.link(v.tensor_tensor(xw[:, :, 0, :], c["leafx"], c["g"], ALU.mult))
                    chain.link(v.tensor_tensor(xw[:, :, 1, :], c["leafx"], vn, ALU.mult))
                    chain.link(v.tensor_tensor(c["w"], c["g"], vn, ALU.add))
                    chain.link(v.tensor_tensor(xw[:, :, 2:6, :], outp[:, :, 1:5, :], c["w"].unsqueeze(2)
                                               .broadcast_to([P, NT, 4, H]), ALU.mult))
                    chain.link(v.tensor_tensor(xw[:, :, 6, :], outp[:, :, 6, :], c["w"], ALU.mult))
                    dve.sem_inc(S["w_ready"], 1)
                    E.wait("sin_ready", 2, 2)
                    chain.link(v.tensor_tensor(c["cos"], c["cos"], c["cos"], ALU.mult))
                    chain.link(v.tensor_scalar(c["cos"], c["cos"], -2.0, 1.0, ALU.mult, ALU.add))
                    b1, b2 = bc3[:, :, :, 0:N // 2], bc3[:, :, :, N // 2:N]
                    cosb = c["cos"].unsqueeze(2).broadcast_to([P, NT, 3, N // 2])
                    sinb = c["sin"].unsqueeze(2).broadcast_to([P, NT, 3, N // 2])
                    for out_half, p, q, op in ((slice(0, N // 2), b1, b2, ALU.add), (slice(N // 2, N), b2, b1, ALU.subtract)):
                        chain.link(v.tensor_tensor(half[0][:], p, cosb, ALU.mult))
                        chain.link(v.tensor_tensor(half[1][:], q, sinb, ALU.mult))
                        chain.link(v.tensor_tensor(rot[:, :, :, out_half], half[0][:], half[1][:], op))
                    chain.link(v.memset(state[:, 0, :], 0.0))
                    dve.sem_inc(S["rot_ready"], 1)

                    def weigh(i):
                        if i >= 2:
                            E.wait("outs_done", i - 1, NT)
                        xin = zx[:, i, 256:768].rearrange("p (h d) -> p h d", h=H).unsqueeze(1).broadcast_to([P, K_V, H, 16])
                        v.tensor_tensor(X[:, i % 2, 0:K_V].rearrange("p k (h d) -> p k h d", h=H), xin,
                                        xw[:, i, 0:K_V].unsqueeze(3).broadcast_to([P, K_V, H, 16]), ALU.mult).then_inc(S["x_ready"], 1)
                        E.wait("s_done", i + 1, NT)
                        v.tensor_tensor(SM[:, i % 2], ps_s[:, i % 2].unsqueeze(1).broadcast_to([P, 6, 2, P]),
                                        masks[:].unsqueeze(2).broadcast_to([P, 6, 2, P]), ALU.mult).then_inc(S["sm_ready"], 1)

                    def finish(j):
                        E.wait("r_done", j + 1, NT)
                        E.wait("urs_ready", j + 1, NT)
                        xt = flat(core.x[:, bass.ds(b * NT + j, 1), :])
                        v.scalar_tensor_tensor(xt, ps_r, urs[:, j % 2:j % 2 + 1], xt, ALU.mult, ALU.add).then_inc(S["added"], 1)
                        E.wait("added", j + 1, NT, 1)
                        core.count(b * NT + j)

                    weigh(0)
                    for i in range(NT):
                        if i + 1 < NT:
                            weigh(i + 1)
                        E.wait("outs_done", i + 1, NT)
                        chain.link(v.tensor_tensor(
                            state[:, (i + 1) % 2, :].rearrange("p (h d) -> p h d", h=H),
                            state[:, i % 2, :].rearrange("p (h d) -> p h d", h=H),
                            outp[0:N, i, 7, :].unsqueeze(2).broadcast_to([N, H, PD]), ALU.mult))
                        v.tensor_tensor(state[:, (i + 1) % 2, :], state[:, (i + 1) % 2, :], ps_st, ALU.add).then_inc(S["state_ready"], 1)
                        if i >= 1:
                            E.wait("u_ready", i, NT)
                        v.tensor_tensor(Y6[:].rearrange("p k (h d) -> p (k h) d", h=H),
                                        ps_o.rearrange("p (q d) -> p q d", d=PD),
                                        outp[:, i, 0:6, :].rearrange("p k h -> p (k h)").unsqueeze(2)
                                        .broadcast_to([P, K_OUT * H, PD]), ALU.mult).then_inc(S["scaled"], 1)
                        E.wait("scaled", i + 1, NT)
                        v.tensor_tensor(Y6[:, 0:3], Y6[:, 0:3], Y6[:, 3:6], ALU.add).then_inc(S["halved"], 1)
                        if i >= 1:
                            finish(i - 1)
                    finish(NT - 1)
                    chain.leave(before, BATCHES)
        core.clear()


def turn_weights(nc, core, ctx, tag, names, loaded, loads, bank):
    turned, copied = core.scoped_sem(ctx, f"{tag}_w_turned"), core.scoped_sem(ctx, f"{tag}_w_copied")
    with nc.Block() as block:
        @block.tensor
        def _(pe):
            pe.wait_ge(loaded, loads)
            for n, (src, dst, cols) in enumerate(names):
                nc.tensor.transpose(bank[:, n, 0:cols], src, core.ident[0:cols, 0:cols]).then_inc(turned, 1)

        @block.scalar
        def _(act):
            for n, (src, dst, cols) in enumerate(names):
                act.wait_ge(turned, n + 1)
                nc.scalar.copy(dst, bank[:, n, 0:cols]).then_inc(copied, 1)
            act.wait_ge(copied, len(names))


def lora_ffn(core, tag, base_w, base_b, gate_w, lora_A, lora_B, order_in):
    nc = core.nc
    ET, RANK, _ = lora_A.shape
    E = gate_w.shape[0]
    v, s, t_, g_ = nc.vector, nc.scalar, nc.tensor, nc.gpsimd
    with ExitStack() as ctx:
        def sb(name, shape, dt=F32):
            return ctx.enter_context(nc.sbuf_tensor(f"{tag}_{name}", shape, dt))

        def sem(name):
            return core.scoped_sem(ctx, f"{tag}_{name}")

        bank = ctx.enter_context(nc.psum_tensor(f"{tag}_ps", [P, 8, 512], F32))
        rows = sb("rows", [P, 4, P])
        wcat = sb("wcat", [P, 2 * D + E])
        lB = sb("lB", [P, D])
        bias = sb("bias", [P, D])
        order = sb("order", [P, E])
        y = sb("y", [P, 2, GROUP, D])
        yT = sb("yT", [P, 2, GROUP * P])
        z = sb("z", [P, TILES, D])
        zw = sb("zw", [P, 2, GROUP, D])
        zwT = sb("zwT", [P, 2, GROUP * P])
        logits, left, eq, key, both = (sb(n, [P, TILES, E]) for n in ("logits", "left", "eq", "key", "both"))
        te = sb("te", [P, TILES, ET])
        top = sb("top", [P, TILES])
        zero = sb("zero", [P, TILES])
        names = ("loaded var_ready rstd_ready dve_chain y_ready y_turned yT_ready proj_done "
                 "z_ready base_added left_ready exp_ready zw_ready zw_turned zwT_ready moe_done added").split()
        S = {n: sem(n) for n in names}
        with nc.Block() as block:
            @block.sync
            def _(sp):
                for dst, src in ((rows[:, 0, :], base_w), (rows[:, 1, :], lora_A.rearrange("e r d -> (e r) d")),
                                 (rows[0:E, 2, :], gate_w), (bias[:], base_b.unsqueeze(0).broadcast_to([P, D])), (order[:], order_in[:, 0:E]),
                                 (rows[:, 3, :].rearrange("p (e r) -> p e r", e=ET), lora_B.rearrange("e o r -> o e r"))):
                    sp.dma_start(dst, src).then_inc(S["loaded"], 16)
        turn_weights(nc, core, ctx, tag, [(rows[:, 0, :], wcat[:, 0:D], P), (rows[:, 1, :], wcat[:, D:2 * D], P),
                                     (rows[0:E, 2, :], wcat[:, 2 * D:2 * D + E], E), (rows[:, 3, :], lB[:], P)],
                     S["loaded"], 96, bank)

        ps_y = [bank[:, i, :] for i in (0, 1)]
        ps_p = [bank[:, i:i + 2, :].rearrange("p b (j c) -> p (b j) c", j=2) for i in (2, 5)]
        ps_l = [bank[:, i, 0:GROUP * E].rearrange("p (j e) -> p j e", j=GROUP) for i in (4, 7)]
        with nc.Block() as block:
            @block.gpsimd
            def _(pool):
                core.ln_rsqrt(pool, S["var_ready"], S["rstd_ready"])

            @block.vector
            def _(dve):
                chain = Chain(dve, S["dve_chain"])
                core.ln_stats(dve, chain, S["var_ready"], S["rstd_ready"])
                def normalize(g, par):
                    dve.wait_ge(S["y_turned"], g + 1)
                    dve.sem_inc(core.passed, 1)
                    for j in range(GROUP):
                        ins = core.normalize(y[:, par, j, :], g * GROUP + j)
                    ins.then_inc(S["y_ready"], 1)

                def add_base(g, par):
                    dve.wait_ge(S["z_ready"], g + 1)
                    dve.sem_inc(core.passed, 1)
                    xg = core.x[:, bass.ds(g * GROUP, GROUP), :]
                    v.scalar_tensor_tensor(xg, ps_p[par][:, :, 0:D], 0.5, xg, ALU.mult, ALU.add).then_inc(S["base_added"], 1)
                    dve.wait_ge(S["base_added"], 2 * g + 5)
                    dve.sem_inc(core.passed, 1)
                    v.tensor_tensor(xg, xg, bias[:].unsqueeze(1).broadcast_to([P, GROUP, D]), ALU.add).then_inc(S["base_added"], 1)

                chain.link(v.tensor_scalar(bias[:], bias[:], 0.5, None, ALU.mult))
                for par in range(2):
                    normalize(par, par)
                with dve.Fori(0, GROUPS // 2 - 1) as g2:
                    for par in range(2):
                        normalize(g2 * 2 + par + 2, par)
                        add_base(g2 * 2 + par, par)
                for par in range(2):
                    add_base(GROUPS - 2 + par, par)
                T3 = [P, TILES, ET]
                select_top2(nc, chain, logits[:], both[:], left[:], eq[:], key[:], top, order[:], E, S["left_ready"])
                dve.wait_ge(S["exp_ready"], 1)
                chain.link(v.tensor_tensor(te[:], left[:, :, 0:ET], both[:, :, 0:ET], ALU.mult))
                chain.link(v.tensor_reduce(top[:], te[:], AX_X, ALU.add))
                chain.link(v.tensor_scalar(zero[:], top[:], 0.0, None, ALU.is_equal))
                chain.link(v.tensor_tensor(top[:], top[:], zero[:], ALU.add))
                chain.link(v.reciprocal(top[:], top[:]))
                chain.link(v.tensor_tensor(te[:], te[:], top[:].unsqueeze(2).broadcast_to(T3), ALU.mult))

                def weigh(g, par):
                    dve.wait_ge(S["zw_turned"], g + 1)
                    dve.sem_inc(core.passed, 1)
                    v.tensor_tensor(zw[:, par].rearrange("p j (e r) -> p (j e) r", e=ET),
                                    z[:, bass.ds(g * GROUP, GROUP), :].rearrange("p j (e r) -> p (j e) r", e=ET),
                                    te[:, bass.ds(g * GROUP, GROUP), :].rearrange("p j e -> p (j e)").unsqueeze(2)
                                    .broadcast_to([P, GROUP * ET, RANK]), ALU.mult).then_inc(S["zw_ready"], 1)

                def add_experts(g, par):
                    dve.wait_ge(S["moe_done"], g + 1)
                    dve.sem_inc(core.passed, 1)
                    xg = core.x[:, bass.ds(g * GROUP, GROUP), :]
                    v.tensor_tensor(xg, xg, ps_p[par][:, :, 0:D], ALU.add).then_inc(S["added"], 1)
                    dve.wait_ge(S["added"], g + 3)
                    dve.sem_inc(core.passed, 1)
                    for j in range(GROUP):
                        core.count(g * GROUP + j)

                for par in range(2):
                    weigh(par, par)
                with dve.Fori(0, GROUPS // 2 - 1) as g2:
                    for par in range(2):
                        weigh(g2 * 2 + par + 2, par)
                        add_experts(g2 * 2 + par, par)
                for par in range(2):
                    add_experts(GROUPS - 2 + par, par)

            @block.tensor
            def _(pe):
                pe.sem_inc(S["y_turned"], 2)
                pe.sem_inc(S["zw_turned"], 2)
                pe.sem_inc(S["base_added"], 4)
                pe.sem_inc(S["added"], 2)

                def turn(src, g, par, ready, turned):
                    pe.wait_ge(S[ready], g + 1)
                    pe.sem_inc(core.passed, 1)
                    for j in range(GROUP):
                        ins = t_.transpose(ps_y[par][:, j * P:(j + 1) * P], src[:, par, j, :], core.ident[:])
                    ins.then_inc(S[turned], 1)

                def project(g, par):
                    pe.wait_ge(S["base_added"], 2 * g + 2)
                    pe.sem_inc(core.passed, 1)
                    pe.wait_ge(S["yT_ready"], g + 1)
                    pe.sem_inc(core.passed, 1)
                    for j in range(GROUP):
                        lhsT = yT[:, par, j * P:(j + 1) * P]
                        t_.matmul(ps_p[par][:, j, :], lhsT, wcat[:, 0:2 * D], start=True, stop=True)
                        ins = t_.matmul(ps_l[par][:, j, :], lhsT, wcat[:, 2 * D:2 * D + E], start=True, stop=True)
                    ins.then_inc(S["proj_done"], 1)

                def experts(g, par):
                    pe.wait_ge(S["added"], g + 1)
                    pe.sem_inc(core.passed, 1)
                    pe.wait_ge(S["zwT_ready"], g + 1)
                    pe.sem_inc(core.passed, 1)
                    for j in range(GROUP):
                        ins = t_.matmul(ps_p[par][:, j, 0:D], zwT[:, par, j * P:(j + 1) * P], lB[:], start=True, stop=True)
                    ins.then_inc(S["moe_done"], 1)

                for src, ready, turned, multiply in ((y, "y_ready", "y_turned", project),
                                                     (zw, "zw_ready", "zw_turned", experts)):
                    turn(src, 0, 0, ready, turned)
                    with pe.Fori(0, GROUPS // 2 - 1) as g2:
                        for par in range(2):
                            turn(src, g2 * 2 + par + 1, 1 - par, ready, turned)
                            multiply(g2 * 2 + par, par)
                    turn(src, GROUPS - 1, 1, ready, turned)
                    multiply(GROUPS - 2, 0)
                    multiply(GROUPS - 1, 1)

            @block.scalar
            def _(act):
                def copy_turned(dst, g, par, turned, ready):
                    act.wait_ge(S[turned], g + 3)
                    act.sem_inc(core.passed, 1)
                    s.copy(dst[:, par, :], ps_y[par]).then_inc(S[ready], 1)

                def copy_out(g, par):
                    act.wait_ge(S["proj_done"], g + 1)
                    act.sem_inc(core.passed, 1)
                    s.copy(logits[:, bass.ds(g * GROUP, GROUP), :], ps_l[par])
                    s.copy(z[:, bass.ds(g * GROUP, GROUP), :], ps_p[par][:, :, D:2 * D]).then_inc(S["z_ready"], 1)

                copy_turned(yT, 0, 0, "y_turned", "yT_ready")
                with act.Fori(0, GROUPS // 2 - 1) as g2:
                    for par in range(2):
                        copy_turned(yT, g2 * 2 + par + 1, 1 - par, "y_turned", "yT_ready")
                        copy_out(g2 * 2 + par, par)
                copy_turned(yT, GROUPS - 1, 1, "y_turned", "yT_ready")
                copy_out(GROUPS - 2, 0)
                copy_out(GROUPS - 1, 1)
                act.wait_ge(S["left_ready"], 1)
                s.activation(flat(left[:]), flat(left[:]), ACT.Exp).then_inc(S["exp_ready"], 1)
                with act.Fori(0, GROUPS // 2) as g2:
                    for par in range(2):
                        copy_turned(zwT, g2 * 2 + par, par, "zw_turned", "zwT_ready")
        core.clear()


def attention(core, tag, a, consts):
    nc = core.nc
    NH, DK = 16, 8
    HG = 4
    SPLIT = 4
    SCALE = float(1.0 / np.sqrt(DK * 2.0) / 1.5)
    UNIT = 64.0
    T = TIME
    VW = DK + 1
    v, s, t_, g_ = nc.vector, nc.scalar, nc.tensor, nc.gpsimd
    with ExitStack() as ctx:
        def sb(name, shape, dt=F32):
            return ctx.enter_context(nc.sbuf_tensor(f"{tag}_{name}", shape, dt))

        def sem(name):
            return core.scoped_sem(ctx, f"{tag}_{name}")

        wqkv = sb("wqkv", [P, 3 * D])
        wo = sb("wo", [P, D])
        bias = sb("bias", [P, 4 * D])
        ident16 = sb("ident16", [P, P], F16)
        tri = sb("tri", [P, P])
        STEPS = BATCHES * HG
        qkT = sb("qkT", [P, STEPS, 2, T], F16)
        V = sb("V", [P, STEPS, BATCH_TILES, HG, VW])
        O = sb("O", [P, STEPS, BATCH_TILES, HG * DK])
        names = ("loaded filled var_ready rstd_ready dve_chain y_ready y_turned yT_ready proj_done "
                 "taken ss_ready norm_ready qn_ready hi_ready lo_ready split_turned qkT_ready zeroed staged v_zeroed v_staged s_done "
                 "e_done m_done pv_done oT_read sums_turned rec_ready o_read ost_ready o_turned oT_ready out_done added bias_halved").split()
        S = {n: sem(n) for n in names}
        with ExitStack() as c2:
            rows = c2.enter_context(nc.sbuf_tensor(f"{tag}_rows", [P, 4, P], F32))
            with nc.Block() as block:
                @block.vector
                def _(dve):
                    v.memset(V[:], 1.0).then_inc(S["filled"], 1)
                    v.tensor_copy(ident16[:], core.ident[:]).then_inc(S["filled"], 1)

                @block.sync
                def _(sp):
                    sp.wait_ge(S["filled"], 2)
                    for n, x in enumerate("qkvo"):
                        sp.dma_start(rows[:, n, :], a[f"L1_attn_W{x}"]).then_inc(S["loaded"], 16)
                        sp.dma_start(bias[:, n * D:(n + 1) * D], a[f"L1_attn_b{x}"].unsqueeze(0).broadcast_to([P, D])).then_inc(S["loaded"], 16)
                    sp.dma_start(tri[:], consts["tri"]).then_inc(S["loaded"], 16)
            bank = c2.enter_context(nc.psum_tensor(f"{tag}_psw", [P, 4, 512], F32))
            turn_weights(nc, core, ctx, tag, [(rows[:, n, :], wqkv[:, n * D:(n + 1) * D] if n < 3 else wo[:], P)
                                         for n in range(4)], S["loaded"], 144, bank)

        with ExitStack() as c2:
            def sb2(name, shape, dt=F32):
                return c2.enter_context(nc.sbuf_tensor(f"{tag}_{name}", shape, dt))

            bank = c2.enter_context(nc.psum_tensor(f"{tag}_psa", [P, 6, 512], F32))
            bank16 = c2.enter_context(nc.psum_tensor(f"{tag}_ps16", [P, 2, 1024], F16))
            y = sb2("y", [P, 2, GROUP, D])
            yT = sb2("yT", [P, 2, GROUP * P])
            qk = sb2("qk", [P, 2, GROUP, 2 * D])
            sq = sb2("sq", [P, GROUP, 2 * D])
            ss = sb2("ss", [P, 2, GROUP * 2 * NH])
            rn = sb2("rn", [P, 2, GROUP * 2 * NH])
            split = sb2("split", [P, 2, GROUP, 2, NH, SPLIT, DK], F16)
            ps_y = [bank[:, i, :] for i in (0, 5)]
            ps_qkv = bank[:, 1:5, 0:3 * D]
            PAIRS = GROUPS // 2

            with nc.Block() as block:
                @block.gpsimd
                def _(pool):
                    core.ln_rsqrt(pool, S["var_ready"], S["rstd_ready"])

                def pipeline(eng, iteration, enter=None):
                    iteration(0, 0, True, False, False)
                    iteration(0, 1, False, False, False)
                    with eng.Fori(0, PAIRS - 2) as i:
                        if enter:
                            enter(i)
                        for par in range(2):
                            iteration(i + 1, par, False, False, False)
                    if enter:
                        enter(None)
                    iteration(PAIRS - 1, 0, False, False, True)
                    iteration(PAIRS - 1, 1, False, True, True)

                @block.vector
                def _(dve):
                    dve.sem_inc(S["y_turned"], 2)
                    chain = Chain(dve, S["dve_chain"])
                    core.ln_stats(dve, chain, S["var_ready"], S["rstd_ready"])
                    dve.wait_ge(S["loaded"], 144)

                    def normalize(g, par):
                        dve.wait_ge(S["y_turned"], g + 1)
                        dve.sem_inc(core.passed, 1)
                        for j in range(GROUP):
                            ins = core.normalize(y[:, par, j, :], g * GROUP + j)
                        ins.then_inc(S["y_ready"], 1)

                    def take(b, g, par):
                        dve.wait_ge(S["proj_done"], g + 3)
                        dve.sem_inc(core.passed, 1)
                        v.tensor_tensor(qk[:, par], ps_qkv[:, :, 0:2 * D],
                                        bias[:, 0:2 * D].unsqueeze(1).broadcast_to([P, GROUP, 2 * D]), ALU.add).then_inc(S["taken"], 1)
                        for j in range(GROUP):
                            v.tensor_tensor(V[:, bass.ds(b * HG, HG), par * GROUP + j, :, 0:DK],
                                            ps_qkv[:, j, 2 * D:3 * D].rearrange("p (g h d) -> p g h d", h=HG, d=DK),
                                            bias[:, 2 * D:3 * D].rearrange("p (g h d) -> p g h d", h=HG, d=DK),
                                            ALU.add).then_inc(S["taken"], 1)

                    def lengths(g, par):
                        dve.wait_ge(S["taken"], (GROUP + 1) * (g + 1))
                        dve.sem_inc(core.passed, 1)
                        chain.link(v.tensor_tensor(sq[:], qk[:, par], qk[:, par], ALU.mult))
                        chain.link(v.tensor_reduce(ss[:, par], sq[:].rearrange("p j (h d) -> p (j h) d", d=DK), AX_X, ALU.add))
                        v.tensor_scalar(ss[:, par], ss[:, par], 1e-16, None, ALU.max).then_inc(S["ss_ready"], 1)

                    def units(g, par):
                        dve.wait_ge(S["norm_ready"], g + 1)
                        dve.sem_inc(core.passed, 1)
                        chain.link(v.reciprocal(rn[:, par], ss[:, par]))
                        qkh = qk[:, par].rearrange("p j (h d) -> p (j h) d", d=DK)
                        v.scalar_tensor_tensor(qkh, qkh, UNIT, rn[:, par].unsqueeze(2).broadcast_to([P, GROUP * 2 * NH, DK]),
                                               ALU.mult, ALU.mult).then_inc(S["qn_ready"], 1)

                    def low_halves(g, par):
                        dve.wait_ge(S["hi_ready"], 4 * g + 4)
                        dve.sem_inc(core.passed, 1)
                        for n in range(2):
                            qn = qk[:, par].rearrange("p j (n h d) -> p j n h d", n=2, d=DK)[:, :, n]
                            for m in range(2):
                                hi, lo = ((m, 2 + m) if n == 0 else (2 * m, 2 * m + 1))
                                ins = v.tensor_tensor(split[:, par, :, n, :, lo, :], qn, split[:, par, :, n, :, hi, :], ALU.subtract)
                        ins.then_inc(S["lo_ready"], 1)

                    def iteration(b, par, first, last, end):
                        g = b * 2 + par
                        take(b, g, par)
                        lengths(g, par)
                        if not first:
                            low_halves(g - 1, 1 - par)
                        if not end:
                            normalize(g + 2, par)
                        units(g, par)

                    def enter(i):
                        if i is None:
                            chain.leave(before[0], PAIRS - 2)
                        else:
                            before.append(chain.n)
                            chain.enter(before[0], i, 6)

                    before = []
                    normalize(0, 0)
                    normalize(1, 1)
                    pipeline(dve, iteration, enter)
                    low_halves(GROUPS - 1, 1)

                @block.scalar
                def _(act):
                    def copy_yT(g, par):
                        act.wait_ge(S["y_turned"], g + 3)
                        act.sem_inc(core.passed, 1)
                        act.wait_ge(S["proj_done"], g + 1)
                        act.sem_inc(core.passed, 1)
                        s.copy(yT[:, par, :], ps_y[par]).then_inc(S["yT_ready"], 1)

                    def norms(g, par):
                        act.wait_ge(S["ss_ready"], g + 1)
                        act.sem_inc(core.passed, 1)
                        s.activation(ss[:, par], ss[:, par], ACT.Sqrt).then_inc(S["norm_ready"], 1)

                    def high_halves(g, par):
                        act.wait_ge(S["qn_ready"], g + 1)
                        act.sem_inc(core.passed, 1)
                        for n in range(2):
                            qn = qk[:, par].rearrange("p j (n h d) -> p j n h d", n=2, d=DK)[:, :, n]
                            for m in range(2):
                                s.copy(split[:, par, :, n, :, m if n == 0 else 2 * m, :], qn).then_inc(S["hi_ready"], 1)

                    def store_turned(b, g, par):
                        for j in range(GROUP):
                            act.wait_ge(S["split_turned"], g * GROUP + j + 1)
                            act.sem_inc(core.passed, 1)
                            tokens = slice((par * GROUP + j) * P, (par * GROUP + j + 1) * P)
                            s.copy(qkT[:, bass.ds(b * HG, HG), :, tokens].rearrange("p g n c -> p n g c"),
                                   bank16[:, j % 2, :].rearrange("p (n g c) -> p n g c", n=2, g=HG)).then_inc(S["qkT_ready"], 1)

                    def iteration(b, par, first, last, end):
                        g = b * 2 + par
                        if not last:
                            copy_yT(g + 1, 1 - par)
                        norms(g, par)
                        if not first:
                            store_turned(b - 1 + par, g - 1, 1 - par)
                        high_halves(g, par)

                    s.activation(core.warm[:], core.minus_half[:, 0:1], ACT.Sqrt, scale=-1.0).then_inc(core.passed, 1)
                    copy_yT(0, 0)
                    pipeline(act, iteration)
                    store_turned(PAIRS - 1, GROUPS - 1, 1)

                @block.tensor
                def _(pe):
                    def turn_y(g, par):
                        pe.wait_ge(S["y_ready"], g + 1)
                        pe.sem_inc(core.passed, 1)
                        for j in range(GROUP):
                            ins = t_.transpose(ps_y[par][:, j * P:(j + 1) * P], y[:, par, j, :], core.ident[:])
                        ins.then_inc(S["y_turned"], 1)

                    def project(g, par, first):
                        pe.wait_ge(S["yT_ready"], g + 1)
                        pe.sem_inc(core.passed, 1)
                        if not first:
                            pe.wait_ge(S["taken"], (GROUP + 1) * g)
                            pe.sem_inc(core.passed, 1)
                        for j in range(GROUP):
                            ins = t_.matmul(ps_qkv[:, j, :], yT[:, par, j * P:(j + 1) * P], wqkv[:], start=True, stop=True)
                        ins.then_inc(S["proj_done"], 1)

                    def turn_split(g, par):
                        pe.wait_ge(S["lo_ready"], g + 1)
                        pe.sem_inc(core.passed, 1)
                        for j in range(GROUP):
                            pe.wait_ge(S["qkT_ready"], g * GROUP + j + 1)
                            pe.sem_inc(core.passed, 1)
                            for n in range(2 * HG):
                                ins = t_.transpose(bank16[:, j % 2, n * P:(n + 1) * P],
                                                   split[:, par, j, n // HG, n % HG * HG:n % HG * HG + HG]
                                                   .rearrange("p h x d -> p (h x d)"), ident16[:])
                            ins.then_inc(S["split_turned"], 1)

                    def iteration(b, par, first, last, end):
                        g = b * 2 + par
                        if not last:
                            turn_y(g + 1, 1 - par)
                        project(g, par, first)
                        if not first:
                            turn_split(g - 1, 1 - par)

                    pe.sem_inc(S["qkT_ready"], 2)
                    pe.sem_inc(S["proj_done"], 2)
                    turn_y(0, 0)
                    pipeline(pe, iteration)
                    turn_split(GROUPS - 1, 1)

        with ExitStack() as c2:
            def sb2(name, shape, dt=F32):
                return c2.enter_context(nc.sbuf_tensor(f"{tag}_{name}", shape, dt))

            SLOTS, PSLOTS = 3, 9
            TURN_AT = 2
            STAGE_AT = 6
            STAGED = HG + 1
            VP = 32
            bank = c2.enter_context(nc.psum_tensor(f"{tag}_psb", [P, 8, 512], F32))
            qs = sb2("qs", [P, 2, T], F16)
            ks = sb2("ks", [P, 2, HG, T], F16)
            vs = sb2("vs", [P, 2, BATCH_TILES, HG, VP])
            probs = sb2("probs", [P, PSLOTS, 1024])
            oTs = sb2("oTs", [P, T])
            rec = sb2("rec", [P, BATCH_TILES * HG])
            ps_s = [bank[:, 2 * i:2 * i + 2, :].rearrange("p b c -> p (b c)") for i in range(SLOTS)]
            ps_o = bank[:, 6:8, :].rearrange("p b c -> p (b c)")
            works, flushes = [], {}
            for k in range(BATCH_TILES // 2):
                for h in range(HG):
                    works.append([(h, 0, 0)] if k == 0 else [(h, k, 0), (h, BATCH_TILES - k, (BATCH_TILES - k) * P)])
                flushes[len(works) - 1] = [k] if k == 0 else [k, BATCH_TILES - k]
            k = BATCH_TILES // 2
            works += [[(0, k, 0), (1, k, 512)], [(2, k, 0), (3, k, 512)]]
            flushes[len(works) - 1] = [k]
            NW = len(works)
            assert NW % SLOTS == 0 and NW % PSLOTS == 0
            NF = len(flushes)
            flush_of = [sum(f < n for f in flushes) for n in range(NW)]
            place = {(h, kb): (n, at) for n, work in enumerate(works) for h, kb, at in work}

            with nc.Block() as block:
                @block.gpsimd
                def _(pool):
                    def stage_v(it, slot):
                        g_.tensor_copy(vs[:, slot, :, :, 0:VW],
                                       V[:, bass.ds(it, 1)].rearrange("p a t h d -> p (a t) h d")).then_inc(S["v_staged"], 1)
                        pool.wait_ge(S["v_staged"], it + 1)
                        pool.sem_inc(core.passed, 1)

                    g_.memset(vs[:], 0.0).then_inc(S["v_zeroed"], 1)
                    pool.wait_ge(S["v_zeroed"], 1)
                    for it in range(2):
                        stage_v(it, it)
                    with pool.Fori(0, STEPS // 2 - 1) as i2:
                        for slot in range(2):
                            it = i2 * 2 + (slot + 2)
                            pool.wait_ge(S["pv_done"], it * NF)
                            pool.sem_inc(core.passed, 1)
                            stage_v(it, slot)

                @block.vector
                def _(dve):
                    v.memset(ks[:], 0.0).then_inc(S["zeroed"], 1)
                    dve.wait_ge(S["zeroed"], 1)

                    def stage(it, slot):
                        step = qkT[:, bass.ds(it, 1)].rearrange("p a n c -> p (a n) c")
                        v.tensor_copy(qs[:, slot, :], step[:, 0]).then_inc(S["staged"], 1)
                        for h in range(HG):
                            r = slice(h * 32, h * 32 + 32)
                            v.tensor_copy(ks[r, slot, h, :], step[r, 1]).then_inc(S["staged"], 1)

                    def mask(it, n):
                        dve.wait_ge(S["e_done"], it * NW + n + 1)
                        dve.sem_inc(core.passed, 1)
                        for _, _, at in works[n]:
                            p = probs[:, n % PSLOTS, at:at + P]
                            ins = v.tensor_tensor(p, p, tri[:], ALU.mult)
                        ins.then_inc(S["m_done"], 1)

                    def read_sums(it):
                        dve.wait_ge(S["pv_done"], (it + 2) * NF)
                        dve.sem_inc(core.passed, 1)
                        v.tensor_copy(oTs[:], ps_o).then_inc(S["oT_read"], 1)

                    def close(it):
                        dve.wait_ge(S["sums_turned"], it + 1)
                        dve.sem_inc(core.passed, 1)
                        o = ps_o.rearrange("p (t h d) -> p t h d", t=BATCH_TILES, h=HG)
                        v.reciprocal(rec[:].rearrange("p (t h) -> p t h", h=HG).unsqueeze(3), o[:, :, :, DK:VW]).then_inc(S["rec_ready"], 1)
                        dve.wait_ge(S["rec_ready"], it + 1)
                        dve.sem_inc(core.passed, 1)
                        v.tensor_tensor(O[:, bass.ds(it, 1)].rearrange("p a t (h d) -> p (a t) h d", d=DK), o[:, :, :, 0:DK],
                                        rec[:].rearrange("p (t h) -> p t h", h=HG).unsqueeze(3)
                                        .broadcast_to([P, BATCH_TILES, HG, DK]), ALU.mult).then_inc(S["o_read"], 1)

                    def step(it, slot, first=False, last=False):
                        for n in range(NW):
                            mask(it, n)
                            if n == STAGE_AT and not last:
                                stage(it + 1, 1 - slot)
                            if n == 0 and not first:
                                read_sums(it - 1)
                            if n == TURN_AT and not first:
                                close(it - 1)

                    stage(0, 0)
                    step(0, 0, first=True)
                    with dve.Fori(0, STEPS // 2 - 1) as i2:
                        step(i2 * 2 + 1, 1)
                        step(i2 * 2 + 2, 0)
                    step(STEPS - 1, 1, last=True)
                    read_sums(STEPS - 1)
                    close(STEPS - 1)

                @block.scalar
                def _(act):
                    s.activation(core.warm[:], core.minus_half[:, 0:1], ACT.Exp).then_inc(core.passed, 1)
                    act.sem_inc(S["pv_done"], NF)
                    with act.Fori(0, STEPS) as it:
                        for n in range(NW):
                            act.wait_ge(S["pv_done"], it * NF + (flush_of[n - PSLOTS] + NF if n >= PSLOTS else flush_of[n + PSLOTS]) + 1)
                            act.sem_inc(core.passed, 1)
                            act.wait_ge(S["s_done"], it * NW + n + 1)
                            act.sem_inc(core.passed, 1)
                            s.activation(probs[:, n % PSLOTS, :], ps_s[n % SLOTS], ACT.Exp,
                                         scale=SCALE / (UNIT * UNIT)).then_inc(S["e_done"], 1)

                @block.tensor
                def _(pe):
                    pe.sem_inc(S["o_read"], 1)

                    def score(slot, n):
                        for h, kb, at in works[n]:
                            width, q0 = T - kb * P, kb * P
                            while width:
                                w = min(width, 512 - at % 512)
                                ins = t_.matmul(ps_s[n % SLOTS][:, at:at + w], ks[:, slot, h, kb * P:(kb + 1) * P],
                                                qs[:, slot, q0:q0 + w], start=True, stop=True, skip_group_check=True)
                                at, q0, width = at + w, q0 + w, width - w
                        ins.then_inc(S["s_done"], 1)

                    def gather(it, slot, n):
                        pe.wait_ge(S["m_done"], it * NW + n + 1)
                        pe.sem_inc(core.passed, 1)
                        for kb in flushes[n]:
                            for half in range(kb // 4, 2):
                                q0 = max(kb * P, half * 512)
                                for h in range(HG):
                                    w, at = place[(h, kb)]
                                    at += q0 - kb * P
                                    ins = t_.matmul(ps_o[VP * h:VP * h + VP, q0:half * 512 + 512],
                                                    vs[:, slot, kb, h, :], probs[:, w % PSLOTS, at:at + half * 512 + 512 - q0],
                                                    start=(kb == 0), stop=(kb == 4), skip_group_check=True)
                        return ins

                    def turn_sums(it):
                        pe.wait_ge(S["oT_read"], it + 1)
                        pe.sem_inc(core.passed, 1)
                        for t in range(BATCH_TILES):
                            ins = t_.transpose(ps_o[:, t * P:(t + 1) * P], oTs[:, t * P:(t + 1) * P], core.ident[:])
                        ins.then_inc(S["sums_turned"], 1)

                    def step(it, slot, first=False, last=False):
                        for n in range(NW):
                            m = n + SLOTS
                            if m == NW and not last:
                                pe.wait_ge(S["staged"], STAGED * (it + 2))
                                pe.sem_inc(core.passed, 1)
                            if m < NW or not last:
                                pe.wait_ge(S["e_done"], it * NW + n + 1)
                                pe.sem_inc(core.passed, 1)
                                score(slot if m < NW else 1 - slot, m % NW)
                            if n == TURN_AT and not first:
                                turn_sums(it - 1)
                            if n == 0 and not first:
                                gather(it - 1, 1 - slot, NW - 1).then_inc(S["pv_done"], 1)
                            if n - 1 in flushes:
                                if n - 1 == min(flushes):
                                    pe.wait_ge(S["v_staged"], it + 1)
                                    pe.sem_inc(core.passed, 1)
                                    pe.wait_ge(S["o_read"], it + 1)
                                    pe.sem_inc(core.passed, 1)
                                gather(it, slot, n - 1).then_inc(S["pv_done"], 1)

                    pe.wait_ge(S["staged"], STAGED)
                    for n in range(SLOTS):
                        score(0, n)
                    step(0, 0, first=True)
                    with pe.Fori(0, STEPS // 2 - 1) as i2:
                        step(i2 * 2 + 1, 1)
                        step(i2 * 2 + 2, 0)
                    step(STEPS - 1, 1, last=True)
                    gather(STEPS - 1, 1, NW - 1).then_inc(S["pv_done"], 1)
                    turn_sums(STEPS - 1)

        ostage = sb("ostage", [P, 2, GROUP, D])
        oT = sb("oT", [P, 2, GROUP * P])
        bank = ctx.enter_context(nc.psum_tensor(f"{tag}_psc", [P, 4, 512], F32))
        ps_t = [bank[:, i, :] for i in (0, 1)]
        ps_f = [bank[:, i, :].rearrange("p (j d) -> p j d", j=GROUP) for i in (2, 3)]
        with nc.Block() as block:
            @block.vector
            def _(dve):
                def stage(b, par, g):
                    dve.wait_ge(S["o_turned"], g + 1)
                    dve.sem_inc(core.passed, 1)
                    v.tensor_copy(ostage[:, par].rearrange("p t (g c) -> p t g c", g=HG),
                                  O[:, bass.ds(b * HG, HG), par * GROUP:(par + 1) * GROUP, :]
                                  .rearrange("p g t c -> p t g c")).then_inc(S["ost_ready"], 1)

                def add(g, par):
                    dve.wait_ge(S["out_done"], g + 1)
                    dve.sem_inc(core.passed, 1)
                    xg = core.x[:, bass.ds(g * GROUP, GROUP), :]
                    v.scalar_tensor_tensor(xg, ps_f[par], 0.5, xg, ALU.mult, ALU.add).then_inc(S["added"], 1)
                    dve.wait_ge(S["added"], 2 * g + 5)
                    dve.sem_inc(core.passed, 1)
                    v.tensor_tensor(xg, xg, bias[:, 3 * D:4 * D].unsqueeze(1).broadcast_to([P, GROUP, D]), ALU.add).then_inc(S["added"], 1)
                    dve.wait_ge(S["added"], 2 * g + 6)
                    dve.sem_inc(core.passed, 1)
                    for j in range(GROUP):
                        core.count(g * GROUP + j)

                dve.sem_inc(S["added"], 4)
                v.tensor_scalar(bias[:, 3 * D:4 * D], bias[:, 3 * D:4 * D], 0.5, None, ALU.mult).then_inc(S["bias_halved"], 1)
                dve.wait_ge(S["bias_halved"], 1)
                stage(0, 0, 0)
                stage(0, 1, 1)
                with dve.Fori(0, GROUPS // 2 - 1) as g2:
                    for par in range(2):
                        stage(g2 + 1, par, g2 * 2 + par + 2)
                        add(g2 * 2 + par, par)
                for par in range(2):
                    add(GROUPS - 2 + par, par)

            @block.tensor
            def _(pe):
                def turn(g, par):
                    pe.wait_ge(S["ost_ready"], g + 1)
                    pe.sem_inc(core.passed, 1)
                    for j in range(GROUP):
                        ins = t_.transpose(ps_t[par][:, j * P:(j + 1) * P], ostage[:, par, j, :], core.ident[:])
                    ins.then_inc(S["o_turned"], 1)

                def project(g, par):
                    pe.wait_ge(S["oT_ready"], g + 1)
                    pe.sem_inc(core.passed, 1)
                    pe.wait_ge(S["added"], 2 * g + 2)
                    pe.sem_inc(core.passed, 1)
                    for j in range(GROUP):
                        ins = t_.matmul(ps_f[par][:, j, :], oT[:, par, j * P:(j + 1) * P], wo[:], start=True, stop=True)
                    ins.then_inc(S["out_done"], 1)

                pe.sem_inc(S["o_turned"], 2)
                turn(0, 0)
                with pe.Fori(0, GROUPS // 2 - 1) as g2:
                    for par in range(2):
                        turn(g2 * 2 + par + 1, 1 - par)
                        project(g2 * 2 + par, par)
                turn(GROUPS - 1, 1)
                project(GROUPS - 2, 0)
                project(GROUPS - 1, 1)

            @block.scalar
            def _(act):
                with act.Fori(0, GROUPS // 2) as g2:
                    for par in range(2):
                        g = g2 * 2 + par
                        act.wait_ge(S["o_turned"], g + 3)
                        act.sem_inc(core.passed, 1)
                        s.copy(oT[:, par, :], ps_t[par]).then_inc(S["oT_ready"], 1)
        core.clear()


def transformer(nc, a, consts, out, stages):
    with ExitStack() as ctx:
        core = Core(nc, ctx, a["L0_attn_x"], consts)
        ffn = (a["L0_ffn_Wg"], a["L0_ffn_bg"], a["L0_ffn_W1"], a["L0_ffn_b1"], a["L0_ffn_W2"], a["L0_ffn_b2"],
               consts["order"])
        lora = (a["L1_ffn_base_w"], a["L1_ffn_base_b"], a["L1_ffn_gate_w"], a["L1_ffn_lora_A"], a["L1_ffn_lora_B"],
                consts["order"])
        steps = [lambda: moe_ffn(core, "ffn1", *ffn),
                 lambda: ssm(core, "ssm", a, consts),
                 lambda: moe_ffn(core, "ffn2", *ffn),
                 lambda: lora_ffn(core, "lora1", *lora),
                 lambda: attention(core, "attn", a, consts),
                 lambda: lora_ffn(core, "lora2", *lora)]
        for n in stages:
            steps[n]()
        stored = core.sem("stored")
        with nc.Block() as block:
            @block.sync
            def _(sp):
                sp.dma_start(out.rearrange("b (t p) d -> p (b t) d", p=P), core.x[:]).then_inc(stored, 16)
                sp.wait_ge(stored, 16)


_INS = ['L0_attn_x', 'L0_attn_W_in', 'L0_attn_A_log', 'L0_attn_dt_bias', 'L0_attn_B_norm_bias', 'L0_attn_C_norm_bias',
        'L0_attn_W_out', 'L0_ffn_Wg', 'L0_ffn_bg', 'L0_ffn_W1', 'L0_ffn_b1', 'L0_ffn_W2', 'L0_ffn_b2', 'L1_attn_Wq',
        'L1_attn_bq', 'L1_attn_Wk', 'L1_attn_bk', 'L1_attn_Wv', 'L1_attn_bv', 'L1_attn_Wo', 'L1_attn_bo',
        'L1_ffn_base_w', 'L1_ffn_base_b', 'L1_ffn_gate_w', 'L1_ffn_lora_A', 'L1_ffn_lora_B']
STAGES = (0, 1, 2, 3, 4, 5)


def constants():
    c = {"ident": np.eye(P, dtype=np.float32),
         "order": np.tile(np.arange(16, 0, -1, dtype=np.float32), (P, 1))}
    c["tri"] = np.triu(np.ones((P, P), np.float32))
    c.update(ssm_constants())
    return c


def kernel(**inputs):
    import numpy as _np
    import concourse.bacc as _bacc
    from concourse.bass_utils import run_bass_kernel_spmd as _run

    nc = _bacc.Bacc("TRN2", target_bir_lowering=False, num_devices=1)
    arrays, args, consts = {}, {}, {}
    for name in _INS:
        a = _np.ascontiguousarray(inputs[name])
        arrays[f"in_{name}"] = a
        args[name] = nc.dram_tensor(f"in_{name}", a.shape, mybir.dt.from_np(a.dtype), kind="ExternalInput").ap()
    for name, a in constants().items():
        arrays[f"const_{name}"] = a
        consts[name] = nc.dram_tensor(f"const_{name}", a.shape, mybir.dt.from_np(a.dtype), kind="ExternalInput").ap()
    out = nc.dram_tensor("out_x", (BATCHES, TIME, D), F32, kind="ExternalOutput").ap()
    transformer(nc, args, consts, out, STAGES)
    r = _run(nc, [arrays], core_ids=[0])
    return r.results[0]["out_x"]
```
